# Optimizing a Trainium2 kernel written in Bass

```python
import numpy as np
import jax
import jax.numpy as jnp

def _softmax(x, axis=-1):
    return jax.nn.softmax(x, axis=axis)

def _gelu(x):
    return jax.nn.gelu(x, approximate=True)

def _silu(x):
    return jax.nn.silu(x)

def _sigmoid(x):
    return jax.nn.sigmoid(x)

def _layernorm(x, axis=-1, eps=1e-05):
    m = jnp.mean(x, axis=axis, keepdims=True)
    v = jnp.var(x, axis=axis, keepdims=True)
    return (x - m) / jnp.sqrt(v + eps)

def _scatter_add(tgt, idx, src, axis=0):
    return tgt.at[idx].add(src)

def _segment_sum(src, seg, n):
    return jax.ops.segment_sum(src, seg, n)
kernel_name = 'mk_metaformer_d1_conv_nchw1024_r4_504821'

def setup_inputs(seed: int=0):
    np.random.seed(seed)
    _w = jnp.asarray

    def _rec_inputs():
        import jax
        import jax.numpy as jnp
        _gk = jax.random.key(seed)
        x = -0.000125 + 0.9999 * jax.random.normal(jax.random.fold_in(_gk, 1), (8, 256, 16, 16), jnp.float32)
        return x
    x = _rec_inputs()

    def _L0_conv_setup():
        import jax, jax.numpy as jnp
        import numpy as np
        from jax import lax
        GROUPS = 32
        EPS = 1e-05

        def _bilinear_resize(img, oh, ow):
            H, W = (img.shape[-2], img.shape[-1])

            def idx(n_in, n_out):
                x = (jnp.arange(n_out, dtype=jnp.float32) + 0.5) * (n_in / n_out) - 0.5
                x = jnp.clip(x, 0.0, n_in - 1)
                i0 = jnp.floor(x).astype(jnp.int32)
                i1 = jnp.minimum(i0 + 1, n_in - 1)
                return (i0, i1, x - i0)
            r0, r1, tr = idx(H, oh)
            c0, c1, tc = idx(W, ow)
            top = img[..., r0, :]
            bot = img[..., r1, :]
            row = top + (bot - top) * tr[:, None]
            left = row[..., c0]
            right = row[..., c1]
            return left + (right - left) * tc
        key = jax.random.key(seed)
        ks = jax.random.split(key, 12)
        b, c, h, w = (8, 256, 16, 16)
        cg = c // GROUPS
        s = 1.0 / np.sqrt(cg)
        inp = {'x': jax.random.normal(ks[0], (b, c, h, w), jnp.float32), 'w1': jax.random.normal(ks[1], (cg, cg), jnp.float32) * s, 'b1': jax.random.normal(ks[2], (cg,), jnp.float32) * 0.01, 'gn_gamma': jnp.ones((cg,), jnp.float32), 'gn_beta': jnp.zeros((cg,), jnp.float32), 'w_dw': jax.random.normal(ks[3], (cg, 1, 3, 3), jnp.float32) * (1.0 / 3.0), 'b_dw': jax.random.normal(ks[4], (cg,), jnp.float32) * 0.01, 'w_pw': jax.random.normal(ks[5], (cg, cg), jnp.float32) * s, 'b_pw': jax.random.normal(ks[6], (cg,), jnp.float32) * 0.01, 'w_fp': jax.random.normal(ks[7], (cg, cg), jnp.float32) * s, 'b_fp': jax.random.normal(ks[8], (cg,), jnp.float32) * 0.01}
        return inp
    _L0_conv_all = _L0_conv_setup()
    _L0_conv_in = {k: v for k, v in _L0_conv_all.items() if k in ('w1', 'b1', 'gn_gamma', 'gn_beta', 'w_dw', 'b_dw', 'w_pw', 'b_pw', 'w_fp', 'b_fp')}
    del _L0_conv_all

    def _L0_ffn_setup():
        import jax, jax.numpy as jnp
        import numpy as np
        TOP_K = 2
        key = jax.random.key(seed)
        ks = jax.random.split(key, 6)
        B, L, D, E, F = (2, 512, 256, 8, 1024)
        x = jax.random.normal(ks[0], (B, L, D), dtype=jnp.float32)
        Wg = jax.random.normal(ks[1], (D, E), dtype=jnp.float32) * D ** (-0.5)
        W1 = jax.random.normal(ks[2], (E, D, F), dtype=jnp.float32) * D ** (-0.5)
        b1 = jnp.zeros((E, F), dtype=jnp.float32)
        W2 = jax.random.normal(ks[3], (E, F, D), dtype=jnp.float32) * F ** (-0.5)
        b2 = jnp.zeros((E, D), dtype=jnp.float32)
        return {'x': x, 'Wg': Wg, 'W1': W1, 'b1': b1, 'W2': W2, 'b2': b2}
    _L0_ffn_all = _L0_ffn_setup()
    _L0_ffn_in = {k: v for k, v in _L0_ffn_all.items() if k in ('Wg', 'W1', 'b1', 'W2', 'b2')}
    del _L0_ffn_all
    return {'x': x, 'L0_conv_w1': _L0_conv_in['w1'], 'L0_conv_b1': _L0_conv_in['b1'], 'L0_conv_gn_gamma': _L0_conv_in['gn_gamma'], 'L0_conv_gn_beta': _L0_conv_in['gn_beta'], 'L0_conv_w_dw': _L0_conv_in['w_dw'], 'L0_conv_b_dw': _L0_conv_in['b_dw'], 'L0_conv_w_pw': _L0_conv_in['w_pw'], 'L0_conv_b_pw': _L0_conv_in['b_pw'], 'L0_conv_w_fp': _L0_conv_in['w_fp'], 'L0_conv_b_fp': _L0_conv_in['b_fp'], 'L0_ffn_Wg': _L0_ffn_in['Wg'], 'L0_ffn_W1': _L0_ffn_in['W1'], 'L0_ffn_b1': _L0_ffn_in['b1'], 'L0_ffn_W2': _L0_ffn_in['W2'], 'L0_ffn_b2': _L0_ffn_in['b2']}

def reference(x, L0_conv_w1, L0_conv_b1, L0_conv_gn_gamma, L0_conv_gn_beta, L0_conv_w_dw, L0_conv_b_dw, L0_conv_w_pw, L0_conv_b_pw, L0_conv_w_fp, L0_conv_b_fp, L0_ffn_Wg, L0_ffn_W1, L0_ffn_b1, L0_ffn_W2, L0_ffn_b2):
    import jax
    import jax.numpy as jnp

    def _L0_conv_ref(x, w1, b1, gn_gamma, gn_beta, w_dw, b_dw, w_pw, b_pw, w_fp, b_fp):
        import jax, jax.numpy as jnp
        import numpy as np
        from jax import lax
        GROUPS = 32
        EPS = 1e-05

        def _bilinear_resize(img, oh, ow):
            H, W = (img.shape[-2], img.shape[-1])

            def idx(n_in, n_out):
                x = (jnp.arange(n_out, dtype=jnp.float32) + 0.5) * (n_in / n_out) - 0.5
                x = jnp.clip(x, 0.0, n_in - 1)
                i0 = jnp.floor(x).astype(jnp.int32)
                i1 = jnp.minimum(i0 + 1, n_in - 1)
                return (i0, i1, x - i0)
            r0, r1, tr = idx(H, oh)
            c0, c1, tc = idx(W, ow)
            top = img[..., r0, :]
            bot = img[..., r1, :]
            row = top + (bot - top) * tr[:, None]
            left = row[..., c0]
            right = row[..., c1]
            return left + (right - left) * tc
        b, c, h, w = x.shape
        cg = c // GROUPS
        bg = b * GROUPS
        gx = x.reshape(bg, cg, h, w)
        x_h = gx.mean(axis=3, keepdims=True)
        x_w = gx.mean(axis=2, keepdims=True)
        cat = jnp.concatenate([x_h, jnp.transpose(x_w, (0, 1, 3, 2))], axis=2)
        hw = jnp.einsum('oc,bcln->boln', w1, cat) + b1[None, :, None, None]
        xh_g, xw_g = (hw[:, :, :h], hw[:, :, h:])
        gated = gx * jax.nn.sigmoid(xh_g) * jax.nn.sigmoid(jnp.transpose(xw_g, (0, 1, 3, 2)))
        mu = gated.mean(axis=(-2, -1), keepdims=True)
        var = gated.var(axis=(-2, -1), keepdims=True)
        x1 = (gated - mu) / jnp.sqrt(var + EPS) * gn_gamma[None, :, None, None] + gn_beta[None, :, None, None]
        dw = lax.conv_general_dilated(gx, w_dw, window_strides=(1, 1), padding=((1, 1), (1, 1)), feature_group_count=cg, dimension_numbers=('NCHW', 'OIHW', 'NCHW'))
        dw = dw + b_dw[None, :, None, None]
        x2 = jnp.einsum('oc,bchw->bohw', w_pw, dw) + b_pw[None, :, None, None]
        freq_mag = jnp.abs(jnp.fft.rfft2(gx, norm='ortho'))
        fm = freq_mag.mean(axis=-1)
        fmap = _bilinear_resize(fm, h, w)
        freq_feat = fmap[:, None] * w_fp.sum(axis=1)[None, :, None, None] + b_fp[None, :, None, None]
        s1 = jax.nn.softmax(x1.mean(axis=(-2, -1)), axis=-1)
        s2 = jax.nn.softmax(x2.mean(axis=(-2, -1)), axis=-1)
        wts = jnp.einsum('bc,bchw->bhw', s1, x2) + jnp.einsum('bc,bchw->bhw', s2, x1)
        weights = wts[:, None] + freq_feat
        return (gx * jax.nn.sigmoid(weights)).reshape(b, c, h, w)

    def _L0_ffn_ref(x, Wg, W1, b1, W2, b2):
        import jax, jax.numpy as jnp
        import numpy as np
        TOP_K = 2
        b, l, d = x.shape
        E = Wg.shape[1]
        xt = x.reshape(b * l, d)
        N = xt.shape[0]
        S = jax.nn.sigmoid(xt @ Wg)
        G, I = jax.lax.top_k(S, TOP_K)
        h = jax.nn.gelu(jnp.einsum('nd,edf->enf', xt, W1) + b1[:, None, :])
        y = jnp.einsum('enf,efd->end', h, W2) + b2[:, None, :]
        combine = jnp.zeros((N, E), dtype=x.dtype).at[jnp.arange(N)[:, None], I].add(G)
        out = jnp.einsum('ne,end->nd', combine, y)
        return out.reshape(b, l, d)

    def _gn(v, G=32, eps=1e-05):
        B_, C_, H_, W_ = v.shape
        g = v.reshape(B_, G, C_ // G, H_, W_)
        m = jnp.mean(g, axis=(2, 3, 4), keepdims=True)
        s = jnp.var(g, axis=(2, 3, 4), keepdims=True)
        return ((g - m) / jnp.sqrt(s + eps)).reshape(v.shape)

    def _ln_c(v, eps=1e-06):
        m = jnp.mean(v, axis=1, keepdims=True)
        s = jnp.var(v, axis=1, keepdims=True)
        return (v - m) / jnp.sqrt(s + eps)

    def _ln_t(v, eps=1e-05):
        m = jnp.mean(v, axis=-1, keepdims=True)
        s = jnp.var(v, axis=-1, keepdims=True)
        return (v - m) / jnp.sqrt(s + eps)

    def _to_tokens(v):
        B_, C_, H_, W_ = v.shape
        return v.reshape(B_, C_, H_ * W_).transpose(0, 2, 1)

    def _from_tokens(t, like):
        B_, C_, H_, W_ = like.shape
        return t.transpose(0, 2, 1).reshape(B_, C_, H_, W_)
    x = x + _L0_conv_ref(_ln_c(x), L0_conv_w1, L0_conv_b1, L0_conv_gn_gamma, L0_conv_gn_beta, L0_conv_w_dw, L0_conv_b_dw, L0_conv_w_pw, L0_conv_b_pw, L0_conv_w_fp, L0_conv_b_fp)
    t = _to_tokens(x)
    t = t + _L0_ffn_ref(_ln_t(t), L0_ffn_Wg, L0_ffn_W1, L0_ffn_b1, L0_ffn_W2, L0_ffn_b2)
    x = _from_tokens(t, x)
    return x

_drawn_inputs = setup_inputs


def setup_inputs(seed=0):
    import zlib

    import numpy as np

    out = dict(_drawn_inputs(seed))
    spreads = {'L0_conv_gn_gamma': (1.0, 0.2),
     'L0_conv_gn_beta': (0.0, 0.1),
     'L0_ffn_b1': (0.0, 0.1),
     'L0_ffn_b2': (0.0, 0.1)}
    factors = {'L0_conv_b1': 155.131, 'L0_conv_b_dw': 6.02, 'L0_conv_b_pw': 12.567, 'L0_conv_b_fp': 2.799}
    for name, (base, spread) in spreads.items():
        noise = np.random.default_rng([zlib.crc32(name.encode()), seed]).standard_normal(out[name].shape)
        drawn = base * np.exp(spread * noise) if base else spread * noise
        out[name] = jnp.asarray(drawn.astype(out[name].dtype))
    for name, factor in factors.items():
        out[name] = (out[name] * factor).astype(out[name].dtype)
    return out
```

```python
from contextlib import ExitStack

import numpy as np

import concourse.bass as bass
from concourse import mybir

ALU = mybir.AluOpType
ACT = mybir.ActivationFunctionType
AX_X = mybir.AxisListType.X
F32 = mybir.dt.float32
F16 = mybir.dt.float16
I32 = mybir.dt.int32
U32 = mybir.dt.uint32

P = 128
B, C, H, W = 8, 256, 16, 16
PX = H * W
NTOK = B * PX
NBLK = NTOK // P
CG = 8
HALVES = C // P
NT = B * HALVES
PAD = H + 2
KW = W // 2 + 1
NF = H * KW
E, F, TOP_K = 8, 1024, 2
DC, FC = C // P, F // P
SLOTS_MOST = NTOK * TOP_K
TILES = SLOTS_MOST // P + E - 1
TCOL = TILES + 1
TROWS = NTOK + P
EPS_C, EPS_G = 1e-6, 1e-5
XS, WS, HS = 64.0, 256.0, 16.0
PIECE = DC * F
EXPERT = 4 * PIECE
EARLY = 4
NSTG = 2
TINY = 1e-30

def _columns(widths):
    at, out = 0, {}
    for name, n in widths:
        out[name] = slice(at, at + n)
        at += n
    return out, at

CONST, NCONST = _columns([("ident", P), ("blocks", P), ("resize", H), ("own", CG), ("iota", P),
                          ("tiles", TCOL), ("before", E * E), ("steps", NBLK), ("token", NBLK),
                          ("spare", 1), ("dft", DC * 2 * NF)])
C16, NC16 = _columns([("ident", P), ("earlier", P), ("ones", P), ("bias", P)])
PAR, NPAR = _columns([("w1", CG), ("wpw", CG), ("wdw", 9), ("b1", 1), ("gamma", 1), ("beta", 1),
                      ("bdw", 1), ("bpw", 1), ("bfp", 1), ("betarow", CG), ("wfp", CG * CG),
                      ("bpwrow", P), ("wg", HALVES * E), ("b1e", E * FC)])


def build(nc, x_tok, x_chan, const, const16, params, w1, w2, b2, out):
    with ExitStack() as ctx:
        def sb(name, shape, dt=F32):
            return ctx.enter_context(nc.sbuf_tensor(name, shape, dt))

        def sem(name):
            return ctx.enter_context(nc.semaphore(name))

        xn_rows = nc.dram_tensor("xn_rows", [TROWS, 2 * C], F16, kind="Internal").ap()

        wt = sb("wt", [P, E * EXPERT], F16)
        late = wt[:, EARLY * EXPERT:].bitcast(F32)
        xln_tok = late[:, 0:NBLK * C].rearrange("p (k c) -> p k c", c=C)
        x_cm = late[:, 0:NT * PX].rearrange("p (t n) -> p t n", n=PX)
        o = NBLK * C
        xln_pad = late[:, o:o + NT * PAD * PAD].rearrange("p (t h w) -> p t h w", h=PAD, w=PAD)
        o += NT * PAD * PAD
        gated = late[:, o:o + NT * PX].rearrange("p (t n) -> p t n", n=PX)
        z = gated
        b2f = late[0:2, o:o + E * C]
        b2hi = late[0:2, o + E * C:o + E * C * 3 // 2].bitcast(F16)
        b2lo = late[0:2, o + E * C * 3 // 2:o + 2 * E * C].bitcast(F16)
        o += NT * PX
        mag = late[:, o:o + NT * NF].rearrange("p (t n) -> p t n", n=NF)

        zrow = late[:, o:o + C].bitcast(F16)
        o += NT * NF
        sg = late[:, o:o + NT * (H + W)].rearrange("p (t n) -> p t n", n=H + W)
        o += NT * (H + W)

        xt = sb("xt", [P, NBLK, C])
        stg = sb("stg", [P, NSTG, PIECE])
        fb = sb("fb", [P, 6144])
        cst = sb("cst", [P, NCONST])
        c16 = sb("c16", [P, NC16], F16)
        par = sb("par", [P, NPAR])
        b2c = sb("b2c", [P, E * C], F16)

        def view(at, n, dt=F32):
            v = fb[:, at:at + n]
            return v if dt is F32 else v.bitcast(dt)

        tapw = view(0, 9 * P).rearrange("p (k m) -> p k m", m=P)
        coefw = view(1152, NT * P).rearrange("p (t m) -> p t m", m=P)
        rf = view(3200, 2 * 512).rearrange("p (s n) -> p s n", s=2)
        sq = view(4224, 2 * 2 * NF).rearrange("p (s n) -> p s n", s=2)
        sig = view(4800, 2 * PX).rearrange("p (s n) -> p s n", s=2)
        xn = view(5312, 2 * C).rearrange("p (s n) -> p s n", s=2)
        xrow = view(0, 1024, F16).rearrange("p (b k n) -> p b k n", b=2, k=2)
        cmp_gt = view(1152, NBLK * E * E).rearrange("p (k e j) -> p k e j", e=E, j=E)
        cmp_eq = view(2176, NBLK * E * E).rearrange("p (k e j) -> p k e j", e=E, j=E)
        pay = view(3200, 2 * NBLK * 2 * TCOL).rearrange("p (a k v i) -> p a k v i", a=2, k=NBLK, v=2)
        hot = xt[:, :, :].rearrange("p k c -> p (k c)").rearrange("p (a k r) -> p a k r", a=2, r=P)
        xg = view(0, 512, F16).rearrange("p (s n) -> p s n", s=2)
        xT = view(512, 512, F16).rearrange("p (s n) -> p s n", s=2)
        hid = view(1024, 2 * F).rearrange("p (s n) -> p s n", s=2)
        hhi = view(3072, F, F16).rearrange("p (s n) -> p s n", s=2)
        hlo = view(4096, F, F16).rearrange("p (s n) -> p s n", s=2)
        yb = view(5120, 2 * C).rearrange("p (s n) -> p s n", s=2)

        bn6 = sb("bn6", [P, NBLK, 6])
        mv = sb("mv", [P, NBLK, 2])
        rstd = sb("rstd", [P, NBLK])
        eps = sb("eps", [P, 2])
        eps_c, eps_g = eps[:, 0:1], eps[:, 1:2]
        ones_row = sb("ones_row", [1, NT])
        w1d = view(5824, P)
        wpwd = sb("wpwd", [P, P])
        wfpd = view(5952, P)
        prow = sb("prow", [P, 16 * CG])
        pcol = sb("pcol", [P, 32])
        wgc = sb("wgc", [P, HALVES, E])
        rc = sb("rc", [P, NT, H + W])
        gbn6 = sb("gbn6", [P, NT, 6])
        gmv = sb("gmv", [P, NT, 2])
        grs = sb("grs", [P, NT])
        tot = sb("tot", [P, NT])
        r3 = sb("r3", [P, NT, 3])
        q3 = sb("q3", [P, NT, 3, 2])
        s9 = late[:, o:o + NT * 9].rearrange("p (t a b) -> p t a b", a=3, b=3)
        dwm = sb("dwm", [P, NT])
        s2r = sb("s2r", [NT, 4, P])
        s2s = sb("s2s", [NT, 2, 16])
        s2c = sb("s2c", [P, NT])
        coef = sb("coef", [P, NT])
        bterm = sb("bterm", [P, NT])
        bias = sb("bias", [P, NT])
        fm = sb("fm", [P, NT, H])
        tmv = sb("tmv", [P, NBLK, 2])
        trs = sb("trs", [P, NBLK])
        trs64 = sb("trs64", [P, NBLK])
        lg = sb("lg", [P, NBLK, E])
        sgl = sb("sgl", [P, NBLK, E])
        rank = sb("rank", [P, NBLK, E])
        sel16 = sb("sel16", [P, NBLK, E], F16)
        cnt = sb("cnt", [P, E])
        tcnt = sb("tcnt", [P, 3, E])
        slot = sb("slot", [P, NBLK, E])
        pick = view(1664, 2 * NBLK * E).rearrange("p (a k e) -> p a k e", a=2, k=NBLK)
        psum_pick = sb("picked", [P, 2, 2, NBLK])
        sloti = sb("sloti", [P, 3, 2, NBLK], I32)
        slotf = sb("slotf", [P, 3, 2, NBLK])
        texpf = view(1920, TCOL * E).rearrange("p (i e) -> p i e", e=E)
        texpc = sb("texpc", [P, TCOL])
        texp = sb("texp", [P, TCOL], I32)
        idx = sb("idx", [P, TCOL], I32)
        idxc = sb("idxc", [P, 4], I32)
        gates = sb("gates", [P, TCOL])

        ps = ctx.enter_context(nc.psum_tensor("ps", [P, 8, 512], F32))
        WB = [6, 7, 0, 1]
        GB = [4, 7]
        xT_ps = ps[:, 0, 0:256].bitcast(F16)

        def h_ps(s):
            return ps[:, 1 + 2 * s:3 + 2 * s, :].rearrange("p b n -> p (b n)")

        def y_ps(s):
            return ps[:, 5 + s, 0:C]

        const_in = sem("const_in")
        x_in = [sem(f"x_in{i}") for i in range(4)]
        stg_in = [sem(f"stg_in{i}") for i in range(NSTG)]
        b2_in = sem("b2_in")
        xcm_in = sem("xcm_in")
        spare_set = sem("spare_set")
        t_out = sem("t_out")
        xn_out = [sem(f"xn_out{i}") for i in range(2)]
        hi_done = sem("hi_done")
        lo_done = sem("lo_done")
        dve_step = sem("dve_step")
        pad_zero = sem("pad_zero")
        ln_done = sem("ln_done")
        eps_set = sem("eps_set")
        var_c = sem("var_c")
        dev_c = sem("dev_c")
        var_g = sem("var_g")
        dev_g = sem("dev_g")
        var_t = sem("var_t")
        dev_t = sem("dev_t")
        tr_done = sem("tr_done")
        tr_copied = sem("tr_copied")
        dft_done = sem("dft_done")
        sq_done = sem("sq_done")
        mag_done = sem("mag_done")
        root_done = sem("root_done")
        fm_done = sem("fm_done")
        rf_done = sem("rf_done")
        rc_done = sem("rc_done")
        gate_mm = sem("gate_mm")
        gate_sig = sem("gate_sig")
        gate_row = sem("gate_row")
        gated_done = sem("gated_done")
        small_ready = sem("small_ready")
        small_mm = sem("small_mm")
        exp_in = sem("exp_in")
        exp_done = sem("exp_done")
        tapw_done = sem("tapw_done")
        coef_done = sem("coef_done")
        map_done = sem("map_done")
        sig_done = sem("sig_done")
        z_done = sem("z_done")
        zt_done = sem("zt_done")
        t_done = sem("t_done")
        xn_done = sem("xn_done")
        xhi_done = sem("xhi_done")
        xlo_done = sem("xlo_done")
        logit_mm = sem("logit_mm")
        logit_done = sem("logit_done")
        sigl_done = sem("sigl_done")
        sel_done = sem("sel_done")
        prefix_mm = sem("prefix_mm")
        hot_done = sem("hot_done")
        table_mm = sem("table_mm")
        table_done = sem("table_done")
        b2_done = sem("b2_done")
        b2_zero = sem("b2_zero")
        gather_index = sem("gather_index")
        sum_index = sem("sum_index")
        g_in = [sem(f"g_in{i}") for i in range(2)]
        add_out = sem("add_out")
        xT_mm = sem("xT_mm")
        xT_done = sem("xT_done")
        l1_mm = sem("l1_mm")
        gelu_done = sem("gelu_done")
        h_done = sem("h_done")
        l2_mm = sem("l2_mm")
        y_done = sem("y_done")

        def wpiece(n, part):
            at = (n // 2) * EXPERT + part * 2 * PIECE + (n % 2) * PIECE
            return wt[:, at:at + PIECE]

        w1_dram = w1.rearrange("e (c p) f -> e p c f", p=P)
        w2_dram = w2.rearrange("e (c p) d -> e p c d", p=P)
        out_rows = out[0:NTOK, :].rearrange("(k p) c -> p k c", p=P)
        xn_dram = xn_rows[0:NTOK, :].rearrange("(k p) c -> p k c", p=P)
        x_dram = x_tok.rearrange("(k p) c -> p k c", p=P)
        col = lambda name, k=0: par[:, PAR[name].start + k:PAR[name].start + k + 1]
        cc = lambda name: cst[:, CONST[name]]
        inner = lambda t0, n: xln_pad[:, t0:t0 + n, 1:1 + H, 1:1 + W]

        block = ctx.enter_context(nc.Block())

        @block.sync
        def _(sp):
            sp.dma_start(x_t := xt[:, 0:4, :], x_dram[:, 0:4, :]).then_inc(x_in[0], 16)
            sp.dma_start(par[:, :], params).then_inc(const_in, 16)
            sp.dma_start(cst[:, :], const).then_inc(const_in, 16)
            sp.dma_start(c16[:, :], const16).then_inc(const_in, 16)
            for q in range(1, 4):
                sp.dma_start(xt[:, 4 * q:4 * q + 4, :], x_dram[:, 4 * q:4 * q + 4, :]).then_inc(x_in[q], 16)

            sp.dma_start(b2f, b2).then_inc(b2_in, 16)

            sp.wait_ge(b2_zero, 2)
            sp.dma_start(xn_rows[NTOK:TROWS, :], zrow).then_inc(spare_set, 16)
            sp.dma_start(out[NTOK:TROWS, :], zrow.bitcast(F32)).then_inc(spare_set, 16)

            def load_piece(n):
                if n >= NSTG:
                    sp.wait_ge(hi_done, n - NSTG + 1)
                    sp.wait_ge(lo_done, n - NSTG + 1)
                src = (w1_dram if n % 2 == 0 else w2_dram)[n // 2]
                dst = stg[:, n % NSTG, :].rearrange("p (c f) -> p c f", c=DC if n % 2 == 0 else FC)
                sp.dma_start(dst, src).then_inc(stg_in[n % NSTG], 16)

            for n in range(2 * EARLY):
                load_piece(n)
            sp.wait_ge(dft_done, NT)
            sp.wait_ge(tr_done, B)
            sp.dma_start(x_cm, x_chan.rearrange("b (a p) n -> p (b a) n", p=P)).then_inc(xcm_in, 16)
            for n in range(2 * EARLY, 2 * EARLY + NSTG):
                load_piece(n)
            for b in range(B):
                sp.wait_ge(t_done, b + 1)
                sp.dma_start(out_rows[:, 2 * b:2 * b + 2, :], xt[:, 2 * b:2 * b + 2, :]).then_inc(t_out, 16)
                sp.wait_ge(xhi_done, 2 * b + 2)
                sp.wait_ge(xlo_done, 2 * b + 2)
                sp.dma_start(xn_dram[:, 2 * b:2 * b + 2, :], xrow[:, b % 2]).then_inc(xn_out[b % 2], 16)
            for n in range(2 * EARLY + NSTG, 2 * E):
                load_piece(n)

        @block.gpsimd
        def _(pool):
            nc.gpsimd.memset(late[:, NBLK * C:NBLK * C + NT * PAD * PAD], 0.0).then_inc(pad_zero, 1)
            nc.gpsimd.memset(b2c[:, :], 0.0).then_inc(b2_zero, 1)
            nc.gpsimd.memset(zrow, 0.0).then_inc(b2_zero, 1)
            for t in range(NT):
                pool.wait_ge(gate_sig, t // CG + 1)
                if t == 0:
                    pool.wait_ge(tr_copied, B)
                    pool.wait_ge(b2_done, 1)
                nc.gpsimd.tensor_tensor(
                    out=gated[:, t].rearrange("p (h w) -> p h w", w=W), in0=xln_pad[:, t, 1:1 + H, 1:1 + W],
                    in1=sg[:, t, 0:H].unsqueeze(2).broadcast_to([P, H, W]), op=ALU.mult).then_inc(gate_row, 1)
            for u in range(NT // 2):
                pool.wait_ge(fm_done, 1)
                if u >= 2:
                    pool.wait_ge(map_done, u - 1)
                for s in range(2):
                    t = 2 * u + s
                    nc.gpsimd.tensor_tensor(
                        out=rf[:, u % 2, s * PX:(s + 1) * PX].rearrange("p (i j) -> p i j", j=W),
                        in0=cc("resize").unsqueeze(2).broadcast_to([P, H, W]),
                        in1=fm[:, t, :].unsqueeze(1).broadcast_to([P, H, W]), op=ALU.mult).then_inc(rf_done, 1)

            pool.wait_ge(table_done, 1)
            pool.wait_ge(spare_set, 32)
            pool.wait_ge(t_out, 16 * B)
            for s in range(2):
                pool.wait_ge(xn_out[s], 16 * (B // 2))

            def gather_start(s, index):
                nc.gpsimd.indirect_dma_start(
                    out=xg[:, s, :], out_offset=None, in_=xn_rows,
                    in_offset=bass.IndirectOffsetOnAxis(ap=index.bitcast(U32), axis=0),
                ).then_inc(g_in[s], 16)

            for s in range(2):
                gather_start(s, idx[:, s:s + 1])

            def body(i, s, ahead):
                nc.gpsimd.tensor_copy(idxc[:, 2 + s:3 + s], idx[:, bass.ds(i, 1)]).then_inc(sum_index, 1)
                if ahead:
                    pool.wait_ge(xT_mm, i + 1)
                    nc.gpsimd.tensor_copy(idxc[:, s:s + 1], idx[:, bass.ds(i + 2, 1)]).then_inc(gather_index, 1)
                    pool.wait_ge(table_done, 1)
                    pool.wait_ge(gather_index, i + 1)
                    gather_start(s, idxc[:, s:s + 1])
                pool.wait_ge(table_done, 1)
                pool.wait_ge(sum_index, i + 1)
                pool.wait_ge(y_done, i + 1)
                nc.gpsimd.indirect_dma_start(
                    out=out, out_offset=bass.IndirectOffsetOnAxis(ap=idxc[:, 2 + s:3 + s].bitcast(U32), axis=0),
                    in_=yb[:, s, :], in_offset=None, compute_op=ALU.add).then_inc(add_out, 16)
                pool.wait_ge(add_out, 16 * i + 16)

            with pool.Fori(0, (TILES - 3) // 2) as j:
                for s in range(2):
                    body(2 * j + s, s, True)
            for i in range((TILES - 3) // 2 * 2, TILES):
                body(i, i % 2, i + 2 < TILES)

        @block.scalar
        def _(act):
            pieces = [0]

            def split_hi():
                n = pieces[0]
                pieces[0] += 1
                act.wait_ge(stg_in[n % NSTG], 16 * (n // NSTG + 1))
                if n == 2 * EARLY:
                    act.wait_ge(logit_mm, 1)
                    act.wait_ge(zt_done, B)
                nc.scalar.activation(wpiece(n, 0), stg[:, n % NSTG, :], ACT.Copy, scale=WS).then_inc(hi_done, 1)

            act.wait_ge(exp_in, 1)
            nc.scalar.activation(prow[:, 2 * CG:3 * CG], prow[:, CG:2 * CG], ACT.Exp).then_inc(exp_done, 1)
            def deviation(dst, var, eps, done):
                nc.scalar.activation(dst, var, ACT.Sqrt, bias=eps[:, 0:1]).then_inc(done, 1)

            act.wait_ge(eps_set, 1)
            for b in range(2):
                act.wait_ge(var_c, b + 1)
                deviation(rstd[:, 2 * b:2 * b + 2], mv[:, 2 * b:2 * b + 2, 1], eps_c, dev_c)
            act.wait_ge(pad_zero, 1)
            for b in range(B):
                if b + 2 < B:
                    act.wait_ge(var_c, b + 3)
                    deviation(rstd[:, 2 * b + 4:2 * b + 6], mv[:, 2 * b + 4:2 * b + 6, 1], eps_c, dev_c)
                act.wait_ge(tr_done, b + 1)
                nc.scalar.activation(inner(2 * b, 2), ps[:, b % 2, :].rearrange("p (t h w) -> p t h w", t=2, w=W),
                                     ACT.Copy).then_inc(tr_copied, 1)
                for t in (2 * b, 2 * b + 1):
                    act.wait_ge(dft_done, t + 1)
                    if t >= 2:
                        act.wait_ge(mag_done, t - 1)
                    nc.scalar.activation(sq[:, t % 2, :], ps[:, 2 + t % 2, 0:2 * NF], ACT.Square).then_inc(sq_done, 1)
            for g in range(2):
                act.wait_ge(gate_mm, g + 1)
                n = NT // 2
                nc.scalar.activation(sg[:, g * n:(g + 1) * n, :],
                                     ps[:, GB[g], 0:256].rearrange("p (t n) -> p t n", t=n),
                                     ACT.Sigmoid, bias=col("b1"), scale=1.0 / H).then_inc(gate_sig, 1)
            for _ in range(2):
                split_hi()
            act.wait_ge(mag_done, NT)
            nc.scalar.activation(mag, mag, ACT.Sqrt).then_inc(root_done, 1)
            for _ in range(4):
                split_hi()
            act.wait_ge(var_g, 1)
            deviation(grs[:, :], gmv[:, :, 1], eps_g, dev_g)
            act.wait_ge(exp_in, 2)
            nc.scalar.activation(s2r[:, 1, :], s2r[:, 0, :], ACT.Exp).then_inc(exp_done, 1)
            for _ in range(2):
                split_hi()
            for t in range(NT):
                act.wait_ge(map_done, t // 2 + 1)
                if t == 0:
                    act.wait_ge(coef_done, NT + 1)
                if t >= 2:
                    act.wait_ge(z_done, t - 1)
                u = t // 2
                nc.scalar.activation(sig[:, t % 2, :], ps[:, WB[u % 4], (t % 2) * PX:(t % 2 + 1) * PX],
                                     ACT.Sigmoid, bias=bias[:, t:t + 1]).then_inc(sig_done, 1)
            for k in range(NBLK):
                b = k // 2
                if k % 2 == 0:
                    for n in ((0, 1) if k == 0 else (b + 1,)):
                        if n < B:
                            act.wait_ge(var_t, n + 1)
                            deviation(trs[:, 2 * n:2 * n + 2], tmv[:, 2 * n:2 * n + 2, 1], eps_g, dev_t)
                act.wait_ge(xn_done, k + 1)
                if k % 2 == 0 and b >= 2:
                    act.wait_ge(xn_out[b % 2], 16 * (b // 2))
                nc.scalar.activation(xrow[:, b % 2, k % 2, 0:C], xn[:, k % 2, :], ACT.Copy).then_inc(xhi_done, 1)
            act.wait_ge(logit_done, 1)
            nc.scalar.activation(sgl[:, :, :], lg[:, :, :], ACT.Sigmoid).then_inc(sigl_done, 1)
            for _ in range(2 * (E - EARLY)):
                split_hi()

            act.wait_ge(table_done, 1)

            def gelu(i, s, first=False):
                e = act.value_load(texp[0:1, bass.ds(i, 1)], min_val=0, max_val=E - 1)
                act.wait_ge(l1_mm, i + 1)
                if not first:
                    act.wait_ge(h_done, i - 1)
                for f in range(FC):
                    a = nc.scalar.activation(hid[:, s, f * P:(f + 1) * P], h_ps(s)[:, f * P:(f + 1) * P],
                                             ACT.Gelu_apprx_tanh,
                                             bias=par[:, bass.ds(e * FC + (PAR["b1e"].start + f), 1)],
                                             scale=1.0 / (XS * WS))
                a.then_inc(gelu_done, 1)

            for i in range(2):
                gelu(i, i, True)
            with act.Fori(1, (TILES - 1) // 2) as j:
                for s in range(2):
                    gelu(2 * j + s, s)
            for i in range((TILES - 1) // 2 * 2, TILES):
                gelu(i, i % 2)

        @block.tensor
        def _(pe):
            ident = cc("ident")
            dft = cc("dft").rearrange("p (c n) -> p c n", c=DC)
            pe.wait_ge(const_in, 48)
            pe.wait_ge(small_ready, 1)
            for a in range(HALVES):
                m = pe.matmul(ps[:, 5, 0:E], w1d[:, :], par[:, PAR["wg"].start + a * E:PAR["wg"].start + (a + 1) * E],
                              start=(a == 0), stop=(a == HALVES - 1))
            m.then_inc(small_mm, 1)
            for b in range(B):
                pe.wait_ge(ln_done, b + 1)
                if b >= 2:
                    pe.wait_ge(tr_copied, b - 1)
                for a in range(HALVES):
                    for k in range(2):
                        m = pe.transpose(ps[:, b % 2, (2 * a + k) * P:(2 * a + k + 1) * P],
                                         xln_tok[:, 2 * b + k, a * P:(a + 1) * P], ident)
                m.then_inc(tr_done, 1)
                for a in range(HALVES):
                    t = 2 * b + a
                    if t >= 2:
                        pe.wait_ge(sq_done, t - 1)
                    for k in range(2):
                        m = pe.matmul(ps[:, 2 + t % 2, 0:2 * NF], xln_tok[:, 2 * b + k, a * P:(a + 1) * P],
                                      dft[:, k, :], start=(k == 0), stop=(k == 1))
                    m.then_inc(dft_done, 1)
            pe.wait_ge(small_ready, 2)
            for g in range(2):
                n = NT // 2
                pe.wait_ge(rc_done, (g + 1) * B // 2)
                pe.matmul(ps[:, GB[g], 0:256], w1d[:, :],
                          rc[:, g * n:(g + 1) * n, :].rearrange("p t n -> p (t n)"),
                          start=True, stop=True).then_inc(gate_mm, 1)
            pe.wait_ge(tapw_done, 1)

            def taps(u):
                if u >= 4:
                    pe.wait_ge(sig_done, 2 * (u - 4) + 2)
                for k in range(9):
                    m = pe.matmul(ps[:, WB[u % 4], :], tapw[:, k, :],
                                  xln_pad[:, 2 * u:2 * u + 2, k // 3:k // 3 + H, k % 3:k % 3 + W],
                                  start=(k == 0), stop=False)

            def rest(u):
                pe.wait_ge(rf_done, 2 * u + 2)
                pe.matmul(ps[:, WB[u % 4], :], wfpd[:, :], rf[:, u % 2, :], start=False, stop=False)
                for t in (2 * u, 2 * u + 1):
                    pe.wait_ge(coef_done, t + 1)
                    m = pe.matmul(ps[:, WB[u % 4], (t % 2) * PX:(t % 2 + 1) * PX], coefw[:, t, :], gated[:, t, :],
                                  start=False, stop=(t % 2 == 1))
                m.then_inc(map_done, 1)

            taps(0)
            pe.wait_ge(small_ready, 3)
            pe.matmul(ps[0:NT, 5, 128:256], dwm[:, :], wpwd[:, :], start=True, stop=False)
            pe.matmul(ps[0:NT, 5, 128:256], ones_row[0:1, 0:NT],
                      par[0:1, PAR["bpwrow"]], start=False, stop=True).then_inc(small_mm, 1)
            pe.wait_ge(gate_sig, 2)
            taps(1)
            pe.wait_ge(small_ready, 4)
            pe.transpose(ps[:, 5, 256:256 + NT], s2r[:, 2, :], ident[0:NT, 0:NT]).then_inc(small_mm, 1)
            taps(2)
            pe.wait_ge(small_ready, 5)
            pe.matmul(ps[:, 5, 288:288 + NT], cc("blocks"), bterm[:, :], start=True, stop=True).then_inc(small_mm, 1)
            taps(3)
            def back(b):
                if b == 0:
                    pe.wait_ge(xcm_in, 16)
                if b >= 2:
                    pe.wait_ge(t_done, b - 1)
                pe.wait_ge(z_done, 2 * b + 2)
                for k in range(2):
                    for a in range(HALVES):
                        m = pe.transpose(ps[:, 2 + b % 2, (2 * k + a) * P:(2 * k + a + 1) * P],
                                         z[:, 2 * b + a, k * P:(k + 1) * P], ident)
                m.then_inc(zt_done, 1)
                for k in range(2):
                    o = (2 * b + k) * E
                    for n, (src, a) in enumerate([(x_cm, 0), (x_cm, 1), (z, 0), (z, 1)]):
                        m = pe.matmul(ps[:, 4, o:o + E], src[:, 2 * b + a, k * P:(k + 1) * P], wgc[:, a, :],
                                      start=(n == 0), stop=(n == 3))
                if b == B - 1:
                    m.then_inc(logit_mm, 1)

            for u in range(NT // 2):
                rest(u)
                if u + 4 < NT // 2:
                    taps(u + 4)
                if u >= 2:
                    back(u - 2)
            for b in range(B - 2, B):
                back(b)

            pe.wait_ge(sel_done, 1)
            ones16, before16 = c16[:, C16["ones"]], c16[:, C16["earlier"]]
            selv = sel16[:, :, :].rearrange("p k e -> p (k e)")
            pre = ps[:, 5, 0:(NBLK + 1) * E].rearrange("p (k e) -> p k e", e=E)
            pe.matmul(pre[:, 0:NBLK, :], before16, sel16[:, :, :], start=True, stop=False, skip_group_check=True)
            for k in range(NBLK):
                n = NBLK - k
                m = pe.matmul(pre[:, k + 1:NBLK + 1, :], ones16,
                              sel16[:, k:k + 1, :].broadcast_to([P, n, E]), start=False, stop=(k == NBLK - 1),
                              skip_group_check=True)
            m.then_inc(prefix_mm, 1)
            table = ps[:, 7, 0:2 * TCOL]
            for a in range(2):
                pe.wait_ge(hot_done, a + 1)
                for k in range(NBLK):
                    m = pe.matmul(table, hot[:, a, k, :], pay[:, a, k].rearrange("p v i -> p (v i)"),
                                  start=(a == 0 and k == 0), stop=(a == 1 and k == NBLK - 1))
            m.then_inc(table_mm, 1)

            pe.wait_ge(table_done, 1)
            pe.wait_ge(b2_done, 1)
            pe.wait_ge(hi_done, 2 * E)
            pe.wait_ge(lo_done, 2 * E)
            ident16 = c16[:, C16["ident"]]

            def turn(i, s, n):
                pe.wait_ge(g_in[s], n)
                for c in range(4):
                    m = pe.transpose(xT_ps[:, c * P:(c + 1) * P], xg[:, s, c * P:(c + 1) * P], ident16)
                m.then_inc(xT_mm, 1)

            def expert(i):
                return pe.value_load(texp[0:1, bass.ds(i, 1)], min_val=0, max_val=E - 1)

            def layer1(i, s, first=False):
                e = expert(i)
                pe.wait_ge(xT_done, i + 1)
                if not first:
                    pe.wait_ge(gelu_done, i - 1)
                for f in range(FC):
                    dst = h_ps(s)[:, f * P:(f + 1) * P]
                    for c in range(DC):
                        hi = wt[:, bass.ds(e * EXPERT + (c * F + f * P), P)]
                        lo = wt[:, bass.ds(e * EXPERT + (2 * PIECE + c * F + f * P), P)]
                        pe.matmul(dst, hi, xT[:, s, c * P:(c + 1) * P], start=(c == 0 and f % 4 == 0), stop=False,
                                  skip_group_check=True)
                        pe.matmul(dst, hi, xT[:, s, (2 + c) * P:(3 + c) * P], start=False, stop=False,
                                  skip_group_check=True)
                        m = pe.matmul(dst, lo, xT[:, s, c * P:(c + 1) * P], start=False, stop=(c == DC - 1),
                                      skip_group_check=True)
                m.then_inc(l1_mm, 1)

            def layer2(i, s, first=False):
                e = expert(i)
                pe.wait_ge(h_done, i + 1)
                if not first:
                    pe.wait_ge(y_done, i - 1)
                dst = y_ps(s)
                for f in range(FC):
                    hi = wt[:, bass.ds(e * EXPERT + (PIECE + f * C), C)]
                    lo = wt[:, bass.ds(e * EXPERT + (3 * PIECE + f * C), C)]
                    pe.matmul(dst, hhi[:, s, f * P:(f + 1) * P], hi, start=(f == 0), stop=False)
                    pe.matmul(dst, hhi[:, s, f * P:(f + 1) * P], lo, start=False, stop=False)
                    pe.matmul(dst, hlo[:, s, f * P:(f + 1) * P], hi, start=False, stop=False)
                pe.matmul(dst, c16[:, C16["bias"]], b2c[:, bass.ds(e * C, C)], start=False, stop=True).then_inc(l2_mm, 1)

            turn(0, 0, 16)
            layer1(0, 0, True)
            turn(1, 1, 16)
            layer1(1, 1, True)
            turn(2, 0, 32)
            layer2(0, 0, True)
            with pe.Fori(1, (TILES - 1) // 2) as j:
                layer1(2 * j, 0)
                turn(2 * j + 1, 1, 16 * j + 16)
                layer2(2 * j - 1, 1)
                layer1(2 * j + 1, 1)
                turn(2 * j + 2, 0, 16 * j + 32)
                layer2(2 * j, 0)
            layer1(TILES - 1, 0)
            layer2(TILES - 2, 1)
            layer2(TILES - 1, 0)

        @block.vector
        def _(dve):
            v = nc.vector
            steps = [0]

            def link(ins):
                steps[0] += 1
                ins.then_inc(dve_step, 1)
                dve.wait_ge(dve_step, steps[0])

            pieces = [0]

            def split_lo():
                n = pieces[0]
                pieces[0] += 1
                dve.wait_ge(hi_done, n + 1)
                v.scalar_tensor_tensor(out=wpiece(n, 1), in0=stg[:, n % NSTG, :], scalar=WS, in1=wpiece(n, 0),
                                       op0=ALU.mult, op1=ALU.subtract).then_inc(lo_done, 1)

            def diag(dst, row):
                return v.tensor_tensor(out=dst.rearrange("p (g c) -> p g c", c=CG),
                                       in0=cc("blocks").rearrange("p (g c) -> p g c", c=CG),
                                       in1=row.unsqueeze(1).broadcast_to([P, P // CG, CG]), op=ALU.mult)

            dve.wait_ge(const_in, 48)
            v.memset(eps_c, EPS_C)
            v.memset(eps_g, EPS_G).then_inc(eps_set, 1)
            v.memset(ones_row[:, :], 1.0)
            v.memset(w1d[:, :], 1.0 / C).then_inc(small_ready, 1)
            s1row, e1, m1 = prow[:, 0:CG], prow[:, 2 * CG:3 * CG], pcol[:, 0:1]
            link(v.tensor_reduce(out=m1, in_=par[:, PAR["betarow"]], axis=AX_X, op=ALU.max))
            v.tensor_scalar(prow[:, CG:2 * CG], par[:, PAR["betarow"]], m1, None, ALU.subtract).then_inc(exp_in, 1)

            def stats_c(b):
                if b % 2 == 0:
                    dve.wait_ge(x_in[b // 2], 16)
                for k in (2 * b, 2 * b + 1):
                    ins = v.bn_stats(bn6[:, k, :], xt[:, k, :])
                link(ins)
                for k in (2 * b, 2 * b + 1):
                    ins = v.bn_aggr(mv[:, k, :], bn6[:, k, :])
                ins.then_inc(var_c, 1)

            def norm_c(b):
                dve.wait_ge(dev_c, b + 1)
                link(v.reciprocal(rstd[:, 2 * b:2 * b + 2], rstd[:, 2 * b:2 * b + 2]))
                for k in (2 * b, 2 * b + 1):
                    ins = v.tensor_scalar(xln_tok[:, k, :], xt[:, k, :], mv[:, k, 0:1], rstd[:, k:k + 1],
                                          ALU.subtract, ALU.mult)
                ins.then_inc(ln_done, 1)

            def sums(b):
                dve.wait_ge(tr_copied, b + 1)
                v.tensor_reduce(out=rc[:, 2 * b:2 * b + 2, 0:H], in_=inner(2 * b, 2), axis=AX_X, op=ALU.add)
                v.tensor_reduce(out=rc[:, 2 * b:2 * b + 2, H:H + W], in_=inner(2 * b, 2).rearrange("p t h w -> p t w h"),
                                axis=AX_X, op=ALU.add).then_inc(rc_done, 1)

            def power(t):
                dve.wait_ge(sq_done, t + 1)
                if t == 0:
                    dve.wait_ge(spare_set, 32)
                v.scalar_tensor_tensor(out=mag[:, t, :], in0=sq[:, t % 2, 0:NF], scalar=TINY, in1=sq[:, t % 2, NF:2 * NF],
                                       op0=ALU.max, op1=ALU.add).then_inc(mag_done, 1)

            for b in range(3):
                stats_c(b)
            for b in range(2):
                norm_c(b)
            dve.wait_ge(b2_in, 16)
            dve.wait_ge(b2_zero, 1)
            link(v.tensor_scalar(b2hi, b2f, WS, None, ALU.mult))
            link(v.scalar_tensor_tensor(out=b2lo, in0=b2f, scalar=WS, in1=b2hi, op0=ALU.mult, op1=ALU.subtract))
            link(v.tensor_scalar(b2lo, b2lo, cst[0:2, 1:2], None, ALU.mult))
            v.scalar_tensor_tensor(out=b2c[0:2, :], in0=b2hi, scalar=cst[0:2, 0:1], in1=b2lo,
                                   op0=ALU.mult, op1=ALU.add).then_inc(b2_done, 1)
            dve.wait_ge(exp_done, 1)
            link(v.tensor_reduce(out=pcol[:, 1:2], in_=e1, axis=AX_X, op=ALU.add))
            link(v.reciprocal(pcol[:, 2:3], pcol[:, 1:2]))
            link(v.tensor_scalar(s1row, e1, pcol[:, 2:3], None, ALU.mult))
            v.tensor_tensor(out=prow[:, 3 * CG:4 * CG], in0=s1row, in1=par[:, PAR["wpw"]], op=ALU.mult)
            link(v.tensor_tensor(out=prow[:, 4 * CG:5 * CG], in0=s1row, in1=cc("own"), op=ALU.mult))
            vcol, s1col = pcol[:, 3:4], pcol[:, 4:5]
            v.tensor_reduce(out=vcol, in_=prow[:, 3 * CG:4 * CG], axis=AX_X, op=ALU.add)
            link(v.tensor_reduce(out=s1col, in_=prow[:, 4 * CG:5 * CG], axis=AX_X, op=ALU.add))
            v.tensor_scalar(pcol[:, 5:14], par[:, PAR["wdw"]], vcol, None, ALU.mult)
            link(v.tensor_scalar(pcol[:, 14:15], vcol, col("bdw"), None, ALU.mult))
            v.scalar_tensor_tensor(out=pcol[:, 15:16], in0=s1col, scalar=col("bpw"), in1=pcol[:, 14:15],
                                   op0=ALU.mult, op1=ALU.add)
            for k in range(9):
                ins = v.tensor_scalar(tapw[:, k, :], cc("blocks"), pcol[:, 5 + k:6 + k], None, ALU.mult)
            ins.then_inc(tapw_done, 1)
            dve.wait_ge(small_mm, 1)
            for a in range(HALVES):
                v.tensor_tensor(out=wgc[:, a, :], in0=par[:, PAR["wg"].start + a * E:PAR["wg"].start + (a + 1) * E],
                                in1=ps[:, 5, 0:E], op=ALU.subtract)
            diag(w1d[:, :], par[:, PAR["w1"]]).then_inc(small_ready, 1)
            diag(wpwd[:, :], par[:, PAR["wpw"]])
            link(v.tensor_reduce(out=prow[:, 5 * CG:6 * CG], in_=par[:, PAR["wfp"]].rearrange("p (o c) -> p o c", c=CG),
                                 axis=AX_X, op=ALU.add))
            diag(wfpd[:, :], prow[:, 5 * CG:6 * CG])
            for b in range(2, B):
                if b + 1 < B:
                    stats_c(b + 1)
                norm_c(b)
                sums(b - 2)
                power(2 * (b - 2))
                power(2 * (b - 2) + 1)
            for b in (B - 2, B - 1):
                sums(b)
                power(2 * b)
                power(2 * b + 1)

            dve.wait_ge(rc_done, B)
            link(v.tensor_reduce(out=tot[:, :], in_=rc[:, :, 0:H], axis=AX_X, op=ALU.add))
            v.tensor_copy(r3[:, :, 1:2], tot[:, :].unsqueeze(2))
            v.tensor_tensor(out=r3[:, :, 0:1], in0=tot[:, :].unsqueeze(2), in1=rc[:, :, H - 1:H], op=ALU.subtract)
            v.tensor_tensor(out=r3[:, :, 2:3], in0=tot[:, :].unsqueeze(2), in1=rc[:, :, 0:1], op=ALU.subtract)
            for n, c in ((0, W - 1), (1, 0)):
                v.tensor_copy(q3[:, :, 1, n:n + 1], rc[:, :, H + c:H + c + 1])
                for d, r in ((0, H - 1), (2, 0)):
                    ins = v.tensor_tensor(out=q3[:, :, d, n:n + 1], in0=rc[:, :, H + c:H + c + 1],
                                          in1=xln_pad[:, :, 1 + r, 1 + c:2 + c], op=ALU.subtract)
            link(ins)
            v.tensor_copy(s9[:, :, :, 1], r3[:, :, :])
            v.tensor_tensor(out=s9[:, :, :, 0], in0=r3[:, :, :], in1=q3[:, :, :, 0], op=ALU.subtract)
            link(v.tensor_tensor(out=s9[:, :, :, 2], in0=r3[:, :, :], in1=q3[:, :, :, 1], op=ALU.subtract))
            s9v = s9[:, :, :, :].rearrange("p t a b -> p t (a b)")
            link(v.tensor_tensor(out=s9v, in0=s9v, in1=par[:, PAR["wdw"]].unsqueeze(1).broadcast_to([P, NT, 9]),
                                 op=ALU.mult))
            link(v.tensor_reduce(out=dwm[:, :], in_=s9v, axis=AX_X, op=ALU.add))
            v.tensor_scalar(dwm[:, :], dwm[:, :], 1.0 / PX, col("bdw"), ALU.mult, ALU.add).then_inc(small_ready, 1)

            def gate(t):
                dve.wait_ge(gate_row, t + 1)
                gv = gated[:, t].rearrange("p (h w) -> p h w", w=W)
                v.tensor_tensor(out=gv, in0=gv, in1=sg[:, t, H:H + W].unsqueeze(1).broadcast_to([P, H, W]),
                                op=ALU.mult).then_inc(gated_done, 1)

            dve.wait_ge(small_mm, 2)
            logits = ps[0:NT, 5, 128:256].rearrange("p (g c) -> p g c", c=CG)
            row = lambda n: s2r[:, n, :].rearrange("p (g c) -> p g c", c=CG)
            wide = lambda n: s2s[:, n, :].unsqueeze(2).broadcast_to([NT, P // CG, CG])
            link(v.tensor_reduce(out=s2s[:, 0, :], in_=logits, axis=AX_X, op=ALU.max))
            v.tensor_tensor(out=row(0), in0=logits, in1=wide(0), op=ALU.subtract).then_inc(exp_in, 1)
            split_lo()
            split_lo()
            dve.wait_ge(root_done, 1)
            v.tensor_reduce(out=fm[:, :, :], in_=mag.rearrange("p t (i j) -> p t i j", j=KW), axis=AX_X,
                            op=ALU.add).then_inc(fm_done, 1)
            for t in range(NT):
                gate(t)
                if t > 0:
                    dve.wait_ge(gated_done, t)
                    v.bn_stats(gbn6[:, t - 1, :], gated[:, t - 1, :])
            dve.wait_ge(gated_done, NT)
            link(v.bn_stats(gbn6[:, NT - 1, :], gated[:, NT - 1, :]))
            for t in range(NT):
                ins = v.bn_aggr(gmv[:, t, :], gbn6[:, t, :])
            ins.then_inc(var_g, 1)
            for _ in range(4):
                split_lo()
            dve.wait_ge(dev_g, 1)
            dve.wait_ge(exp_done, 2)
            link(v.tensor_reduce(out=s2s[:, 1, :], in_=row(1), axis=AX_X, op=ALU.add))
            link(v.reciprocal(s2s[:, 0, :], s2s[:, 1, :]))
            v.tensor_tensor(out=row(2), in0=row(1), in1=wide(0), op=ALU.mult).then_inc(small_ready, 1)
            link(v.reciprocal(grs[:, :], grs[:, :]))
            v.tensor_scalar(grs[:, :], grs[:, :], col("gamma"), None, ALU.mult)
            dve.wait_ge(small_mm, 3)
            link(v.tensor_copy(s2c[:, :], ps[:, 5, 256:256 + NT]))
            link(v.tensor_tensor(out=coef[:, :], in0=s2c[:, :], in1=grs[:, :], op=ALU.mult))
            link(v.tensor_tensor(out=bterm[:, :], in0=coef[:, :], in1=gmv[:, :, 0], op=ALU.mult))
            link(v.scalar_tensor_tensor(out=bterm[:, :], in0=s2c[:, :], scalar=col("beta"), in1=bterm[:, :],
                                        op0=ALU.mult, op1=ALU.subtract))
            v.tensor_scalar(bterm[:, :], bterm[:, :], pcol[:, 15:16], None, ALU.add).then_inc(small_ready, 1)
            for t in range(NT):
                v.tensor_scalar(coefw[:, t, :], cc("blocks"), coef[:, t:t + 1], None, ALU.mult).then_inc(coef_done, 1)
            dve.wait_ge(small_mm, 4)
            v.tensor_scalar(bias[:, :], ps[:, 5, 288:288 + NT], col("bfp"), None, ALU.add).then_inc(coef_done, 1)
            split_lo()
            split_lo()

            def apply_gate(t):
                dve.wait_ge(sig_done, t + 1)
                v.tensor_tensor(out=z[:, t, :].rearrange("p (h w) -> p h w", w=W), in0=inner(t, 1)[:, 0],
                                in1=sig[:, t % 2, :].rearrange("p (h w) -> p h w", w=W), op=ALU.mult).then_inc(z_done, 1)

            def add_x(b):
                dve.wait_ge(zt_done, b + 1)
                v.tensor_tensor(out=xt[:, 2 * b:2 * b + 2, :], in0=ps[:, 2 + b % 2, :].rearrange("p (k c) -> p k c", c=C),
                                in1=xt[:, 2 * b:2 * b + 2, :], op=ALU.add).then_inc(t_done, 1)

            def stats_t(b):
                dve.wait_ge(t_done, b + 1)
                for k in (2 * b, 2 * b + 1):
                    ins = v.bn_stats(bn6[:, k, :], xt[:, k, :])
                link(ins)
                for k in (2 * b, 2 * b + 1):
                    ins = v.bn_aggr(tmv[:, k, :], bn6[:, k, :])
                ins.then_inc(var_t, 1)

            def norm_t(b):
                dve.wait_ge(dev_t, b + 1)
                link(v.reciprocal(trs[:, 2 * b:2 * b + 2], trs[:, 2 * b:2 * b + 2]))
                link(v.tensor_scalar(trs64[:, 2 * b:2 * b + 2], trs[:, 2 * b:2 * b + 2], XS, None, ALU.mult))
                for k in (2 * b, 2 * b + 1):
                    if k >= 2:
                        dve.wait_ge(xlo_done, k - 1)
                        dve.wait_ge(xhi_done, k - 1)
                    v.tensor_scalar(xn[:, k % 2, :], xt[:, k, :], tmv[:, k, 0:1], trs64[:, k:k + 1],
                                    ALU.subtract, ALU.mult).then_inc(xn_done, 1)
                for k in (2 * b, 2 * b + 1):
                    dve.wait_ge(xhi_done, k + 1)
                    v.tensor_tensor(out=xrow[:, b % 2, k % 2, C:2 * C], in0=xn[:, k % 2, :],
                                    in1=xrow[:, b % 2, k % 2, 0:C], op=ALU.subtract).then_inc(xlo_done, 1)

            for b in range(B):
                apply_gate(2 * b)
                apply_gate(2 * b + 1)
                if b >= 1:
                    add_x(b - 1)
            add_x(B - 1)
            stats_t(0)
            for b in range(B):
                if b + 1 < B:
                    stats_t(b + 1)
                norm_t(b)

            dve.wait_ge(logit_mm, 1)
            lgv = lg[:, :, :]
            link(v.tensor_tensor(out=lgv, in0=ps[:, 4, 0:NBLK * E].rearrange("p (k e) -> p k e", e=E),
                                 in1=trs[:, :].unsqueeze(2).broadcast_to([P, NBLK, E]), op=ALU.mult))
            dve.wait_ge(dve_step, steps[0])
            mine = lgv.unsqueeze(3).broadcast_to([P, NBLK, E, E])
            other = lgv.unsqueeze(2).broadcast_to([P, NBLK, E, E])
            v.tensor_tensor(out=cmp_eq, in0=other, in1=mine, op=ALU.is_equal).then_inc(logit_done, 1)
            v.tensor_tensor(out=cmp_gt, in0=other, in1=mine, op=ALU.is_gt)
            dve.wait_ge(logit_done, 1)
            link(v.tensor_tensor(out=cmp_eq.rearrange("p k e j -> p k (e j)"), in0=cmp_eq.rearrange("p k e j -> p k (e j)"),
                                 in1=cc("before").unsqueeze(1).broadcast_to([P, NBLK, E * E]), op=ALU.mult))
            link(v.tensor_tensor(out=cmp_gt, in0=cmp_gt, in1=cmp_eq, op=ALU.add))
            link(v.tensor_reduce(out=rank[:, :, :], in_=cmp_gt, axis=AX_X, op=ALU.add))
            v.tensor_scalar(sel16[:, :, :], rank[:, :, :], float(TOP_K), None, ALU.is_lt).then_inc(sel_done, 1)
            for a in range(TOP_K):
                v.tensor_scalar(pick[:, a], rank[:, :, :], float(a), None, ALU.is_equal)
            dve.wait_ge(prefix_mm, 1)
            link(v.tensor_copy(cnt[:, :], ps[:, 5, NBLK * E:(NBLK + 1) * E]))
            over = view(2176, E * NBLK).rearrange("p (e k) -> p e k", k=NBLK)
            link(v.tensor_tensor(out=over, in0=cnt[:, :].unsqueeze(2).broadcast_to([P, E, NBLK]),
                                 in1=cc("steps").unsqueeze(1).broadcast_to([P, E, NBLK]), op=ALU.is_gt))
            link(v.tensor_reduce(out=tcnt[:, 0, :], in_=over, axis=AX_X, op=ALU.add))
            low = view(2176 + E * NBLK, E * E).rearrange("p (e j) -> p e j", j=E)
            link(v.tensor_tensor(out=low, in0=cc("before").rearrange("p (e j) -> p e j", j=E),
                                 in1=tcnt[:, 0, :].unsqueeze(1).broadcast_to([P, E, E]), op=ALU.mult))
            link(v.tensor_reduce(out=tcnt[:, 1, :], in_=low, axis=AX_X, op=ALU.add))
            v.tensor_tensor(out=tcnt[:, 2, :], in0=tcnt[:, 1, :], in1=tcnt[:, 0, :], op=ALU.add)
            link(v.tensor_scalar(cnt[:, :], tcnt[:, 1, :], float(P), None, ALU.mult))
            link(v.tensor_tensor(out=slot[:, :, :], in0=ps[:, 5, 0:NBLK * E].rearrange("p (k e) -> p k e", e=E),
                                 in1=cnt[:, :].unsqueeze(1).broadcast_to([P, NBLK, E]), op=ALU.add))
            dve.wait_ge(sigl_done, 1)
            picked = view(1152, 4 * NBLK * E).rearrange("p (a v k e) -> p a v k e", a=2, v=2, k=NBLK)
            for a in range(TOP_K):
                v.tensor_tensor(out=picked[:, a, 0], in0=pick[:, a], in1=slot[:, :, :], op=ALU.mult)
                ins = v.tensor_tensor(out=picked[:, a, 1], in0=pick[:, a], in1=sgl[:, :, :], op=ALU.mult)
            link(ins)
            link(v.tensor_reduce(out=psum_pick[:, :, :, :].rearrange("p a v k -> p (a v k)"),
                                 in_=picked.rearrange("p a v k e -> p (a v k) e"), axis=AX_X, op=ALU.add))
            link(v.tensor_copy(sloti[:, 0], psum_pick[:, :, 0, :]))
            v.tensor_scalar(sloti[:, 1], sloti[:, 0], 7, None, ALU.arith_shift_right)
            link(v.tensor_scalar(sloti[:, 2], sloti[:, 0], P - 1, None, ALU.bitwise_and))
            v.tensor_copy(slotf[:, 0], sloti[:, 1])
            link(v.tensor_copy(slotf[:, 1], sloti[:, 2]))
            link(v.tensor_tensor(out=slotf[:, 2], in0=cc("token").unsqueeze(1).broadcast_to([P, 2, NBLK]),
                                 in1=slotf[:, 1], op=ALU.subtract))
            dve.wait_ge(t_out, 16 * B)
            for a in range(TOP_K):
                v.tensor_tensor(out=hot[:, a], in0=cc("iota").unsqueeze(1).broadcast_to([P, NBLK, P]),
                                in1=slotf[:, 1, a, :].unsqueeze(2).broadcast_to([P, NBLK, P]), op=ALU.is_equal)
                link(v.tensor_tensor(out=pay[:, a, :, 0, :], in0=cc("tiles").unsqueeze(1).broadcast_to([P, NBLK, TCOL]),
                                     in1=slotf[:, 0, a, :].unsqueeze(2).broadcast_to([P, NBLK, TCOL]), op=ALU.is_equal))
                link(v.tensor_tensor(out=pay[:, a, :, 1, :], in0=pay[:, a, :, 0, :],
                                     in1=psum_pick[:, a, 1, :].unsqueeze(2).broadcast_to([P, NBLK, TCOL]), op=ALU.mult))
                v.tensor_tensor(out=pay[:, a, :, 0, :], in0=pay[:, a, :, 0, :],
                                in1=slotf[:, 2, a, :].unsqueeze(2).broadcast_to([P, NBLK, TCOL]), op=ALU.mult)\
                    .then_inc(hot_done, 1)
            link(v.tensor_tensor(out=texpf[:, :, :], in0=cc("tiles").unsqueeze(2).broadcast_to([P, TCOL, E]),
                                 in1=tcnt[:, 2, :].unsqueeze(1).broadcast_to([P, TCOL, E]), op=ALU.is_ge))
            link(v.tensor_reduce(out=texpc[:, :], in_=texpf[:, :, :], axis=AX_X, op=ALU.add))
            v.tensor_scalar(texp[:, :], texpc[:, :], float(E - 1), None, ALU.min)
            for _ in range(2 * (E - EARLY)):
                split_lo()
            dve.wait_ge(table_mm, 1)
            v.tensor_scalar(idx[:, :], ps[:, 7, 0:TCOL], cc("spare"), None, ALU.add)
            v.tensor_scalar(gates[:, :], ps[:, 7, TCOL:2 * TCOL], 1.0 / (WS * HS), None, ALU.mult).then_inc(table_done, 1)

            def rows_T(i, s, first=False):
                dve.wait_ge(xT_mm, i + 1)
                if not first:
                    dve.wait_ge(l1_mm, i - 1)
                v.tensor_copy(xT[:, s, :], xT_ps).then_inc(xT_done, 1)

            def halves(i, s, at, first=False):
                dve.wait_ge(gelu_done, i + 1)
                if not first:
                    dve.wait_ge(l2_mm, i - 1)
                v.tensor_scalar(hhi[:, s, :], hid[:, s, :], HS, None, ALU.mult).then_inc(dve_step, 1)
                dve.wait_ge(dve_step, at + 1)
                v.scalar_tensor_tensor(out=hlo[:, s, :], in0=hid[:, s, :], scalar=HS, in1=hhi[:, s, :],
                                       op0=ALU.mult, op1=ALU.subtract).then_inc(h_done, 1)

            def scaled(i, s, first=False):
                dve.wait_ge(l2_mm, i + 1)
                if not first:
                    dve.wait_ge(add_out, 16 * i - 16)
                v.tensor_scalar(yb[:, s, :], y_ps(s), gates[:, bass.ds(i, 1)], None, ALU.mult).then_inc(y_done, 1)

            base = steps[0]
            rows_T(0, 0, True)
            rows_T(1, 1, True)
            halves(0, 0, base, True)
            rows_T(2, 0)
            halves(1, 1, base + 1, True)
            scaled(0, 0, True)
            rows_T(3, 1)
            halves(2, 0, base + 2)
            scaled(1, 1, True)
            with dve.Fori(1, (TILES - 3) // 2) as j:
                rows_T(2 * j + 2, 0)
                halves(2 * j + 1, 1, 2 * j + (base + 1))
                scaled(2 * j, 0)
                rows_T(2 * j + 3, 1)
                halves(2 * j + 2, 0, 2 * j + (base + 2))
                scaled(2 * j + 1, 1)
            i = (TILES - 3) // 2 * 2
            rows_T(i + 2, 0)
            halves(i + 1, 1, base + i + 1)
            scaled(i, 0)
            halves(i + 2, 0, base + i + 2)
            scaled(i + 1, 1)
            scaled(i + 2, 0)


def _constants():
    p = np.arange(P)
    c = np.zeros((P, NCONST), np.float32)
    c[:, CONST["ident"]] = np.eye(P)
    c[:, CONST["blocks"]] = p[:, None] // CG == p[None, :] // CG
    pos = np.clip((np.arange(H) + 0.5) * (CG / H) - 0.5, 0, CG - 1)
    lo = np.floor(pos).astype(int)
    resize = np.zeros((CG, H))
    np.add.at(resize, (lo, np.arange(H)), 1 - (pos - lo))
    np.add.at(resize, (np.minimum(lo + 1, CG - 1), np.arange(H)), pos - lo)
    c[:, CONST["resize"]] = resize[p % CG] / KW
    c[:, CONST["own"]] = p[:, None] % CG == np.arange(CG)
    c[:, CONST["iota"]] = p[None, :]
    c[:, CONST["tiles"]] = np.arange(TCOL)
    c[:, CONST["before"]] = (np.arange(E)[None, :] < np.arange(E)[:, None]).ravel()
    c[:, CONST["steps"]] = P * np.arange(NBLK)
    c[:, CONST["token"]] = P * np.arange(NBLK)[None, :] + p[:, None] - NTOK
    c[:, CONST["spare"]] = NTOK + p[:, None]
    px = np.arange(PX)
    n = np.arange(NF)
    turns = (np.outer(px // W, n // KW) % H) / H + (np.outer(px % W, n % KW) % W) / W
    quarter = np.round(turns * 4 * 4).astype(int) % 16
    cos = np.cos(2 * np.pi * np.arange(16) / 16)
    cos[[4, 12]] = 0
    dft = np.concatenate([cos[quarter], cos[(quarter - 4) % 16]], 1) / np.sqrt(PX)
    c[:, CONST["dft"]] = dft.reshape(DC, P, 2 * NF).transpose(1, 0, 2).reshape(P, -1)
    h = np.zeros((P, NC16), np.float16)
    h[:, C16["ident"]] = np.eye(P)
    h[:, C16["earlier"]] = p[:, None] < p[None, :]
    h[:, C16["ones"]] = 1
    h[:, C16["bias"]] = HS
    return c, h


def kernel(**inputs):
    import concourse.bacc as bacc
    from concourse.bass_utils import run_bass_kernel_spmd

    a = {k: np.asarray(v) for k, v in inputs.items()}
    g = {k[len("L0_conv_"):]: v for k, v in a.items() if k.startswith("L0_conv_")}
    f = {k[len("L0_ffn_"):]: v for k, v in a.items() if k.startswith("L0_ffn_")}
    n = P // CG
    par = np.zeros((P, NPAR), np.float32)
    par[:, PAR["w1"]] = np.tile(g["w1"].T, (n, 1))
    par[:, PAR["wpw"]] = np.tile(g["w_pw"].T, (n, 1))
    par[:, PAR["wdw"]] = np.tile(g["w_dw"].reshape(CG, 9), (n, 1))
    for name, key in (("b1", "b1"), ("gamma", "gn_gamma"), ("beta", "gn_beta"), ("bdw", "b_dw"), ("bpw", "b_pw"), ("bfp", "b_fp")):
        par[:, PAR[name]] = np.tile(g[key][:, None], (n, 1))
    par[:, PAR["betarow"]] = g["gn_beta"][None, :]
    par[:, PAR["wfp"]] = g["w_fp"].reshape(1, -1)
    par[:, PAR["bpwrow"]] = np.tile(g["b_pw"], n)[None, :]
    par[:, PAR["wg"]] = f["Wg"].reshape(HALVES, P, E).transpose(1, 0, 2).reshape(P, -1)
    par[:, PAR["b1e"]] = f["b1"].reshape(E, FC, P).transpose(2, 0, 1).reshape(P, -1)
    const, const16 = _constants()
    x = a["x"]
    arrays = {
        "x_tok": np.ascontiguousarray(x.reshape(B, C, PX).transpose(0, 2, 1).reshape(NTOK, C)),
        "x_chan": np.ascontiguousarray(x.reshape(B, C, PX)),
        "const": const, "const16": const16, "params": par,
        "w1": np.ascontiguousarray(f["W1"]), "w2": np.ascontiguousarray(f["W2"]),
        "b2": np.ascontiguousarray(np.tile(f["b2"].reshape(1, -1), (2, 1))),
    }
    nc = bacc.Bacc("TRN2", target_bir_lowering=False, num_devices=1)
    aps = [nc.dram_tensor(k, v.shape, mybir.dt.from_np(v.dtype), kind="ExternalInput").ap() for k, v in arrays.items()]
    out = nc.dram_tensor("out", (TROWS, C), F32, kind="ExternalOutput").ap()
    build(nc, *aps, out)
    r = run_bass_kernel_spmd(nc, [arrays], core_ids=[0])
    got = np.asarray(r.results[0]["out"])[:NTOK]
    return np.ascontiguousarray(got.reshape(B, PX, C).transpose(0, 2, 1)).reshape(B, C, H, W)
```

```python
from contextlib import ExitStack

import numpy as np

import concourse.bass as bass
from concourse import mybir

ALU = mybir.AluOpType
ACT = mybir.ActivationFunctionType
AX_X = mybir.AxisListType.X
F32 = mybir.dt.float32
F16 = mybir.dt.float16
I32 = mybir.dt.int32
U32 = mybir.dt.uint32

P = 128
B, C, H, W = 8, 256, 16, 16
PX = H * W
NTOK = B * PX
NBLK = NTOK // P
CG = 8
HALVES = C // P
NT = B * HALVES
PAD = H + 2
KW = W // 2 + 1
NF = H * KW
E, F, TOP_K = 8, 1024, 2
DC, FC = C // P, F // P
SLOTS_MOST = NTOK * TOP_K
TILES = SLOTS_MOST // P + E - 1
TCOL = TILES + 1
TROWS = NTOK + P
EPS_C, EPS_G = 1e-6, 1e-5
XS, WS, HS = 64.0, 256.0, 16.0
PIECE = DC * F
EXPERT = 4 * PIECE
EARLY = 4
NSTG = 2
UNROLL = 4
LEAD = 3
PEELED = 4
ROUNDS = (TILES - PEELED - 1) // UNROLL
TINY = 1e-30

def _columns(widths):
    at, out = 0, {}
    for name, n in widths:
        out[name] = slice(at, at + n)
        at += n
    return out, at

CONST, NCONST = _columns([("ident", P), ("blocks", P), ("resize", H), ("own", CG), ("iota", P),
                          ("tiles", TCOL), ("before", E * E), ("steps", NBLK), ("token", NBLK),
                          ("spare", 1), ("dft", DC * 2 * NF)])
C16, NC16 = _columns([("ident", P), ("earlier", P), ("ones", P), ("bias", P)])
PAR, NPAR = _columns([("w1", CG), ("wpw", CG), ("wdw", 9), ("b1", 1), ("gamma", 1), ("beta", 1),
                      ("bdw", 1), ("bpw", 1), ("bfp", 1), ("betarow", CG), ("wfp", CG * CG),
                      ("bpwrow", P), ("wg", HALVES * E), ("b1e", E * FC)])


def build(nc, x_tok, x_chan, const, const16, params, w1, w2, b2, out):
    with ExitStack() as ctx:
        def sb(name, shape, dt=F32):
            return ctx.enter_context(nc.sbuf_tensor(name, shape, dt))

        def sem(name):
            return ctx.enter_context(nc.semaphore(name))

        xn_rows = nc.dram_tensor("xn_rows", [TROWS, 2 * C], F16, kind="Internal").ap()

        wt = sb("wt", [P, E * EXPERT], F16)
        late = wt[:, EARLY * EXPERT:].bitcast(F32)
        xln_tok = late[:, 0:NBLK * C].rearrange("p (k c) -> p k c", c=C)
        x_cm = late[:, 0:NT * PX].rearrange("p (t n) -> p t n", n=PX)
        o = NBLK * C
        xln_pad = late[:, o:o + NT * PAD * PAD].rearrange("p (t h w) -> p t h w", h=PAD, w=PAD)
        o += NT * PAD * PAD
        gated = late[:, o:o + NT * PX].rearrange("p (t n) -> p t n", n=PX)
        z = gated
        b2f = late[0:2, o:o + E * C]
        b2hi = late[0:2, o + E * C:o + E * C * 3 // 2].bitcast(F16)
        b2lo = late[0:2, o + E * C * 3 // 2:o + 2 * E * C].bitcast(F16)
        o += NT * PX
        mag = late[:, o:o + NT * NF].rearrange("p (t n) -> p t n", n=NF)

        zrow = late[:, o:o + C].bitcast(F16)
        o += NT * NF
        sg = late[:, o:o + NT * (H + W)].rearrange("p (t n) -> p t n", n=H + W)
        o += NT * (H + W)

        xt = sb("xt", [P, NBLK, C])
        stg = sb("stg", [P, NSTG, PIECE])
        fb = sb("fb", [P, 6144])
        cst = sb("cst", [P, NCONST])
        c16 = sb("c16", [P, NC16], F16)
        par = sb("par", [P, NPAR])
        b2c = sb("b2c", [P, E * C], F16)

        def view(at, n, dt=F32):
            v = fb[:, at:at + n]
            return v if dt is F32 else v.bitcast(dt)

        tapw = view(0, 9 * P).rearrange("p (k m) -> p k m", m=P)
        coefw = view(1152, NT * P).rearrange("p (t m) -> p t m", m=P)
        rf = view(3200, 2 * 512).rearrange("p (s n) -> p s n", s=2)
        sq = view(4224, 2 * 2 * NF).rearrange("p (s n) -> p s n", s=2)
        sig = view(4800, 2 * PX).rearrange("p (s n) -> p s n", s=2)
        xn = view(5312, 2 * C).rearrange("p (s n) -> p s n", s=2)
        xrow = view(0, 1024, F16).rearrange("p (b k n) -> p b k n", b=2, k=2)
        cmp_gt = view(1152, NBLK * E * E).rearrange("p (k e j) -> p k e j", e=E, j=E)
        cmp_eq = view(2176, NBLK * E * E).rearrange("p (k e j) -> p k e j", e=E, j=E)
        pay = view(3200, 2 * NBLK * 2 * TCOL).rearrange("p (a k v i) -> p a k v i", a=2, k=NBLK, v=2)
        hot = xt[:, :, :].rearrange("p k c -> p (k c)").rearrange("p (a k r) -> p a k r", a=2, r=P)
        xg = view(0, UNROLL * C, F16).rearrange("p (s n) -> p s n", s=UNROLL)
        xT = view(1024, 512, F16).rearrange("p (s n) -> p s n", s=2)
        hid = view(1536, 2 * F).rearrange("p (s n) -> p s n", s=2)
        hhi = view(3584, F, F16).rearrange("p (s n) -> p s n", s=2)
        hlo = view(4608, F, F16).rearrange("p (s n) -> p s n", s=2)
        yb = view(5632, 2 * C).rearrange("p (s n) -> p s n", s=2)

        bn6 = sb("bn6", [P, NBLK, 6])
        mv = sb("mv", [P, NBLK, 2])
        rstd = sb("rstd", [P, NBLK])
        eps = sb("eps", [P, 2])
        eps_c, eps_g = eps[:, 0:1], eps[:, 1:2]
        ones_row = sb("ones_row", [1, NT])
        w1d = view(5824, P)
        wpwd = sb("wpwd", [P, P])
        wfpd = view(5952, P)
        prow = sb("prow", [P, 16 * CG])
        pcol = sb("pcol", [P, 32])
        wgc = sb("wgc", [P, HALVES, E])
        rc = sb("rc", [P, NT, H + W])
        gbn6 = sb("gbn6", [P, NT, 6])
        gmv = sb("gmv", [P, NT, 2])
        grs = sb("grs", [P, NT])
        tot = sb("tot", [P, NT])
        r3 = sb("r3", [P, NT, 3])
        q3 = sb("q3", [P, NT, 3, 2])
        s9 = late[:, o:o + NT * 9].rearrange("p (t a b) -> p t a b", a=3, b=3)
        dwm = sb("dwm", [P, NT])
        s2r = sb("s2r", [NT, 4, P])
        s2s = sb("s2s", [NT, 2, 16])
        s2c = sb("s2c", [P, NT])
        coef = sb("coef", [P, NT])
        bterm = sb("bterm", [P, NT])
        bias = sb("bias", [P, NT])
        fm = sb("fm", [P, NT, H])
        tmv = sb("tmv", [P, NBLK, 2])
        trs = sb("trs", [P, NBLK])
        trs64 = sb("trs64", [P, NBLK])
        lg = sb("lg", [P, NBLK, E])
        sgl = sb("sgl", [P, NBLK, E])
        rank = sb("rank", [P, NBLK, E])
        sel16 = sb("sel16", [P, NBLK, E], F16)
        cnt = sb("cnt", [P, E])
        tcnt = sb("tcnt", [P, 3, E])
        slot = sb("slot", [P, NBLK, E])
        pick = view(1664, 2 * NBLK * E).rearrange("p (a k e) -> p a k e", a=2, k=NBLK)
        psum_pick = sb("picked", [P, 2, 2, NBLK])
        sloti = sb("sloti", [P, 3, 2, NBLK], I32)
        slotf = sb("slotf", [P, 3, 2, NBLK])
        texpf = view(1920, TCOL * E).rearrange("p (i e) -> p i e", e=E)
        texpc = sb("texpc", [P, TCOL])
        texp = sb("texp", [P, TCOL], I32)
        idx = sb("idx", [P, TCOL], I32)
        idxc = sb("idxc", [P, UNROLL + 2], I32)
        gates = sb("gates", [P, TCOL])

        ps = ctx.enter_context(nc.psum_tensor("ps", [P, 8, 512], F32))
        WB = [6, 7, 0, 1]
        GB = [4, 7]
        xT_ps = ps[:, 0, 0:256].bitcast(F16)

        def h_ps(s):
            return ps[:, 1 + 2 * s:3 + 2 * s, :].rearrange("p b n -> p (b n)")

        def y_ps(s):
            return ps[:, 5 + s, :]

        const_in = sem("const_in")
        x_in = [sem(f"x_in{i}") for i in range(4)]
        stg_in = [sem(f"stg_in{i}") for i in range(NSTG)]
        b2_in = sem("b2_in")
        xcm_in = sem("xcm_in")
        spare_set = sem("spare_set")
        t_out = sem("t_out")
        xn_out = [sem(f"xn_out{i}") for i in range(2)]
        hi_done = sem("hi_done")
        lo_done = sem("lo_done")
        dve_step = sem("dve_step")
        pad_zero = sem("pad_zero")
        ln_done = sem("ln_done")
        eps_set = sem("eps_set")
        var_c = sem("var_c")
        dev_c = sem("dev_c")
        var_g = sem("var_g")
        dev_g = sem("dev_g")
        var_t = sem("var_t")
        dev_t = sem("dev_t")
        tr_done = sem("tr_done")
        tr_copied = sem("tr_copied")
        dft_done = sem("dft_done")
        sq_done = sem("sq_done")
        mag_done = sem("mag_done")
        root_done = sem("root_done")
        fm_done = sem("fm_done")
        rf_done = sem("rf_done")
        rc_done = sem("rc_done")
        gate_mm = sem("gate_mm")
        gate_sig = sem("gate_sig")
        gate_row = sem("gate_row")
        gated_done = sem("gated_done")
        small_ready = sem("small_ready")
        small_mm = sem("small_mm")
        exp_in = sem("exp_in")
        exp_done = sem("exp_done")
        tapw_done = sem("tapw_done")
        coef_done = sem("coef_done")
        map_done = sem("map_done")
        sig_done = sem("sig_done")
        z_done = sem("z_done")
        zt_done = sem("zt_done")
        t_done = sem("t_done")
        xn_done = sem("xn_done")
        xhi_done = sem("xhi_done")
        xlo_done = sem("xlo_done")
        logit_mm = sem("logit_mm")
        logit_done = sem("logit_done")
        sigl_done = sem("sigl_done")
        sel_done = sem("sel_done")
        prefix_mm = sem("prefix_mm")
        hot_done = sem("hot_done")
        table_mm = sem("table_mm")
        table_done = sem("table_done")
        b2_done = sem("b2_done")
        b2_zero = sem("b2_zero")
        first_index = sem("first_index")
        gather_index = sem("gather_index")
        sum_index = sem("sum_index")
        g_in = [sem(f"g_in{i}") for i in range(UNROLL)]
        add_out = sem("add_out")
        xT_mm = sem("xT_mm")
        xT_done = sem("xT_done")
        l1_mm = sem("l1_mm")
        gelu_done = sem("gelu_done")
        hhi_done = sem("hhi_done")
        h_done = sem("h_done")
        ylo_done = sem("ylo_done")
        l2_mm = sem("l2_mm")
        y_done = sem("y_done")

        def wpiece(n, part):
            at = (n // 2) * EXPERT
            if n % 2 == 0:
                return wt[:, at + part * PIECE:at + (part + 1) * PIECE]
            return wt[:, at + 2 * PIECE:at + EXPERT].rearrange("p (f v d) -> p f v d", f=FC, v=2)[:, :, part, :]

        def staged(n):
            v = stg[:, n % NSTG, :]
            return v if n % 2 == 0 else v.rearrange("p (f d) -> p f d", f=FC)

        w1_dram = w1.rearrange("e (c p) f -> e p c f", p=P)
        w2_dram = w2.rearrange("e (c p) d -> e p c d", p=P)
        out_rows = out[0:NTOK, :].rearrange("(k p) c -> p k c", p=P)
        xn_dram = xn_rows[0:NTOK, :].rearrange("(k p) c -> p k c", p=P)
        x_dram = x_tok.rearrange("(k p) c -> p k c", p=P)
        col = lambda name, k=0: par[:, PAR[name].start + k:PAR[name].start + k + 1]
        cc = lambda name: cst[:, CONST[name]]
        inner = lambda t0, n: xln_pad[:, t0:t0 + n, 1:1 + H, 1:1 + W]

        def moe(engine, step):
            for n in range(PEELED):
                step(0, n)
            with engine.Fori(0, ROUNDS) as j:
                for n in range(PEELED, PEELED + UNROLL):
                    step(j, n)
            for n in range(PEELED + UNROLL * ROUNDS, TILES):
                step(0, n)

        block = ctx.enter_context(nc.Block())

        @block.sync
        def _(sp):
            sp.dma_start(x_t := xt[:, 0:4, :], x_dram[:, 0:4, :]).then_inc(x_in[0], 16)
            sp.dma_start(par[:, :], params).then_inc(const_in, 16)
            sp.dma_start(cst[:, :], const).then_inc(const_in, 16)
            sp.dma_start(c16[:, :], const16).then_inc(const_in, 16)
            for q in range(1, 4):
                sp.dma_start(xt[:, 4 * q:4 * q + 4, :], x_dram[:, 4 * q:4 * q + 4, :]).then_inc(x_in[q], 16)

            sp.dma_start(b2f, b2).then_inc(b2_in, 16)

            sp.wait_ge(b2_zero, 2)
            sp.dma_start(xn_rows[NTOK:TROWS, :], zrow).then_inc(spare_set, 16)
            sp.dma_start(out[NTOK:TROWS, :], zrow.bitcast(F32)).then_inc(spare_set, 16)

            def load_piece(n):
                if n >= NSTG:
                    sp.wait_ge(hi_done, n - NSTG + 1)
                    sp.wait_ge(lo_done, n - NSTG + 1)
                src = (w1_dram if n % 2 == 0 else w2_dram)[n // 2]
                dst = stg[:, n % NSTG, :].rearrange("p (c f) -> p c f", c=DC if n % 2 == 0 else FC)
                sp.dma_start(dst, src).then_inc(stg_in[n % NSTG], 16)

            for n in range(2 * EARLY):
                load_piece(n)
            sp.wait_ge(dft_done, NT)
            sp.wait_ge(tr_done, B)
            sp.dma_start(x_cm, x_chan.rearrange("b (a p) n -> p (b a) n", p=P)).then_inc(xcm_in, 16)
            for n in range(2 * EARLY, 2 * EARLY + NSTG):
                load_piece(n)
            for b in range(B):
                sp.wait_ge(t_done, b + 1)
                sp.dma_start(out_rows[:, 2 * b:2 * b + 2, :], xt[:, 2 * b:2 * b + 2, :]).then_inc(t_out, 16)
                sp.wait_ge(xhi_done, 2 * b + 2)
                sp.wait_ge(xlo_done, 2 * b + 2)
                sp.dma_start(xn_dram[:, 2 * b:2 * b + 2, :], xrow[:, b % 2]).then_inc(xn_out[b % 2], 16)
            for n in range(2 * EARLY + NSTG, 2 * E):
                load_piece(n)

        @block.gpsimd
        def _(pool):
            nc.gpsimd.memset(late[:, NBLK * C:NBLK * C + NT * PAD * PAD], 0.0).then_inc(pad_zero, 1)
            nc.gpsimd.memset(b2c[:, :], 0.0).then_inc(b2_zero, 1)
            nc.gpsimd.memset(zrow, 0.0).then_inc(b2_zero, 1)
            for t in range(NT):
                pool.wait_ge(gate_sig, t // CG + 1)
                if t == 0:
                    pool.wait_ge(tr_copied, B)
                    pool.wait_ge(b2_done, 1)
                nc.gpsimd.tensor_tensor(
                    out=gated[:, t].rearrange("p (h w) -> p h w", w=W), in0=xln_pad[:, t, 1:1 + H, 1:1 + W],
                    in1=sg[:, t, 0:H].unsqueeze(2).broadcast_to([P, H, W]), op=ALU.mult).then_inc(gate_row, 1)
            for u in range(NT // 2):
                pool.wait_ge(fm_done, 1)
                if u >= 2:
                    pool.wait_ge(map_done, u - 1)
                for s in range(2):
                    t = 2 * u + s
                    nc.gpsimd.tensor_tensor(
                        out=rf[:, u % 2, s * PX:(s + 1) * PX].rearrange("p (i j) -> p i j", j=W),
                        in0=cc("resize").unsqueeze(2).broadcast_to([P, H, W]),
                        in1=fm[:, t, :].unsqueeze(1).broadcast_to([P, H, W]), op=ALU.mult).then_inc(rf_done, 1)

            pool.wait_ge(table_done, 1)
            pool.wait_ge(spare_set, 32)
            pool.wait_ge(t_out, 16 * B)
            for s in range(2):
                pool.wait_ge(xn_out[s], 16 * (B // 2))

            def gather(j, n):
                i, g = UNROLL * j + n, n % UNROLL
                if n >= UNROLL:
                    pool.wait_ge(xT_mm, i - (UNROLL - 1))
                copied, count = (gather_index, i - (UNROLL - 1)) if n >= UNROLL else (first_index, n + 1)
                nc.gpsimd.tensor_copy(idxc[:, g:g + 1], idx[:, bass.ds(i, 1)]).then_inc(copied, 1)
                pool.wait_ge(table_done, 1)
                pool.wait_ge(copied, count)
                nc.gpsimd.indirect_dma_start(
                    out=xg[:, g, :], out_offset=None, in_=xn_rows,
                    in_offset=bass.IndirectOffsetOnAxis(ap=idxc[:, g:g + 1].bitcast(U32), axis=0),
                ).then_inc(g_in[g], 16)

            def add(j, n):
                i, s = UNROLL * j + n, n % 2
                if n > 0:
                    pool.wait_ge(add_out, 16 * i)
                pool.wait_ge(y_done, i + 1)
                nc.gpsimd.tensor_copy(idxc[:, UNROLL + s:UNROLL + s + 1], idx[:, bass.ds(i, 1)])\
                    .then_inc(sum_index, 1)
                pool.wait_ge(table_done, 1)
                pool.wait_ge(sum_index, i + 1)
                nc.gpsimd.indirect_dma_start(
                    out=out, out_offset=bass.IndirectOffsetOnAxis(
                        ap=idxc[:, UNROLL + s:UNROLL + s + 1].bitcast(U32), axis=0),
                    in_=yb[:, s, :], in_offset=None, compute_op=ALU.add).then_inc(add_out, 16)

            def step(j, n):
                if n >= LEAD:
                    add(j, n - LEAD)
                if not isinstance(j, int) or n + LEAD < TILES:
                    gather(j, n + LEAD)

            for n in range(LEAD):
                gather(0, n)
            moe(pool, step)
            for n in range(TILES - LEAD, TILES):
                add(0, n)
            pool.wait_ge(add_out, 16 * TILES)

        @block.scalar
        def _(act):
            pieces = [0]

            def split_hi():
                n = pieces[0]
                pieces[0] += 1
                act.wait_ge(stg_in[n % NSTG], 16 * (n // NSTG + 1))
                if n == 2 * EARLY:
                    act.wait_ge(logit_mm, 1)
                    act.wait_ge(zt_done, B)
                nc.scalar.activation(wpiece(n, 0), staged(n), ACT.Copy, scale=WS).then_inc(hi_done, 1)

            act.wait_ge(exp_in, 1)
            nc.scalar.activation(prow[:, 2 * CG:3 * CG], prow[:, CG:2 * CG], ACT.Exp).then_inc(exp_done, 1)
            def deviation(dst, var, eps, done):
                nc.scalar.activation(dst, var, ACT.Sqrt, bias=eps[:, 0:1]).then_inc(done, 1)

            act.wait_ge(eps_set, 1)
            for b in range(2):
                act.wait_ge(var_c, b + 1)
                deviation(rstd[:, 2 * b:2 * b + 2], mv[:, 2 * b:2 * b + 2, 1], eps_c, dev_c)
            act.wait_ge(pad_zero, 1)
            for b in range(B):
                if b + 2 < B:
                    act.wait_ge(var_c, b + 3)
                    deviation(rstd[:, 2 * b + 4:2 * b + 6], mv[:, 2 * b + 4:2 * b + 6, 1], eps_c, dev_c)
                act.wait_ge(tr_done, b + 1)
                nc.scalar.activation(inner(2 * b, 2), ps[:, b % 2, :].rearrange("p (t h w) -> p t h w", t=2, w=W),
                                     ACT.Copy).then_inc(tr_copied, 1)
                for t in (2 * b, 2 * b + 1):
                    act.wait_ge(dft_done, t + 1)
                    if t >= 2:
                        act.wait_ge(mag_done, t - 1)
                    nc.scalar.activation(sq[:, t % 2, :], ps[:, 2 + t % 2, 0:2 * NF], ACT.Square).then_inc(sq_done, 1)
            for g in range(2):
                act.wait_ge(gate_mm, g + 1)
                n = NT // 2
                nc.scalar.activation(sg[:, g * n:(g + 1) * n, :],
                                     ps[:, GB[g], 0:256].rearrange("p (t n) -> p t n", t=n),
                                     ACT.Sigmoid, bias=col("b1"), scale=1.0 / H).then_inc(gate_sig, 1)
            for _ in range(2):
                split_hi()
            act.wait_ge(mag_done, NT)
            nc.scalar.activation(mag, mag, ACT.Sqrt).then_inc(root_done, 1)
            for _ in range(4):
                split_hi()
            act.wait_ge(var_g, 1)
            deviation(grs[:, :], gmv[:, :, 1], eps_g, dev_g)
            act.wait_ge(exp_in, 2)
            nc.scalar.activation(s2r[:, 1, :], s2r[:, 0, :], ACT.Exp).then_inc(exp_done, 1)
            for _ in range(2):
                split_hi()
            for t in range(NT):
                act.wait_ge(map_done, t // 2 + 1)
                if t == 0:
                    act.wait_ge(coef_done, NT + 1)
                if t >= 2:
                    act.wait_ge(z_done, t - 1)
                u = t // 2
                nc.scalar.activation(sig[:, t % 2, :], ps[:, WB[u % 4], (t % 2) * PX:(t % 2 + 1) * PX],
                                     ACT.Sigmoid, bias=bias[:, t:t + 1]).then_inc(sig_done, 1)
            for k in range(NBLK):
                b = k // 2
                if k % 2 == 0:
                    for n in ((0, 1) if k == 0 else (b + 1,)):
                        if n < B:
                            act.wait_ge(var_t, n + 1)
                            deviation(trs[:, 2 * n:2 * n + 2], tmv[:, 2 * n:2 * n + 2, 1], eps_g, dev_t)
                act.wait_ge(xn_done, k + 1)
                if k % 2 == 0 and b >= 2:
                    act.wait_ge(xn_out[b % 2], 16 * (b // 2))
                nc.scalar.activation(xrow[:, b % 2, k % 2, 0:C], xn[:, k % 2, :], ACT.Copy).then_inc(xhi_done, 1)
            act.wait_ge(logit_done, 1)
            nc.scalar.activation(sgl[:, :, :], lg[:, :, :], ACT.Sigmoid).then_inc(sigl_done, 1)
            for _ in range(2 * (E - EARLY)):
                split_hi()

            act.wait_ge(table_done, 1)

            def step(j, n):
                i, s = UNROLL * j + n, n % 2
                e = act.value_load(texp[0:1, bass.ds(i, 1)], min_val=0, max_val=E - 1)
                act.wait_ge(l1_mm, i + 1)
                if n >= 2:
                    act.wait_ge(h_done, i - 1)
                for f in range(FC):
                    a = nc.scalar.activation(hid[:, s, f * P:(f + 1) * P], h_ps(s)[:, f * P:(f + 1) * P],
                                             ACT.Gelu_apprx_tanh,
                                             bias=par[:, bass.ds(e * FC + (PAR["b1e"].start + f), 1)],
                                             scale=1.0 / (XS * WS))
                a.then_inc(gelu_done, 1)

            moe(act, step)

        @block.tensor
        def _(pe):
            ident = cc("ident")
            dft = cc("dft").rearrange("p (c n) -> p c n", c=DC)
            pe.wait_ge(const_in, 48)
            pe.wait_ge(small_ready, 1)
            for a in range(HALVES):
                m = pe.matmul(ps[:, 5, 0:E], w1d[:, :], par[:, PAR["wg"].start + a * E:PAR["wg"].start + (a + 1) * E],
                              start=(a == 0), stop=(a == HALVES - 1))
            m.then_inc(small_mm, 1)
            for b in range(B):
                pe.wait_ge(ln_done, b + 1)
                if b >= 2:
                    pe.wait_ge(tr_copied, b - 1)
                for a in range(HALVES):
                    for k in range(2):
                        m = pe.transpose(ps[:, b % 2, (2 * a + k) * P:(2 * a + k + 1) * P],
                                         xln_tok[:, 2 * b + k, a * P:(a + 1) * P], ident)
                m.then_inc(tr_done, 1)
                for a in range(HALVES):
                    t = 2 * b + a
                    if t >= 2:
                        pe.wait_ge(sq_done, t - 1)
                    for k in range(2):
                        m = pe.matmul(ps[:, 2 + t % 2, 0:2 * NF], xln_tok[:, 2 * b + k, a * P:(a + 1) * P],
                                      dft[:, k, :], start=(k == 0), stop=(k == 1))
                    m.then_inc(dft_done, 1)
            pe.wait_ge(small_ready, 2)
            for g in range(2):
                n = NT // 2
                pe.wait_ge(rc_done, (g + 1) * B // 2)
                pe.matmul(ps[:, GB[g], 0:256], w1d[:, :],
                          rc[:, g * n:(g + 1) * n, :].rearrange("p t n -> p (t n)"),
                          start=True, stop=True).then_inc(gate_mm, 1)
            pe.wait_ge(tapw_done, 1)

            def taps(u):
                if u >= 4:
                    pe.wait_ge(sig_done, 2 * (u - 4) + 2)
                for k in range(9):
                    m = pe.matmul(ps[:, WB[u % 4], :], tapw[:, k, :],
                                  xln_pad[:, 2 * u:2 * u + 2, k // 3:k // 3 + H, k % 3:k % 3 + W],
                                  start=(k == 0), stop=False)

            def rest(u):
                pe.wait_ge(rf_done, 2 * u + 2)
                pe.matmul(ps[:, WB[u % 4], :], wfpd[:, :], rf[:, u % 2, :], start=False, stop=False)
                for t in (2 * u, 2 * u + 1):
                    pe.wait_ge(coef_done, t + 1)
                    m = pe.matmul(ps[:, WB[u % 4], (t % 2) * PX:(t % 2 + 1) * PX], coefw[:, t, :], gated[:, t, :],
                                  start=False, stop=(t % 2 == 1))
                m.then_inc(map_done, 1)

            taps(0)
            pe.wait_ge(small_ready, 3)
            pe.matmul(ps[0:NT, 5, 128:256], dwm[:, :], wpwd[:, :], start=True, stop=False)
            pe.matmul(ps[0:NT, 5, 128:256], ones_row[0:1, 0:NT],
                      par[0:1, PAR["bpwrow"]], start=False, stop=True).then_inc(small_mm, 1)
            pe.wait_ge(gate_sig, 2)
            taps(1)
            pe.wait_ge(small_ready, 4)
            pe.transpose(ps[:, 5, 256:256 + NT], s2r[:, 2, :], ident[0:NT, 0:NT]).then_inc(small_mm, 1)
            taps(2)
            pe.wait_ge(small_ready, 5)
            pe.matmul(ps[:, 5, 288:288 + NT], cc("blocks"), bterm[:, :], start=True, stop=True).then_inc(small_mm, 1)
            taps(3)
            def back(b):
                if b == 0:
                    pe.wait_ge(xcm_in, 16)
                if b >= 2:
                    pe.wait_ge(t_done, b - 1)
                pe.wait_ge(z_done, 2 * b + 2)
                for k in range(2):
                    for a in range(HALVES):
                        m = pe.transpose(ps[:, 2 + b % 2, (2 * k + a) * P:(2 * k + a + 1) * P],
                                         z[:, 2 * b + a, k * P:(k + 1) * P], ident)
                m.then_inc(zt_done, 1)
                for k in range(2):
                    o = (2 * b + k) * E
                    for n, (src, a) in enumerate([(x_cm, 0), (x_cm, 1), (z, 0), (z, 1)]):
                        m = pe.matmul(ps[:, 4, o:o + E], src[:, 2 * b + a, k * P:(k + 1) * P], wgc[:, a, :],
                                      start=(n == 0), stop=(n == 3))
                if b == B - 1:
                    m.then_inc(logit_mm, 1)

            for u in range(NT // 2):
                rest(u)
                if u + 4 < NT // 2:
                    taps(u + 4)
                if u >= 2:
                    back(u - 2)
            for b in range(B - 2, B):
                back(b)

            pe.wait_ge(sel_done, 1)
            ones16, before16 = c16[:, C16["ones"]], c16[:, C16["earlier"]]
            selv = sel16[:, :, :].rearrange("p k e -> p (k e)")
            pre = ps[:, 5, 0:(NBLK + 1) * E].rearrange("p (k e) -> p k e", e=E)
            pe.matmul(pre[:, 0:NBLK, :], before16, sel16[:, :, :], start=True, stop=False, skip_group_check=True)
            for k in range(NBLK):
                n = NBLK - k
                m = pe.matmul(pre[:, k + 1:NBLK + 1, :], ones16,
                              sel16[:, k:k + 1, :].broadcast_to([P, n, E]), start=False, stop=(k == NBLK - 1),
                              skip_group_check=True)
            m.then_inc(prefix_mm, 1)
            table = ps[:, 7, 0:2 * TCOL]
            for a in range(2):
                pe.wait_ge(hot_done, a + 1)
                for k in range(NBLK):
                    m = pe.matmul(table, hot[:, a, k, :], pay[:, a, k].rearrange("p v i -> p (v i)"),
                                  start=(a == 0 and k == 0), stop=(a == 1 and k == NBLK - 1))
            m.then_inc(table_mm, 1)

            pe.wait_ge(table_done, 1)
            pe.wait_ge(b2_done, 1)
            pe.wait_ge(hi_done, 2 * E)
            pe.wait_ge(lo_done, 2 * E)
            ident16 = c16[:, C16["ident"]]

            def turn(j, n):
                g = n % UNROLL
                pe.wait_ge(g_in[g], 16 * (j + n // UNROLL) + 16)
                for c in range(4):
                    m = pe.transpose(xT_ps[:, c * P:(c + 1) * P], xg[:, g, c * P:(c + 1) * P], ident16)
                m.then_inc(xT_mm, 1)

            expert = [pe.alloc_register(f"expert{n}") for n in range(UNROLL)]

            def load_expert(j, n):
                pe.reg_load(expert[n % UNROLL], texp[0:1, bass.ds(UNROLL * j + n, 1)])

            def step(j, n):
                i, s = UNROLL * j + n, n % 2
                one, two = n < TILES, n >= 2
                if one:
                    e1 = pe.snap(expert[n % UNROLL], min_val=0, max_val=E - 1)
                if two:
                    e2 = pe.snap(expert[(n - 2) % UNROLL], min_val=0, max_val=E - 1)
                if n < 2:
                    pe.wait_ge(xT_done, i + 1)
                else:
                    pe.wait_ge(h_done, i - 1)
                for f in range(FC):
                    for c in range(DC if one else 0):
                        dst = h_ps(s)[:, f * P:(f + 1) * P]
                        hi = wt[:, bass.ds(e1 * EXPERT + (c * F + f * P), P)]
                        lo = wt[:, bass.ds(e1 * EXPERT + (PIECE + c * F + f * P), P)]
                        pe.matmul(dst, hi, xT[:, s, c * P:(c + 1) * P], start=(c == 0 and f % 4 == 0), stop=False,
                                  skip_group_check=True)
                        pe.matmul(dst, hi, xT[:, s, (2 + c) * P:(3 + c) * P], start=False, stop=False,
                                  skip_group_check=True)
                        m = pe.matmul(dst, lo, xT[:, s, c * P:(c + 1) * P], start=False, stop=(c == DC - 1),
                                      skip_group_check=True)
                        if (f, c) == (FC - 1, DC - 1):
                            m.then_inc(l1_mm, 1)
                    if two:
                        w = wt[:, bass.ds(e2 * EXPERT + (2 * PIECE + f * 2 * C), 2 * C)]
                        hi = wt[:, bass.ds(e2 * EXPERT + (2 * PIECE + f * 2 * C), C)]
                        pe.matmul(y_ps(s), hhi[:, s, f * P:(f + 1) * P], w, start=(f == 0), stop=False)
                        pe.matmul(y_ps(s)[:, 0:C], hlo[:, s, f * P:(f + 1) * P], hi, start=False, stop=False)
                    if f == 1 and (not isinstance(j, int) or n + 1 < TILES):
                        turn(j, n + 1)
                    if f == FC // 2 and (not isinstance(j, int) or n + 1 < TILES):
                        load_expert(j, n + 1)
                if two:
                    pe.matmul(y_ps(s)[:, 0:C], c16[:, C16["bias"]], b2c[:, bass.ds(e2 * C, C)],
                              start=False, stop=True).then_inc(l2_mm, 1)

            turn(0, 0)
            load_expert(0, 0)
            moe(pe, step)
            for n in range(TILES, TILES + 2):
                step(0, n)

        @block.vector
        def _(dve):
            v = nc.vector
            steps = [0]

            def link(ins):
                steps[0] += 1
                ins.then_inc(dve_step, 1)
                dve.wait_ge(dve_step, steps[0])

            pieces = [0]

            def split_lo():
                n = pieces[0]
                pieces[0] += 1
                dve.wait_ge(hi_done, n + 1)
                v.scalar_tensor_tensor(out=wpiece(n, 1), in0=staged(n), scalar=WS, in1=wpiece(n, 0),
                                       op0=ALU.mult, op1=ALU.subtract).then_inc(lo_done, 1)

            def diag(dst, row):
                return v.tensor_tensor(out=dst.rearrange("p (g c) -> p g c", c=CG),
                                       in0=cc("blocks").rearrange("p (g c) -> p g c", c=CG),
                                       in1=row.unsqueeze(1).broadcast_to([P, P // CG, CG]), op=ALU.mult)

            dve.wait_ge(const_in, 48)
            v.memset(eps_c, EPS_C)
            v.memset(eps_g, EPS_G).then_inc(eps_set, 1)
            v.memset(ones_row[:, :], 1.0)
            v.memset(w1d[:, :], 1.0 / C).then_inc(small_ready, 1)
            s1row, e1, m1 = prow[:, 0:CG], prow[:, 2 * CG:3 * CG], pcol[:, 0:1]
            link(v.tensor_reduce(out=m1, in_=par[:, PAR["betarow"]], axis=AX_X, op=ALU.max))
            v.tensor_scalar(prow[:, CG:2 * CG], par[:, PAR["betarow"]], m1, None, ALU.subtract).then_inc(exp_in, 1)

            def stats_c(b):
                if b % 2 == 0:
                    dve.wait_ge(x_in[b // 2], 16)
                for k in (2 * b, 2 * b + 1):
                    ins = v.bn_stats(bn6[:, k, :], xt[:, k, :])
                link(ins)
                for k in (2 * b, 2 * b + 1):
                    ins = v.bn_aggr(mv[:, k, :], bn6[:, k, :])
                ins.then_inc(var_c, 1)

            def norm_c(b):
                dve.wait_ge(dev_c, b + 1)
                link(v.reciprocal(rstd[:, 2 * b:2 * b + 2], rstd[:, 2 * b:2 * b + 2]))
                for k in (2 * b, 2 * b + 1):
                    ins = v.tensor_scalar(xln_tok[:, k, :], xt[:, k, :], mv[:, k, 0:1], rstd[:, k:k + 1],
                                          ALU.subtract, ALU.mult)
                ins.then_inc(ln_done, 1)

            def sums(b):
                dve.wait_ge(tr_copied, b + 1)
                v.tensor_reduce(out=rc[:, 2 * b:2 * b + 2, 0:H], in_=inner(2 * b, 2), axis=AX_X, op=ALU.add)
                v.tensor_reduce(out=rc[:, 2 * b:2 * b + 2, H:H + W], in_=inner(2 * b, 2).rearrange("p t h w -> p t w h"),
                                axis=AX_X, op=ALU.add).then_inc(rc_done, 1)

            def power(t):
                dve.wait_ge(sq_done, t + 1)
                if t == 0:
                    dve.wait_ge(spare_set, 32)
                v.scalar_tensor_tensor(out=mag[:, t, :], in0=sq[:, t % 2, 0:NF], scalar=TINY, in1=sq[:, t % 2, NF:2 * NF],
                                       op0=ALU.max, op1=ALU.add).then_inc(mag_done, 1)

            for b in range(3):
                stats_c(b)
            for b in range(2):
                norm_c(b)
            dve.wait_ge(b2_in, 16)
            dve.wait_ge(b2_zero, 1)
            link(v.tensor_scalar(b2hi, b2f, WS, None, ALU.mult))
            link(v.scalar_tensor_tensor(out=b2lo, in0=b2f, scalar=WS, in1=b2hi, op0=ALU.mult, op1=ALU.subtract))
            link(v.tensor_scalar(b2lo, b2lo, cst[0:2, 1:2], None, ALU.mult))
            v.scalar_tensor_tensor(out=b2c[0:2, :], in0=b2hi, scalar=cst[0:2, 0:1], in1=b2lo,
                                   op0=ALU.mult, op1=ALU.add).then_inc(b2_done, 1)
            dve.wait_ge(exp_done, 1)
            link(v.tensor_reduce(out=pcol[:, 1:2], in_=e1, axis=AX_X, op=ALU.add))
            link(v.reciprocal(pcol[:, 2:3], pcol[:, 1:2]))
            link(v.tensor_scalar(s1row, e1, pcol[:, 2:3], None, ALU.mult))
            v.tensor_tensor(out=prow[:, 3 * CG:4 * CG], in0=s1row, in1=par[:, PAR["wpw"]], op=ALU.mult)
            link(v.tensor_tensor(out=prow[:, 4 * CG:5 * CG], in0=s1row, in1=cc("own"), op=ALU.mult))
            vcol, s1col = pcol[:, 3:4], pcol[:, 4:5]
            v.tensor_reduce(out=vcol, in_=prow[:, 3 * CG:4 * CG], axis=AX_X, op=ALU.add)
            link(v.tensor_reduce(out=s1col, in_=prow[:, 4 * CG:5 * CG], axis=AX_X, op=ALU.add))
            v.tensor_scalar(pcol[:, 5:14], par[:, PAR["wdw"]], vcol, None, ALU.mult)
            link(v.tensor_scalar(pcol[:, 14:15], vcol, col("bdw"), None, ALU.mult))
            v.scalar_tensor_tensor(out=pcol[:, 15:16], in0=s1col, scalar=col("bpw"), in1=pcol[:, 14:15],
                                   op0=ALU.mult, op1=ALU.add)
            for k in range(9):
                ins = v.tensor_scalar(tapw[:, k, :], cc("blocks"), pcol[:, 5 + k:6 + k], None, ALU.mult)
            ins.then_inc(tapw_done, 1)
            dve.wait_ge(small_mm, 1)
            for a in range(HALVES):
                v.tensor_tensor(out=wgc[:, a, :], in0=par[:, PAR["wg"].start + a * E:PAR["wg"].start + (a + 1) * E],
                                in1=ps[:, 5, 0:E], op=ALU.subtract)
            diag(w1d[:, :], par[:, PAR["w1"]]).then_inc(small_ready, 1)
            diag(wpwd[:, :], par[:, PAR["wpw"]])
            link(v.tensor_reduce(out=prow[:, 5 * CG:6 * CG], in_=par[:, PAR["wfp"]].rearrange("p (o c) -> p o c", c=CG),
                                 axis=AX_X, op=ALU.add))
            diag(wfpd[:, :], prow[:, 5 * CG:6 * CG])
            for b in range(2, B):
                if b + 1 < B:
                    stats_c(b + 1)
                norm_c(b)
                sums(b - 2)
                power(2 * (b - 2))
                power(2 * (b - 2) + 1)
            for b in (B - 2, B - 1):
                sums(b)
                power(2 * b)
                power(2 * b + 1)

            dve.wait_ge(rc_done, B)
            link(v.tensor_reduce(out=tot[:, :], in_=rc[:, :, 0:H], axis=AX_X, op=ALU.add))
            v.tensor_copy(r3[:, :, 1:2], tot[:, :].unsqueeze(2))
            v.tensor_tensor(out=r3[:, :, 0:1], in0=tot[:, :].unsqueeze(2), in1=rc[:, :, H - 1:H], op=ALU.subtract)
            v.tensor_tensor(out=r3[:, :, 2:3], in0=tot[:, :].unsqueeze(2), in1=rc[:, :, 0:1], op=ALU.subtract)
            for n, c in ((0, W - 1), (1, 0)):
                v.tensor_copy(q3[:, :, 1, n:n + 1], rc[:, :, H + c:H + c + 1])
                for d, r in ((0, H - 1), (2, 0)):
                    ins = v.tensor_tensor(out=q3[:, :, d, n:n + 1], in0=rc[:, :, H + c:H + c + 1],
                                          in1=xln_pad[:, :, 1 + r, 1 + c:2 + c], op=ALU.subtract)
            link(ins)
            v.tensor_copy(s9[:, :, :, 1], r3[:, :, :])
            v.tensor_tensor(out=s9[:, :, :, 0], in0=r3[:, :, :], in1=q3[:, :, :, 0], op=ALU.subtract)
            link(v.tensor_tensor(out=s9[:, :, :, 2], in0=r3[:, :, :], in1=q3[:, :, :, 1], op=ALU.subtract))
            s9v = s9[:, :, :, :].rearrange("p t a b -> p t (a b)")
            link(v.tensor_tensor(out=s9v, in0=s9v, in1=par[:, PAR["wdw"]].unsqueeze(1).broadcast_to([P, NT, 9]),
                                 op=ALU.mult))
            link(v.tensor_reduce(out=dwm[:, :], in_=s9v, axis=AX_X, op=ALU.add))
            v.tensor_scalar(dwm[:, :], dwm[:, :], 1.0 / PX, col("bdw"), ALU.mult, ALU.add).then_inc(small_ready, 1)

            def gate(t):
                dve.wait_ge(gate_row, t + 1)
                gv = gated[:, t].rearrange("p (h w) -> p h w", w=W)
                v.tensor_tensor(out=gv, in0=gv, in1=sg[:, t, H:H + W].unsqueeze(1).broadcast_to([P, H, W]),
                                op=ALU.mult).then_inc(gated_done, 1)

            dve.wait_ge(small_mm, 2)
            logits = ps[0:NT, 5, 128:256].rearrange("p (g c) -> p g c", c=CG)
            row = lambda n: s2r[:, n, :].rearrange("p (g c) -> p g c", c=CG)
            wide = lambda n: s2s[:, n, :].unsqueeze(2).broadcast_to([NT, P // CG, CG])
            link(v.tensor_reduce(out=s2s[:, 0, :], in_=logits, axis=AX_X, op=ALU.max))
            v.tensor_tensor(out=row(0), in0=logits, in1=wide(0), op=ALU.subtract).then_inc(exp_in, 1)
            split_lo()
            split_lo()
            dve.wait_ge(root_done, 1)
            v.tensor_reduce(out=fm[:, :, :], in_=mag.rearrange("p t (i j) -> p t i j", j=KW), axis=AX_X,
                            op=ALU.add).then_inc(fm_done, 1)
            for t in range(NT):
                gate(t)
                if t > 0:
                    dve.wait_ge(gated_done, t)
                    v.bn_stats(gbn6[:, t - 1, :], gated[:, t - 1, :])
            dve.wait_ge(gated_done, NT)
            link(v.bn_stats(gbn6[:, NT - 1, :], gated[:, NT - 1, :]))
            for t in range(NT):
                ins = v.bn_aggr(gmv[:, t, :], gbn6[:, t, :])
            ins.then_inc(var_g, 1)
            for _ in range(4):
                split_lo()
            dve.wait_ge(dev_g, 1)
            dve.wait_ge(exp_done, 2)
            link(v.tensor_reduce(out=s2s[:, 1, :], in_=row(1), axis=AX_X, op=ALU.add))
            link(v.reciprocal(s2s[:, 0, :], s2s[:, 1, :]))
            v.tensor_tensor(out=row(2), in0=row(1), in1=wide(0), op=ALU.mult).then_inc(small_ready, 1)
            link(v.reciprocal(grs[:, :], grs[:, :]))
            v.tensor_scalar(grs[:, :], grs[:, :], col("gamma"), None, ALU.mult)
            dve.wait_ge(small_mm, 3)
            link(v.tensor_copy(s2c[:, :], ps[:, 5, 256:256 + NT]))
            link(v.tensor_tensor(out=coef[:, :], in0=s2c[:, :], in1=grs[:, :], op=ALU.mult))
            link(v.tensor_tensor(out=bterm[:, :], in0=coef[:, :], in1=gmv[:, :, 0], op=ALU.mult))
            link(v.scalar_tensor_tensor(out=bterm[:, :], in0=s2c[:, :], scalar=col("beta"), in1=bterm[:, :],
                                        op0=ALU.mult, op1=ALU.subtract))
            v.tensor_scalar(bterm[:, :], bterm[:, :], pcol[:, 15:16], None, ALU.add).then_inc(small_ready, 1)
            for t in range(NT):
                v.tensor_scalar(coefw[:, t, :], cc("blocks"), coef[:, t:t + 1], None, ALU.mult).then_inc(coef_done, 1)
            dve.wait_ge(small_mm, 4)
            v.tensor_scalar(bias[:, :], ps[:, 5, 288:288 + NT], col("bfp"), None, ALU.add).then_inc(coef_done, 1)
            split_lo()
            split_lo()

            def apply_gate(t):
                dve.wait_ge(sig_done, t + 1)
                v.tensor_tensor(out=z[:, t, :].rearrange("p (h w) -> p h w", w=W), in0=inner(t, 1)[:, 0],
                                in1=sig[:, t % 2, :].rearrange("p (h w) -> p h w", w=W), op=ALU.mult).then_inc(z_done, 1)

            def add_x(b):
                dve.wait_ge(zt_done, b + 1)
                v.tensor_tensor(out=xt[:, 2 * b:2 * b + 2, :], in0=ps[:, 2 + b % 2, :].rearrange("p (k c) -> p k c", c=C),
                                in1=xt[:, 2 * b:2 * b + 2, :], op=ALU.add).then_inc(t_done, 1)

            def stats_t(b):
                dve.wait_ge(t_done, b + 1)
                for k in (2 * b, 2 * b + 1):
                    ins = v.bn_stats(bn6[:, k, :], xt[:, k, :])
                link(ins)
                for k in (2 * b, 2 * b + 1):
                    ins = v.bn_aggr(tmv[:, k, :], bn6[:, k, :])
                ins.then_inc(var_t, 1)

            def norm_t(b):
                dve.wait_ge(dev_t, b + 1)
                link(v.reciprocal(trs[:, 2 * b:2 * b + 2], trs[:, 2 * b:2 * b + 2]))
                link(v.tensor_scalar(trs64[:, 2 * b:2 * b + 2], trs[:, 2 * b:2 * b + 2], XS, None, ALU.mult))
                for k in (2 * b, 2 * b + 1):
                    if k >= 2:
                        dve.wait_ge(xlo_done, k - 1)
                        dve.wait_ge(xhi_done, k - 1)
                    v.tensor_scalar(xn[:, k % 2, :], xt[:, k, :], tmv[:, k, 0:1], trs64[:, k:k + 1],
                                    ALU.subtract, ALU.mult).then_inc(xn_done, 1)
                for k in (2 * b, 2 * b + 1):
                    dve.wait_ge(xhi_done, k + 1)
                    v.tensor_tensor(out=xrow[:, b % 2, k % 2, C:2 * C], in0=xn[:, k % 2, :],
                                    in1=xrow[:, b % 2, k % 2, 0:C], op=ALU.subtract).then_inc(xlo_done, 1)

            for b in range(B):
                apply_gate(2 * b)
                apply_gate(2 * b + 1)
                if b >= 1:
                    add_x(b - 1)
            add_x(B - 1)
            stats_t(0)
            for b in range(B):
                if b + 1 < B:
                    stats_t(b + 1)
                norm_t(b)

            dve.wait_ge(logit_mm, 1)
            lgv = lg[:, :, :]
            link(v.tensor_tensor(out=lgv, in0=ps[:, 4, 0:NBLK * E].rearrange("p (k e) -> p k e", e=E),
                                 in1=trs[:, :].unsqueeze(2).broadcast_to([P, NBLK, E]), op=ALU.mult))
            dve.wait_ge(dve_step, steps[0])
            mine = lgv.unsqueeze(3).broadcast_to([P, NBLK, E, E])
            other = lgv.unsqueeze(2).broadcast_to([P, NBLK, E, E])
            v.tensor_tensor(out=cmp_eq, in0=other, in1=mine, op=ALU.is_equal).then_inc(logit_done, 1)
            v.tensor_tensor(out=cmp_gt, in0=other, in1=mine, op=ALU.is_gt)
            dve.wait_ge(logit_done, 1)
            link(v.tensor_tensor(out=cmp_eq.rearrange("p k e j -> p k (e j)"), in0=cmp_eq.rearrange("p k e j -> p k (e j)"),
                                 in1=cc("before").unsqueeze(1).broadcast_to([P, NBLK, E * E]), op=ALU.mult))
            link(v.tensor_tensor(out=cmp_gt, in0=cmp_gt, in1=cmp_eq, op=ALU.add))
            link(v.tensor_reduce(out=rank[:, :, :], in_=cmp_gt, axis=AX_X, op=ALU.add))
            v.tensor_scalar(sel16[:, :, :], rank[:, :, :], float(TOP_K), None, ALU.is_lt).then_inc(sel_done, 1)
            for a in range(TOP_K):
                v.tensor_scalar(pick[:, a], rank[:, :, :], float(a), None, ALU.is_equal)
            dve.wait_ge(prefix_mm, 1)
            link(v.tensor_copy(cnt[:, :], ps[:, 5, NBLK * E:(NBLK + 1) * E]))
            over = view(2176, E * NBLK).rearrange("p (e k) -> p e k", k=NBLK)
            link(v.tensor_tensor(out=over, in0=cnt[:, :].unsqueeze(2).broadcast_to([P, E, NBLK]),
                                 in1=cc("steps").unsqueeze(1).broadcast_to([P, E, NBLK]), op=ALU.is_gt))
            link(v.tensor_reduce(out=tcnt[:, 0, :], in_=over, axis=AX_X, op=ALU.add))
            low = view(2176 + E * NBLK, E * E).rearrange("p (e j) -> p e j", j=E)
            link(v.tensor_tensor(out=low, in0=cc("before").rearrange("p (e j) -> p e j", j=E),
                                 in1=tcnt[:, 0, :].unsqueeze(1).broadcast_to([P, E, E]), op=ALU.mult))
            link(v.tensor_reduce(out=tcnt[:, 1, :], in_=low, axis=AX_X, op=ALU.add))
            v.tensor_tensor(out=tcnt[:, 2, :], in0=tcnt[:, 1, :], in1=tcnt[:, 0, :], op=ALU.add)
            link(v.tensor_scalar(cnt[:, :], tcnt[:, 1, :], float(P), None, ALU.mult))
            link(v.tensor_tensor(out=slot[:, :, :], in0=ps[:, 5, 0:NBLK * E].rearrange("p (k e) -> p k e", e=E),
                                 in1=cnt[:, :].unsqueeze(1).broadcast_to([P, NBLK, E]), op=ALU.add))
            dve.wait_ge(sigl_done, 1)
            picked = view(1152, 4 * NBLK * E).rearrange("p (a v k e) -> p a v k e", a=2, v=2, k=NBLK)
            for a in range(TOP_K):
                v.tensor_tensor(out=picked[:, a, 0], in0=pick[:, a], in1=slot[:, :, :], op=ALU.mult)
                ins = v.tensor_tensor(out=picked[:, a, 1], in0=pick[:, a], in1=sgl[:, :, :], op=ALU.mult)
            link(ins)
            link(v.tensor_reduce(out=psum_pick[:, :, :, :].rearrange("p a v k -> p (a v k)"),
                                 in_=picked.rearrange("p a v k e -> p (a v k) e"), axis=AX_X, op=ALU.add))
            link(v.tensor_copy(sloti[:, 0], psum_pick[:, :, 0, :]))
            v.tensor_scalar(sloti[:, 1], sloti[:, 0], 7, None, ALU.arith_shift_right)
            link(v.tensor_scalar(sloti[:, 2], sloti[:, 0], P - 1, None, ALU.bitwise_and))
            v.tensor_copy(slotf[:, 0], sloti[:, 1])
            link(v.tensor_copy(slotf[:, 1], sloti[:, 2]))
            link(v.tensor_tensor(out=slotf[:, 2], in0=cc("token").unsqueeze(1).broadcast_to([P, 2, NBLK]),
                                 in1=slotf[:, 1], op=ALU.subtract))
            dve.wait_ge(t_out, 16 * B)
            for a in range(TOP_K):
                v.tensor_tensor(out=hot[:, a], in0=cc("iota").unsqueeze(1).broadcast_to([P, NBLK, P]),
                                in1=slotf[:, 1, a, :].unsqueeze(2).broadcast_to([P, NBLK, P]), op=ALU.is_equal)
                link(v.tensor_tensor(out=pay[:, a, :, 0, :], in0=cc("tiles").unsqueeze(1).broadcast_to([P, NBLK, TCOL]),
                                     in1=slotf[:, 0, a, :].unsqueeze(2).broadcast_to([P, NBLK, TCOL]), op=ALU.is_equal))
                link(v.tensor_tensor(out=pay[:, a, :, 1, :], in0=pay[:, a, :, 0, :],
                                     in1=psum_pick[:, a, 1, :].unsqueeze(2).broadcast_to([P, NBLK, TCOL]), op=ALU.mult))
                v.tensor_tensor(out=pay[:, a, :, 0, :], in0=pay[:, a, :, 0, :],
                                in1=slotf[:, 2, a, :].unsqueeze(2).broadcast_to([P, NBLK, TCOL]), op=ALU.mult)\
                    .then_inc(hot_done, 1)
            link(v.tensor_tensor(out=texpf[:, :, :], in0=cc("tiles").unsqueeze(2).broadcast_to([P, TCOL, E]),
                                 in1=tcnt[:, 2, :].unsqueeze(1).broadcast_to([P, TCOL, E]), op=ALU.is_ge))
            link(v.tensor_reduce(out=texpc[:, :], in_=texpf[:, :, :], axis=AX_X, op=ALU.add))
            v.tensor_scalar(texp[:, :], texpc[:, :], float(E - 1), None, ALU.min)
            for _ in range(2 * (E - EARLY)):
                split_lo()
            dve.wait_ge(table_mm, 1)
            v.tensor_scalar(idx[:, :], ps[:, 7, 0:TCOL], cc("spare"), None, ALU.add)
            v.tensor_scalar(gates[:, :], ps[:, 7, TCOL:2 * TCOL], 1.0 / (WS * HS), None, ALU.mult).then_inc(table_done, 1)

            def rows_T(j, n):
                i, s = UNROLL * j + n, n % 2
                dve.wait_ge(xT_mm, i + 1)
                if n >= 2:
                    dve.wait_ge(l1_mm, i - 1)
                v.tensor_copy(xT[:, s, :], xT_ps).then_inc(xT_done, 1)

            def halves(j, n):
                i, s = UNROLL * j + n, n % 2
                dve.wait_ge(gelu_done, i + 1)
                if n >= 2:
                    dve.wait_ge(l2_mm, i - 1)
                v.tensor_scalar(hhi[:, s, :], hid[:, s, :], HS, None, ALU.mult).then_inc(hhi_done, 1)
                dve.wait_ge(hhi_done, i + 1)
                v.scalar_tensor_tensor(out=hlo[:, s, :], in0=hid[:, s, :], scalar=HS, in1=hhi[:, s, :],
                                       op0=ALU.mult, op1=ALU.subtract).then_inc(h_done, 1)

            def scaled(j, n):
                i, s = UNROLL * j + n, n % 2
                gate = gates[:, bass.ds(i, 1)]
                dve.wait_ge(l2_mm, i + 1)
                if n >= 2:
                    dve.wait_ge(add_out, 16 * i - 16)
                v.tensor_scalar(yb[:, s, :], y_ps(s)[:, C:2 * C], gate, None, ALU.mult).then_inc(ylo_done, 1)
                dve.wait_ge(ylo_done, i + 1)
                v.scalar_tensor_tensor(out=yb[:, s, :], in0=y_ps(s)[:, 0:C], scalar=gate, in1=yb[:, s, :],
                                       op0=ALU.mult, op1=ALU.add).then_inc(y_done, 1)

            def step(j, n):
                if not isinstance(j, int) or n + 1 < TILES:
                    rows_T(j, n + 1)
                if n >= 1:
                    halves(j, n - 1)
                if n >= 2:
                    scaled(j, n - 2)

            rows_T(0, 0)
            moe(dve, step)
            for n in range(TILES, TILES + 2):
                if n == TILES:
                    halves(0, n - 1)
                scaled(0, n - 2)


def _constants():
    p = np.arange(P)
    c = np.zeros((P, NCONST), np.float32)
    c[:, CONST["ident"]] = np.eye(P)
    c[:, CONST["blocks"]] = p[:, None] // CG == p[None, :] // CG
    pos = np.clip((np.arange(H) + 0.5) * (CG / H) - 0.5, 0, CG - 1)
    lo = np.floor(pos).astype(int)
    resize = np.zeros((CG, H))
    np.add.at(resize, (lo, np.arange(H)), 1 - (pos - lo))
    np.add.at(resize, (np.minimum(lo + 1, CG - 1), np.arange(H)), pos - lo)
    c[:, CONST["resize"]] = resize[p % CG] / KW
    c[:, CONST["own"]] = p[:, None] % CG == np.arange(CG)
    c[:, CONST["iota"]] = p[None, :]
    c[:, CONST["tiles"]] = np.arange(TCOL)
    c[:, CONST["before"]] = (np.arange(E)[None, :] < np.arange(E)[:, None]).ravel()
    c[:, CONST["steps"]] = P * np.arange(NBLK)
    c[:, CONST["token"]] = P * np.arange(NBLK)[None, :] + p[:, None] - NTOK
    c[:, CONST["spare"]] = NTOK + p[:, None]
    px = np.arange(PX)
    n = np.arange(NF)
    turns = (np.outer(px // W, n // KW) % H) / H + (np.outer(px % W, n % KW) % W) / W
    quarter = np.round(turns * 4 * 4).astype(int) % 16
    cos = np.cos(2 * np.pi * np.arange(16) / 16)
    cos[[4, 12]] = 0
    dft = np.concatenate([cos[quarter], cos[(quarter - 4) % 16]], 1) / np.sqrt(PX)
    c[:, CONST["dft"]] = dft.reshape(DC, P, 2 * NF).transpose(1, 0, 2).reshape(P, -1)
    h = np.zeros((P, NC16), np.float16)
    h[:, C16["ident"]] = np.eye(P)
    h[:, C16["earlier"]] = p[:, None] < p[None, :]
    h[:, C16["ones"]] = 1
    h[:, C16["bias"]] = HS
    return c, h


def kernel(**inputs):
    import concourse.bacc as bacc
    from concourse.bass_utils import run_bass_kernel_spmd

    a = {k: np.asarray(v) for k, v in inputs.items()}
    g = {k[len("L0_conv_"):]: v for k, v in a.items() if k.startswith("L0_conv_")}
    f = {k[len("L0_ffn_"):]: v for k, v in a.items() if k.startswith("L0_ffn_")}
    n = P // CG
    par = np.zeros((P, NPAR), np.float32)
    par[:, PAR["w1"]] = np.tile(g["w1"].T, (n, 1))
    par[:, PAR["wpw"]] = np.tile(g["w_pw"].T, (n, 1))
    par[:, PAR["wdw"]] = np.tile(g["w_dw"].reshape(CG, 9), (n, 1))
    for name, key in (("b1", "b1"), ("gamma", "gn_gamma"), ("beta", "gn_beta"), ("bdw", "b_dw"), ("bpw", "b_pw"), ("bfp", "b_fp")):
        par[:, PAR[name]] = np.tile(g[key][:, None], (n, 1))
    par[:, PAR["betarow"]] = g["gn_beta"][None, :]
    par[:, PAR["wfp"]] = g["w_fp"].reshape(1, -1)
    par[:, PAR["bpwrow"]] = np.tile(g["b_pw"], n)[None, :]
    par[:, PAR["wg"]] = f["Wg"].reshape(HALVES, P, E).transpose(1, 0, 2).reshape(P, -1)
    par[:, PAR["b1e"]] = f["b1"].reshape(E, FC, P).transpose(2, 0, 1).reshape(P, -1)
    const, const16 = _constants()
    x = a["x"]
    arrays = {
        "x_tok": np.ascontiguousarray(x.reshape(B, C, PX).transpose(0, 2, 1).reshape(NTOK, C)),
        "x_chan": np.ascontiguousarray(x.reshape(B, C, PX)),
        "const": const, "const16": const16, "params": par,
        "w1": np.ascontiguousarray(f["W1"]), "w2": np.ascontiguousarray(f["W2"]),
        "b2": np.ascontiguousarray(np.tile(f["b2"].reshape(1, -1), (2, 1))),
    }
    nc = bacc.Bacc("TRN2", target_bir_lowering=False, num_devices=1)
    aps = [nc.dram_tensor(k, v.shape, mybir.dt.from_np(v.dtype), kind="ExternalInput").ap() for k, v in arrays.items()]
    out = nc.dram_tensor("out", (TROWS, C), F32, kind="ExternalOutput").ap()
    build(nc, *aps, out)
    r = run_bass_kernel_spmd(nc, [arrays], core_ids=[0])
    got = np.asarray(r.results[0]["out"])[:NTOK]
    return np.ascontiguousarray(got.reshape(B, PX, C).transpose(0, 2, 1)).reshape(B, C, H, W)
```

```python
from contextlib import ExitStack

import numpy as np

import concourse.bass as bass
from concourse import mybir

ALU = mybir.AluOpType
ACT = mybir.ActivationFunctionType
AX_X = mybir.AxisListType.X
F32 = mybir.dt.float32
F16 = mybir.dt.float16
I32 = mybir.dt.int32
U32 = mybir.dt.uint32

P = 128
B, C, H, W = 8, 256, 16, 16
PX = H * W
NTOK = B * PX
NBLK = NTOK // P
CG = 8
HALVES = C // P
NT = B * HALVES
PAD = H + 2
KW = W // 2 + 1
NF = H * KW
NMIX = 2 * NF + H + W
TAPS = 3
E, F, TOP_K = 8, 1024, 2
DC, FC = C // P, F // P
SLOTS_MOST = NTOK * TOP_K
TILES = SLOTS_MOST // P + E - 1
TCOL = TILES + 1
TROWS = NTOK + P
EPS_C, EPS_G = 1e-6, 1e-5
XS, WS, HS, GS = 64.0, 256.0, 16.0, 16384.0
LOW = -3e38
PIECE = DC * F
EXPERT = 4 * PIECE
EARLY = 4
NSTG = 2
ORDER = (1, 0, 3, 5, 2, 7, 4, 6, 8, 9, 15, 10, 11, 12, 13, 14)
POOL_SPLITS = (0, 2, 4, 8, 10, 12, 14)
DVE_SPLITS = tuple(n for n in ORDER if n not in POOL_SPLITS)
UNROLL = 4
LEAD = 3
PEELED = 4
assert PEELED <= (TOP_K - 1) * NBLK
ROUNDS = (TILES - PEELED - 1) // UNROLL
DVE_GATES = 12
POOL_PADS = 6
TINY = 1e-30

def _columns(widths):
    at, out = 0, {}
    for name, n in widths:
        out[name] = slice(at, at + n)
        at += n
    return out, at

CONST, NCONST = _columns([("ident", P), ("blocks", P), ("resize", H), ("own", CG),
                          ("tiles", TCOL), ("before", E * E), ("steps", NBLK), ("token", NBLK), ("rev", E),
                          ("spare", 1), ("minusrow", 1), ("spread", P), ("dft", DC * NMIX)])
C16, NC16 = _columns([("ident", P), ("earlier", P), ("ones", P), ("bias", P), ("iota", P), ("tiles", TCOL)])
PAR, NPAR = _columns([("w1", CG), ("wpw", CG), ("wdw", 9), ("b1", 1), ("gamma", 1), ("beta", 1),
                      ("bdw", 1), ("bpw", 1), ("bfp", 1), ("betarow", CG), ("wfp", CG * CG),
                      ("bpwrow", P), ("wg", HALVES * E), ("b1e", E * FC)])


def build(nc, x_tok, const, const16, params, w1, w2, b2, out):
    with ExitStack() as ctx:
        def sb(name, shape, dt=F32):
            return ctx.enter_context(nc.sbuf_tensor(name, shape, dt))

        def sem(name):
            return ctx.enter_context(nc.semaphore(name))

        xn_rows = nc.dram_tensor("xn_rows", [TROWS, 2 * C], F16, kind="Internal").ap()

        wt = sb("wt", [P, E * EXPERT + NSTG * 2 * PIECE], F16)
        late = wt[:, EARLY * EXPERT:].bitcast(F32)
        stg = late[:, 2 * (E - EARLY) * PIECE:].rearrange("p (s n) -> p s n", n=PIECE)
        xln_tok = late[:, 0:NBLK * C].rearrange("p (k c) -> p k c", c=C)
        o = NBLK * C
        xln_pad = late[:, o:o + NT * PAD * PAD].rearrange("p (t h w) -> p t h w", h=PAD, w=PAD)
        o += NT * PAD * PAD
        gated = late[:, o:o + NT * PX].rearrange("p (t n) -> p t n", n=PX)
        z = gated
        b2f = late[0:33, o:o + E * C]
        o += NT * PX
        mag = late[:, o:o + NT * NF].rearrange("p (t n) -> p t n", n=NF)

        zrow = late[:, o:o + C].bitcast(F16)
        o += NT * NF
        sg = late[:, o:o + NT * (H + W)].rearrange("p (t n) -> p t n", n=H + W)
        o += NT * (H + W)

        xt = sb("xt", [P, NBLK, C])
        fb = sb("fb", [P, 6144])
        cst = sb("cst", [P, NCONST])
        c16 = sb("c16", [P, NC16], F16)
        par = sb("par", [P, NPAR])
        b2c = sb("b2c", [33, E * C], F16)

        def view(at, n, dt=F32):
            v = fb[:, at:at + n]
            return v if dt is F32 else v.bitcast(dt)

        tapw = view(1024, TAPS * 96).rearrange("p (k m) -> p k m", m=96)
        coefw = view(1312, 4 * P).rearrange("p (t m) -> p t m", m=P)
        shifted = [view(at, 512) for at in (1824, 2336, 0, 512)]
        rf = view(2848, 2 * 512).rearrange("p (s n) -> p s n", s=2)
        xc = rf
        sq = view(3872, 2 * 2 * NF).rearrange("p (s n) -> p s n", s=2)
        sig = view(4448, 2 * PX).rearrange("p (s n) -> p s n", s=2)
        xn = view(4960, 4 * C).rearrange("p (s n) -> p s n", s=4)
        xrow = view(0, 1024, F16).rearrange("p (b k n) -> p b k n", b=2, k=2)
        eq = view(1152, NBLK * E).rearrange("p (k e) -> p k e", e=E)
        rest = view(1280, NBLK * E).rearrange("p (k e) -> p k e", e=E)
        pay = view(2400, 2 * NBLK * 4 * TCOL // 2, F16).rearrange("p (k v i) -> p k v i", v=4, i=TCOL)
        hot = xt[:, :, :].rearrange("p k c -> p (k c)")[:, 0:NTOK].bitcast(F16).rearrange("p (k r) -> p k r", r=P)
        xg = view(0, UNROLL * C, F16).rearrange("p (s n) -> p s n", s=UNROLL)
        xT = view(1024, 512, F16).rearrange("p (s n) -> p s n", s=2)
        hid = view(1536, 2 * F).rearrange("p (s n) -> p s n", s=2)
        hhi = view(3584, F, F16).rearrange("p (s n) -> p s n", s=2)
        hlo = view(4608, F, F16).rearrange("p (s n) -> p s n", s=2)
        yb = view(5632, 2 * C).rearrange("p (s n) -> p s n", s=2)

        bn6 = sb("bn6", [P, NBLK, 6])
        mv = sb("mv", [P, NBLK, 2])
        dev = sb("dev", [P, NBLK])
        rstd = sb("rstd", [P, NBLK])
        xlg = sb("xlg", [P, NBLK, E])
        eps = sb("eps", [P, 2])
        scrap = sb("scrap", [P, 1])
        eps_c, eps_g = eps[:, 0:1], eps[:, 1:2]
        ones_row = sb("ones_row", [1, NT])
        w1d = view(5472, P)
        wpwd = sb("wpwd", [P, P])
        wfpd = view(5600, P)
        prow = sb("prow", [P, 16 * CG])
        pcol = sb("pcol", [P, 32])
        wgc = sb("wgc", [P, HALVES, E])
        rc = sb("rc", [P, NT, H + W])
        gbn6 = sb("gbn6", [P, NT, 6])
        gmv = sb("gmv", [P, NT, 2])
        grs = sb("grs", [P, NT])
        tot = sb("tot", [P, NT])
        r3 = view(5728, NT * 3).rearrange("p (t a) -> p t a", a=3)
        q3 = view(5776, NT * 6).rearrange("p (t a b) -> p t a b", a=3, b=2)
        s9 = late[:, o:o + NT * 9].rearrange("p (t a b) -> p t a b", a=3, b=3)
        dwm = sb("dwm", [P, NT])
        s2r = sb("s2r", [NT, 4, P])
        s2s = sb("s2s", [NT, 2, 16])
        s2c = sb("s2c", [P, NT])
        coef = sb("coef", [P, NT])
        bterm = sb("bterm", [P, NT])
        bias = sb("bias", [P, NT])
        fm = sb("fm", [P, NT, H])
        tmv = sb("tmv", [P, NBLK, 2])
        trs = sb("trs", [P, NBLK])
        trs64 = sb("trs64", [P, NBLK])
        lg = sb("lg", [P, NBLK, E])
        best = sb("best", [P, 2, NBLK])
        sgl = sb("sgl", [P, NBLK, E])
        sel16 = sb("sel16", [P, NBLK, E], F16)
        cnt = sb("cnt", [P, E])
        tcnt = sb("tcnt", [P, 3, E])
        slot = sb("slot", [P, NBLK, E])
        pick = view(1664, 2 * NBLK * E).rearrange("p (a k e) -> p a k e", a=2, k=NBLK)
        psum_pick = sb("picked", [P, 2, 2, NBLK])
        sloti = sb("sloti", [P, 3, 2, NBLK], I32)
        place16 = sb("place16", [P, 4, 2, NBLK], F16)
        tok16 = sb("tok16", [P, NBLK], F16)
        texpf = view(1920, TCOL * E).rearrange("p (i e) -> p i e", e=E)
        texpc = sb("texpc", [P, TCOL])
        texp = sb("texp", [P, TCOL], I32)
        idx = sb("idx", [P, TCOL], I32)
        idxc = sb("idxc", [P, UNROLL + 2], I32)
        gates = sb("gates", [P, TCOL])
        found = sb("found", [P, TCOL])

        ps = ctx.enter_context(nc.psum_tensor("ps", [P, 8, 512], F32))
        QB, WB = [6, 7], [0, 1]
        xT_ps = ps[:, 0, 0:256].bitcast(F16)

        def h_ps(s):
            return ps[:, 1 + 2 * s:3 + 2 * s, :].rearrange("p b n -> p (b n)")

        def y_ps(s):
            return ps[:, 5 + s, :]

        const_in = sem("const_in")
        x_in = [sem(f"x_in{i}") for i in range(4)]
        stg_in = [sem(f"stg_in{i}") for i in range(NSTG)]
        b2_in = sem("b2_in")
        spare_set = sem("spare_set")
        t_out = sem("t_out")
        xn_out = [sem(f"xn_out{i}") for i in range(2)]
        hi_done = sem("hi_done")
        scaled_done = sem("scaled_done")
        x_logit_mm = sem("x_logit_mm")
        pool_lo = sem("pool_lo")
        dve_lo = sem("dve_lo")
        dve_step = sem("dve_step")
        pad_zero = sem("pad_zero")
        ln_done = sem("ln_done")
        eps_set = sem("eps_set")
        var_c = sem("var_c")
        dev_c = sem("dev_c")
        var_g = sem("var_g")
        dev_g = sem("dev_g")
        var_t = sem("var_t")
        dev_t = sem("dev_t")
        tr_done = sem("tr_done")
        tr_copied = sem("tr_copied")
        padded = sem("padded")
        dft_done = sem("dft_done")
        sq_done = sem("sq_done")
        mag_done = sem("mag_done")
        root_done = sem("root_done")
        fm_done = sem("fm_done")
        rf_done = sem("rf_done")
        gate_mm = sem("gate_mm")
        gate_sig = sem("gate_sig")
        gate_row = sem("gate_row")
        gated_done = sem("gated_done")
        gate_col = sem("gate_col")
        small_ready = sem("small_ready")
        small_mm = sem("small_mm")
        exp_in = sem("exp_in")
        exp_done = sem("exp_done")
        tapw_done = sem("tapw_done")
        coef_done = sem("coef_done")
        taps_mm = sem("taps_mm")
        shift_done = sem("shift_done")
        map_done = sem("map_done")
        sig_done = sem("sig_done")
        z_done = sem("z_done")
        zt_done = sem("zt_done")
        t_done = sem("t_done")
        xn_done = sem("xn_done")
        xhi_done = sem("xhi_done")
        xlo_done = sem("xlo_done")
        logit_mm = sem("logit_mm")
        logit_done = sem("logit_done")
        sigl_done = sem("sigl_done")
        sel_done = sem("sel_done")
        prefix_mm = sem("prefix_mm")
        pay_done = sem("pay_done")
        hot_done = sem("hot_done")
        table_mm = sem("table_mm")
        table_done = sem("table_done")
        b2_done = sem("b2_done")
        spare_zero = sem("spare_zero")
        first_index = sem("first_index")
        gather_index = sem("gather_index")
        sum_index = sem("sum_index")
        g_in = [sem(f"g_in{i}") for i in range(UNROLL)]
        add_out = sem("add_out")
        xT_mm = sem("xT_mm")
        xT_done = sem("xT_done")
        l1_mm = sem("l1_mm")
        gelu_done = sem("gelu_done")
        hhi_done = sem("hhi_done")
        h_done = sem("h_done")
        ylo_done = sem("ylo_done")
        l2_mm = sem("l2_mm")
        y_done = sem("y_done")

        def wpiece(n, part):
            at = (n // 2) * EXPERT
            if n % 2 == 0:
                return wt[:, at + part * PIECE:at + (part + 1) * PIECE]
            return wt[:, at + 2 * PIECE:at + EXPERT].rearrange("p (f v d) -> p f v d", f=FC, v=2)[:, :, part, :]

        def splits(n):
            return (POOL_SPLITS, 0) if n in POOL_SPLITS else (DVE_SPLITS, 1)

        def wait_hi(engine, n):
            engine.wait_ge(hi_done, ORDER.index(n) + 1)

        def wait_lo(engine, n):
            engine.wait_ge(pool_lo if n in POOL_SPLITS else dve_lo, splits(n)[0].index(n) + 1)

        def slot_of(u):
            return u if u < 4 else u % 2

        def staged(n):
            piece = stg[:, splits(n)[1], :]
            return piece if n % 2 == 0 else piece.rearrange("p (f d) -> p f d", f=FC)

        w1_dram = w1.rearrange("e (c p) f -> e p c f", p=P)
        w2_dram = w2.rearrange("e (c p) d -> e p c d", p=P)
        out_rows = out[0:NTOK, :].rearrange("(k p) c -> p k c", p=P)
        xn_dram = xn_rows[0:NTOK, :].rearrange("(k p) c -> p k c", p=P)
        x_dram = x_tok.rearrange("(k p) c -> p k c", p=P)
        col = lambda name, k=0: par[:, PAR[name].start + k:PAR[name].start + k + 1]
        cc = lambda name: cst[:, CONST[name]]
        inner = lambda t0, n: xln_pad[:, t0:t0 + n, 1:1 + H, 1:1 + W]

        def moe(engine, step, before_loop=None):
            for n in range(PEELED):
                step(0, n)
            if before_loop:
                before_loop()
            with engine.Fori(0, ROUNDS) as j:
                for n in range(PEELED, PEELED + UNROLL):
                    step(j, n)
            for n in range(PEELED + UNROLL * ROUNDS, TILES):
                step(0, n)

        block = ctx.enter_context(nc.Block())

        @block.sync
        def _(sp):
            sp.dma_start(x_t := xt[:, 0:4, :], x_dram[:, 0:4, :]).then_inc(x_in[0], 16)
            sp.dma_start(par[:, :], params).then_inc(const_in, 16)
            sp.dma_start(cst[:, :], const).then_inc(const_in, 16)
            sp.dma_start(c16[:, :], const16).then_inc(const_in, 16)
            for q in range(1, 4):
                sp.dma_start(xt[:, 4 * q:4 * q + 4, :], x_dram[:, 4 * q:4 * q + 4, :]).then_inc(x_in[q], 16)

            sp.dma_start(b2f, b2.broadcast_to([33, E * C])).then_inc(b2_in, 16)

            sp.wait_ge(spare_zero, 1)
            sp.dma_start(xn_rows[NTOK:TROWS, :], zrow).then_inc(spare_set, 16)
            sp.dma_start(out[NTOK:TROWS, :], zrow.bitcast(F32)).then_inc(spare_set, 16)

            def load(n):
                shared, slot = splits(n)
                if n != shared[0]:
                    wait_lo(sp, shared[shared.index(n) - 1])
                src = (w1_dram if n % 2 == 0 else w2_dram)[n // 2]
                dst = stg[:, slot, :].rearrange("p (c f) -> p c f", c=DC if n % 2 == 0 else FC)
                sp.dma_start(dst, src).then_inc(stg_in[slot], 16)

            for n in ORDER[0:6]:
                load(n)
            for n in ORDER[6:10]:
                load(n)

            def rows_out(b):
                sp.wait_ge(xhi_done, 2 * b + 2)
                sp.wait_ge(xlo_done, 2 * b + 2)
                sp.dma_start(xn_dram[:, 2 * b:2 * b + 2, :], xrow[:, b % 2]).then_inc(xn_out[b % 2], 16)

            for b in range(B):
                sp.wait_ge(t_done, b + 1)
                sp.dma_start(out_rows[:, 2 * b:2 * b + 2, :], xt[:, 2 * b:2 * b + 2, :]).then_inc(t_out, 16)
                if b in (0, 1, 3, 4):
                    load({0: 15, 1: 10, 3: 11, 4: 12}[b])
            for b in range(B):
                rows_out(b)
                if b in (2, 5):
                    load({2: 14, 5: 13}[b])

        @block.gpsimd
        def _(pool):
            nc.gpsimd.memset(late[:, NBLK * C:NBLK * C + NT * PAD * PAD], 0.0).then_inc(pad_zero, 1)
            nc.gpsimd.memset(zrow, 0.0).then_inc(spare_zero, 1)
            nc.gpsimd.memset(fb[:, 1824:2848], 0.0)
            nc.gpsimd.memset(fb[:, 0:1024], 0.0).then_inc(pad_zero, 1)
            g = nc.gpsimd
            pool.wait_ge(pad_zero, 2)
            def split_lo(n):
                pool.wait_ge(scaled_done, POOL_SPLITS.index(n) + 1)
                g.tensor_tensor(out=wpiece(n, 1), in0=staged(n), in1=wpiece(n, 0), op=ALU.subtract)\
                    .then_inc(pool_lo, 1)

            def rows_lo(b):
                for k in (2 * b, 2 * b + 1):
                    pool.wait_ge(xhi_done, k + 1)
                    g.tensor_tensor(out=xrow[:, b % 2, k % 2, C:2 * C], in0=xn[:, k % 4, :],
                                    in1=xrow[:, b % 2, k % 2, 0:C], op=ALU.subtract).then_inc(xlo_done, 1)

            for b in range(POOL_PADS):
                pool.wait_ge(tr_copied, b + 1)
                g.tensor_copy(inner(2 * b, 2), xc[:, b % 2, :].rearrange("p (t h w) -> p t h w", t=2, w=W))\
                    .then_inc(padded, 1)
                if b == 4:
                    split_lo(0)
            for t in range(NT):
                pool.wait_ge(gate_sig, t // CG + 1)
                if t == 0:
                    pool.wait_ge(padded, POOL_PADS)
                    pool.wait_ge(tr_copied, B)
                g.tensor_tensor(
                    out=gated[:, t].rearrange("p (h w) -> p h w", w=W), in0=xln_pad[:, t, 1:1 + H, 1:1 + W],
                    in1=sg[:, t, 0:H].unsqueeze(2).broadcast_to([P, H, W]), op=ALU.mult).then_inc(gate_row, 1)
            for t in range(DVE_GATES, NT):
                pool.wait_ge(gate_row, t + 1)
                gv = gated[:, t].rearrange("p (h w) -> p h w", w=W)
                g.tensor_tensor(out=gv, in0=gv, in1=sg[:, t, H:H + W].unsqueeze(1).broadcast_to([P, H, W]),
                                op=ALU.mult).then_inc(gate_col, 1)
            split_lo(2)
            for u in range(NT // 2):
                if u == 0:
                    pool.wait_ge(fm_done, 1)
                if u >= 2:
                    pool.wait_ge(map_done, u - 1)
                for s in range(2):
                    t = 2 * u + s
                    g.tensor_tensor(
                        out=rf[:, u % 2, s * PX:(s + 1) * PX].rearrange("p (i j) -> p i j", j=W),
                        in0=cc("resize").unsqueeze(2).broadcast_to([P, H, W]),
                        in1=fm[:, t, :].unsqueeze(1).broadcast_to([P, H, W]), op=ALU.mult).then_inc(rf_done, 1)
                if u in (1, 3, 7):
                    split_lo({1: 4, 3: 8, 7: 10}[u])
            for b in range(B):
                rows_lo(b)
                if b == 1:
                    split_lo(12)

            pool.wait_ge(table_done, 1)
            pool.wait_ge(spare_set, 32)
            pool.wait_ge(t_out, 16 * B)
            for s in range(2):
                pool.wait_ge(xn_out[s], 16 * (B // 2))

            def gather(j, n):
                i, g = UNROLL * j + n, n % UNROLL
                if n >= UNROLL:
                    pool.wait_ge(xT_mm, i - (UNROLL - 1))
                copied, count = (gather_index, i - (UNROLL - 1)) if n >= UNROLL else (first_index, n + 1)
                nc.gpsimd.tensor_copy(idxc[:, g:g + 1], idx[:, bass.ds(i, 1)]).then_inc(copied, 1)
                pool.wait_ge(table_done, 1)
                pool.wait_ge(copied, count)
                nc.gpsimd.indirect_dma_start(
                    out=xg[:, g, :], out_offset=None, in_=xn_rows,
                    in_offset=bass.IndirectOffsetOnAxis(ap=idxc[:, g:g + 1].bitcast(U32), axis=0),
                ).then_inc(g_in[g], 16)

            def add(j, n):
                i, s = UNROLL * j + n, n % 2
                if n > 0:
                    pool.wait_ge(add_out, 16 * i)
                pool.wait_ge(y_done, i + 1)
                nc.gpsimd.tensor_copy(idxc[:, UNROLL + s:UNROLL + s + 1], idx[:, bass.ds(i, 1)])\
                    .then_inc(sum_index, 1)
                pool.wait_ge(table_done, 1)
                pool.wait_ge(sum_index, i + 1)
                nc.gpsimd.indirect_dma_start(
                    out=out, out_offset=bass.IndirectOffsetOnAxis(
                        ap=idxc[:, UNROLL + s:UNROLL + s + 1].bitcast(U32), axis=0),
                    in_=yb[:, s, :], in_offset=None, compute_op=ALU.add).then_inc(add_out, 16)

            def step(j, n):
                if n >= LEAD:
                    add(j, n - LEAD)
                if not isinstance(j, int) or n + LEAD < TILES:
                    gather(j, n + LEAD)

            for n in range(LEAD):
                gather(0, n)
            split_lo(14)
            moe(pool, step)
            for n in range(TILES - LEAD, TILES):
                add(0, n)
            pool.wait_ge(add_out, 16 * TILES)

        @block.scalar
        def _(act):
            pieces = [0]

            def scale(n):
                wait_hi(act, n)
                nc.scalar.activation(staged(n), staged(n), ACT.Copy, scale=WS).then_inc(scaled_done, 1)

            def split_hi():
                n = ORDER[pieces[0]]
                pieces[0] += 1
                shared, slot = splits(n)
                act.wait_ge(stg_in[slot], 16 * (shared.index(n) + 1))
                if n in (8, 9):
                    act.wait_ge(x_logit_mm, 1)
                elif n == 15:
                    act.wait_ge(fm_done, 1)
                elif n in (10, 11, 12):
                    act.wait_ge(z_done, {10: 7, 11: 13, 12: 16}[n])
                elif n in (13, 14):
                    act.wait_ge(logit_mm, 1)
                nc.scalar.activation(wpiece(n, 0), staged(n), ACT.Copy, scale=WS).then_inc(hi_done, 1)
                if n in POOL_SPLITS[2:]:
                    scale(n)

            def deviation(dst, var, eps, done):
                nc.scalar.activation(dst, var, ACT.Sqrt, bias=eps[:, 0:1]).then_inc(done, 1)

            act.wait_ge(eps_set, 1)
            for b in range(2):
                act.wait_ge(var_c, b + 1)
                deviation(dev[:, 2 * b:2 * b + 2], mv[:, 2 * b:2 * b + 2, 1], eps_c, dev_c)
            act.wait_ge(exp_in, 1)
            nc.scalar.activation(prow[:, 2 * CG:3 * CG], prow[:, CG:2 * CG], ACT.Exp).then_inc(exp_done, 1)
            for b in range(B):
                if b + 2 < B:
                    act.wait_ge(var_c, b + 3)
                    deviation(dev[:, 2 * b + 4:2 * b + 6], mv[:, 2 * b + 4:2 * b + 6, 1], eps_c, dev_c)
                act.wait_ge(tr_done, b + 1)
                if b >= 2:
                    act.wait_ge(padded, b - 1)
                if b >= POOL_PADS:
                    nc.scalar.activation(inner(2 * b, 2), ps[:, b % 2, :].rearrange("p (t h w) -> p t h w", t=2, w=W),
                                         ACT.Copy)
                nc.scalar.activation(xc[:, b % 2, :], ps[:, b % 2, :], ACT.Copy).then_inc(tr_copied, 1)
                for t in (2 * b, 2 * b + 1):
                    act.wait_ge(dft_done, t + 1)
                    if t >= 2:
                        act.wait_ge(mag_done, t - 1)
                    nc.scalar.activation(rc[:, t, :], ps[:, 2 + t % 2, 2 * NF:NMIX], ACT.Copy)
                    nc.scalar.activation(sq[:, t % 2, :], ps[:, 2 + t % 2, 0:2 * NF], ACT.Square).then_inc(sq_done, 1)
                if b in (1, 2, 3, 6, 7):
                    split_hi()
                if b == 4:
                    scale(0)
            def shift(u):
                act.wait_ge(taps_mm, u + 1)
                if u >= 4:
                    act.wait_ge(map_done, u - 3 if u < 6 else u - 1)
                for r in range(TAPS):
                    q = slice(32 * r, 32 * r + 32)
                    src, dst, n = max(r - 1, 0), max(1 - r, 0), H - abs(r - 1)
                    a = nc.scalar.activation(
                        shifted[slot_of(u)][q, :].rearrange("p (t h w) -> p t h w", t=2, w=W)[:, :, dst:dst + n, :],
                        ps[q, QB[u % 2], :].rearrange("p (t h w) -> p t h w", t=2, w=W)[:, :, src:src + n, :],
                        ACT.Copy)
                a.then_inc(shift_done, 1)

            act.wait_ge(gate_mm, 1)
            for g in range(2):
                n = NT // 2
                nc.scalar.activation(sg[:, g * n:(g + 1) * n, :],
                                     ps[:, 4, g * 256:(g + 1) * 256].rearrange("p (t n) -> p t n", t=n),
                                     ACT.Sigmoid, bias=col("b1"), scale=1.0 / H).then_inc(gate_sig, 1)
            shift(0)
            scale(2)
            act.wait_ge(exp_in, 2)
            nc.scalar.activation(s2r[:, 1, :], s2r[:, 0, :], ACT.Exp).then_inc(exp_done, 1)
            shift(1)
            shift(2)
            act.wait_ge(mag_done, NT)
            nc.scalar.activation(mag, mag, ACT.Sqrt).then_inc(root_done, 1)
            shift(3)
            act.wait_ge(var_g, 1)
            deviation(grs[:, :], gmv[:, :, 1], eps_g, dev_g)
            split_hi()
            split_hi()

            def sigmoids(u):
                act.wait_ge(map_done, u + 1)
                for t in (2 * u, 2 * u + 1):
                    if t == 0:
                        act.wait_ge(coef_done, 5)
                    if t >= 2:
                        act.wait_ge(z_done, t - 1)
                    nc.scalar.activation(sig[:, t % 2, :], ps[:, WB[u % 2], (t % 2) * PX:(t % 2 + 1) * PX],
                                         ACT.Sigmoid, bias=bias[:, t:t + 1]).then_inc(sig_done, 1)

            def rows_hi(b):
                for k in (2 * b, 2 * b + 1):
                    act.wait_ge(xn_done, k + 1)
                    if k % 2 == 0 and b >= 2:
                        act.wait_ge(xn_out[b % 2], 16 * (b // 2))
                    nc.scalar.activation(xrow[:, b % 2, k % 2, 0:C], xn[:, k % 4, :], ACT.Copy).then_inc(xhi_done, 1)

            def deviations(b):
                act.wait_ge(var_t, b + 4)
                deviation(trs[:, 2 * b:2 * b + 8], tmv[:, 2 * b:2 * b + 8, 1], eps_g, dev_t)

            for u in range(B):
                sigmoids(u)
                if u in (0, 1, 4, 5):
                    shift(u + 4 if u < 2 else u + 2)
                if u in (0, 1, 2, 4, 5):
                    split_hi()
            deviations(0)
            split_hi()
            rows_hi(0)
            deviations(4)
            rows_hi(1)
            split_hi()
            act.wait_ge(logit_done, 1)
            nc.scalar.activation(sgl[:, :, :], lg[:, :, :], ACT.Sigmoid).then_inc(sigl_done, 1)
            rows_hi(2)
            for b in range(3, B):
                rows_hi(b)
            split_hi()
            split_hi()

            nc.scalar.activation(scrap[:, :], eps_c, ACT.Gelu_apprx_tanh)
            act.wait_ge(table_done, 1)

            def step(j, n):
                i, s = UNROLL * j + n, n % 2
                e = act.value_load(texp[0:1, bass.ds(i, 1)], min_val=0, max_val=E - 1)
                act.wait_ge(l1_mm, i + 1)
                if n >= 2:
                    act.wait_ge(h_done, i - 1)
                for f in range(FC):
                    a = nc.scalar.activation(hid[:, s, f * P:(f + 1) * P], h_ps(s)[:, f * P:(f + 1) * P],
                                             ACT.Gelu_apprx_tanh,
                                             bias=par[:, bass.ds(e * FC + (PAR["b1e"].start + f), 1)],
                                             scale=1.0 / (XS * WS))
                a.then_inc(gelu_done, 1)

            moe(act, step)

        @block.tensor
        def _(pe):
            ident = cc("ident")
            dft = cc("dft").rearrange("p (c n) -> p c n", c=DC)
            pe.wait_ge(const_in, 48)
            pe.wait_ge(small_ready, 1)
            for a in range(HALVES):
                m = pe.matmul(ps[:, 5, 0:E], w1d[:, :], par[:, PAR["wg"].start + a * E:PAR["wg"].start + (a + 1) * E],
                              start=(a == 0), stop=(a == HALVES - 1))
            m.then_inc(small_mm, 1)
            def x_logits(b):
                if b == 0:
                    pe.wait_ge(small_ready, 2)
                pe.wait_ge(tr_copied, b + 1)
                for k in range(2):
                    o = (2 * b + k) * E
                    for a in range(HALVES):
                        m = pe.matmul(ps[:, 7, o:o + E], xc[:, b % 2, a * PX + k * P:a * PX + (k + 1) * P],
                                      wgc[:, a, :], start=(b == 0 and k == 0 and a == 0), stop=(a == HALVES - 1),
                                      skip_group_check=True)
                if b == B - 1:
                    m.then_inc(x_logit_mm, 1)

            for b in range(B):
                pe.wait_ge(ln_done, b + 1)
                if b >= 2:
                    pe.wait_ge(tr_copied, b - 1)
                for a in range(HALVES):
                    for k in range(2):
                        m = pe.transpose(ps[:, b % 2, (2 * a + k) * P:(2 * a + k + 1) * P],
                                         xln_tok[:, 2 * b + k, a * P:(a + 1) * P], ident)
                m.then_inc(tr_done, 1)
                for a in range(HALVES):
                    t = 2 * b + a
                    if t >= 2:
                        pe.wait_ge(sq_done, t - 1)
                    for k in range(2):
                        m = pe.matmul(ps[:, 2 + t % 2, 0:NMIX], xln_tok[:, 2 * b + k, a * P:(a + 1) * P],
                                      dft[:, k, :], start=(k == 0), stop=(k == 1))
                    m.then_inc(dft_done, 1)
                if b > 0:
                    x_logits(b - 1)
            x_logits(B - 1)
            pe.wait_ge(sq_done, NT)
            pe.matmul(ps[:, 4, :], w1d[:, :], rc[:, :, :].rearrange("p t n -> p (t n)"),
                      start=True, stop=True).then_inc(gate_mm, 1)
            pe.wait_ge(tapw_done, 1)
            pe.wait_ge(padded, POOL_PADS)
            pe.wait_ge(tr_copied, B)

            def taps(u):
                if u >= 2:
                    pe.wait_ge(shift_done, u - 1)
                for k in range(TAPS):
                    m = pe.matmul(ps[0:96, QB[u % 2], :], tapw[:, k, :],
                                  xln_pad[:, 2 * u:2 * u + 2, 1:1 + H, k:k + W],
                                  start=(k == 0), stop=(k == TAPS - 1))
                m.then_inc(taps_mm, 1)

            def rest(u):
                if u >= 2:
                    pe.wait_ge(sig_done, 2 * u - 2)
                pe.wait_ge(shift_done, u + 1)
                pe.matmul(ps[:, WB[u % 2], :], cst[0:96, CONST["spread"]], shifted[slot_of(u)][0:96, :],
                          start=True, stop=False)
                for t in (2 * u, 2 * u + 1):
                    pe.wait_ge(coef_done, t + 1 if t < 4 else t + 2)
                    pe.matmul(ps[:, WB[u % 2], (t % 2) * PX:(t % 2 + 1) * PX], coefw[:, t % 4, :], gated[:, t, :],
                              start=False, stop=False)
                pe.wait_ge(rf_done, 2 * u + 2)
                pe.matmul(ps[:, WB[u % 2], :], wfpd[:, :], rf[:, u % 2, :], start=False, stop=True)\
                    .then_inc(map_done, 1)

            taps(0)
            pe.wait_ge(small_ready, 3)
            pe.matmul(ps[0:NT, 5, 128:256], dwm[:, :], wpwd[:, :], start=True, stop=False)
            pe.matmul(ps[0:NT, 5, 128:256], ones_row[0:1, 0:NT],
                      par[0:1, PAR["bpwrow"]], start=False, stop=True).then_inc(small_mm, 1)
            for u in range(1, 4):
                taps(u)
            pe.wait_ge(small_ready, 4)
            pe.transpose(ps[:, 5, 256:256 + NT], s2r[:, 2, :], ident[0:NT, 0:NT]).then_inc(small_mm, 1)
            taps(4)
            pe.wait_ge(small_ready, 5)
            pe.matmul(ps[:, 5, 288:288 + NT], cc("blocks"), bterm[:, :], start=True, stop=True).then_inc(small_mm, 1)
            taps(5)

            def back(b):
                if b == 0:
                    pe.wait_ge(gate_sig, 2)
                if b >= 2:
                    pe.wait_ge(t_done, b - 1)
                pe.wait_ge(z_done, 2 * b + 2)
                for k in range(2):
                    for a in range(HALVES):
                        m = pe.transpose(ps[:, 2 + b % 2, (2 * k + a) * P:(2 * k + a + 1) * P],
                                         z[:, 2 * b + a, k * P:(k + 1) * P], ident)
                m.then_inc(zt_done, 1)
                for k in range(2):
                    o = (2 * b + k) * E
                    for a in range(HALVES):
                        m = pe.matmul(ps[:, 4, o:o + E], z[:, 2 * b + a, k * P:(k + 1) * P], wgc[:, a, :],
                                      start=(b == 0 and k == 0 and a == 0), stop=(a == HALVES - 1), skip_group_check=True)
                if b == B - 1:
                    m.then_inc(logit_mm, 1)

            for u in range(NT // 2):
                rest(u)
                if 1 <= u < 3:
                    taps(u + 5)
                if u >= 2:
                    back(u - 2)
            for b in range(B - 2, B):
                back(b)

            pe.wait_ge(sel_done, 1)
            ones16, before16 = c16[:, C16["ones"]], c16[:, C16["earlier"]]
            selv = sel16[:, :, :].rearrange("p k e -> p (k e)")
            pre = ps[:, 5, 0:(NBLK + 1) * E].rearrange("p (k e) -> p k e", e=E)
            pe.matmul(pre[:, 0:NBLK, :], before16, sel16[:, :, :], start=True, stop=False, skip_group_check=True)
            for k in range(NBLK):
                n = NBLK - k
                m = pe.matmul(pre[:, k + 1:NBLK + 1, :], ones16,
                              sel16[:, k:k + 1, :].broadcast_to([P, n, E]), start=False, stop=(k == NBLK - 1),
                              skip_group_check=True)
            m.then_inc(prefix_mm, 1)
            for v, bank in ((0, 7), (2, 6)):
                for k in range(2 * NBLK):
                    if k % NBLK == 0:
                        pe.wait_ge(hot_done, k // NBLK + 1 if v == 0 else 3)
                    m = pe.matmul(ps[:, bank, 0:2 * TCOL], hot[:, k, :],
                                  pay[:, k, v:v + 2, :].rearrange("p v i -> p (v i)"),
                                  start=(k == 0), stop=(k == 2 * NBLK - 1))
                m.then_inc(table_mm, 1)

            pe.wait_ge(table_done, 1)
            pe.wait_ge(b2_done, 1)
            wait_lo(pe, POOL_SPLITS[-2])
            wait_lo(pe, DVE_SPLITS[-1])
            ident16 = c16[:, C16["ident"]]

            def turn(j, n):
                g = n % UNROLL
                pe.wait_ge(g_in[g], 16 * (j + n // UNROLL) + 16)
                for c in range(4):
                    m = pe.transpose(xT_ps[:, c * P:(c + 1) * P], xg[:, g, c * P:(c + 1) * P], ident16)
                m.then_inc(xT_mm, 1)

            expert = [pe.alloc_register(f"expert{n}") for n in range(UNROLL)]

            def load_expert(j, n):
                pe.reg_load(expert[n % UNROLL], texp[0:1, bass.ds(UNROLL * j + n, 1)])

            def step(j, n):
                i, s = UNROLL * j + n, n % 2
                one, two = n < TILES, n >= 2
                if one:
                    e1 = pe.snap(expert[n % UNROLL], min_val=0, max_val=E - 1)
                if two:
                    e2 = pe.snap(expert[(n - 2) % UNROLL], min_val=0, max_val=E - 1)
                if n < 2:
                    pe.wait_ge(xT_done, i + 1)
                else:
                    pe.wait_ge(h_done, i - 1)
                for f in range(FC):
                    for c in range(DC if one else 0):
                        dst = h_ps(s)[:, f * P:(f + 1) * P]
                        hi = wt[:, bass.ds(e1 * EXPERT + (c * F + f * P), P)]
                        lo = wt[:, bass.ds(e1 * EXPERT + (PIECE + c * F + f * P), P)]
                        pe.matmul(dst, hi, xT[:, s, c * P:(c + 1) * P], start=(c == 0 and f % 4 == 0), stop=False,
                                  skip_group_check=True)
                        pe.matmul(dst, hi, xT[:, s, (2 + c) * P:(3 + c) * P], start=False, stop=False,
                                  skip_group_check=True)
                        m = pe.matmul(dst, lo, xT[:, s, c * P:(c + 1) * P], start=False, stop=(c == DC - 1),
                                      skip_group_check=True)
                        if (f, c) == (FC - 1, DC - 1):
                            m.then_inc(l1_mm, 1)
                    if two:
                        w = wt[:, bass.ds(e2 * EXPERT + (2 * PIECE + f * 2 * C), 2 * C)]
                        hi = wt[:, bass.ds(e2 * EXPERT + (2 * PIECE + f * 2 * C), C)]
                        pe.matmul(y_ps(s), hhi[:, s, f * P:(f + 1) * P], w, start=(f == 0), stop=False)
                        pe.matmul(y_ps(s)[:, 0:C], hlo[:, s, f * P:(f + 1) * P], hi, start=False, stop=False)
                    if f == 1 and (not isinstance(j, int) or n + 1 < TILES):
                        turn(j, n + 1)
                    if f == FC // 2 and (not isinstance(j, int) or n + 1 < TILES):
                        load_expert(j, n + 1)
                if two:
                    pe.matmul(y_ps(s)[:, 0:C], c16[0:33, C16["bias"]], b2c[:, bass.ds(e2 * C, C)],
                              start=False, stop=True).then_inc(l2_mm, 1)

            turn(0, 0)
            load_expert(0, 0)
            moe(pe, step, lambda: wait_lo(pe, POOL_SPLITS[-1]))
            for n in range(TILES, TILES + 2):
                step(0, n)

        @block.vector
        def _(dve):
            v = nc.vector
            steps = [0]

            def link(ins):
                steps[0] += 1
                ins.then_inc(dve_step, 1)
                dve.wait_ge(dve_step, steps[0])

            def split_lo(n):
                wait_hi(dve, n)
                v.scalar_tensor_tensor(out=wpiece(n, 1), in0=staged(n), scalar=WS, in1=wpiece(n, 0),
                                       op0=ALU.mult, op1=ALU.subtract).then_inc(dve_lo, 1)

            def diag(dst, row):
                return v.tensor_tensor(out=dst.rearrange("p (g c) -> p g c", c=CG),
                                       in0=cc("blocks").rearrange("p (g c) -> p g c", c=CG),
                                       in1=row.unsqueeze(1).broadcast_to([P, P // CG, CG]), op=ALU.mult)

            v.memset(eps_c, EPS_C)
            v.memset(eps_g, EPS_G).then_inc(eps_set, 1)
            v.memset(ones_row[:, :], 1.0)
            v.memset(w1d[:, :], 1.0 / C).then_inc(small_ready, 1)

            def stats_c(b):
                if b % 2 == 0:
                    dve.wait_ge(x_in[b // 2], 16)
                for k in (2 * b, 2 * b + 1):
                    ins = v.bn_stats(bn6[:, k, :], xt[:, k, :])
                link(ins)
                for k in (2 * b, 2 * b + 1):
                    ins = v.bn_aggr(mv[:, k, :], bn6[:, k, :])
                ins.then_inc(var_c, 1)

            def norm_c(b):
                dve.wait_ge(dev_c, b + 1)
                link(v.reciprocal(rstd[:, 2 * b:2 * b + 2], dev[:, 2 * b:2 * b + 2]))
                for k in (2 * b, 2 * b + 1):
                    ins = v.tensor_scalar(xln_tok[:, k, :], xt[:, k, :], mv[:, k, 0:1], rstd[:, k:k + 1],
                                          ALU.subtract, ALU.mult)
                ins.then_inc(ln_done, 1)

            def power(t):
                dve.wait_ge(sq_done, t + 1)
                if t == 0:
                    dve.wait_ge(spare_set, 32)
                v.scalar_tensor_tensor(out=mag[:, t, :], in0=sq[:, t % 2, 0:NF], scalar=TINY, in1=sq[:, t % 2, NF:2 * NF],
                                       op0=ALU.max, op1=ALU.add).then_inc(mag_done, 1)

            for b in range(2):
                stats_c(b)
            norm_c(0)
            stats_c(2)
            norm_c(1)
            dve.wait_ge(const_in, 48)
            s1row, e1, m1 = prow[:, 0:CG], prow[:, 2 * CG:3 * CG], pcol[:, 0:1]
            link(v.tensor_reduce(out=m1, in_=par[:, PAR["betarow"]], axis=AX_X, op=ALU.max))
            v.tensor_scalar(prow[:, CG:2 * CG], par[:, PAR["betarow"]], m1, None, ALU.subtract).then_inc(exp_in, 1)
            dve.wait_ge(exp_done, 1)
            link(v.tensor_reduce(out=pcol[:, 1:2], in_=e1, axis=AX_X, op=ALU.add))
            link(v.reciprocal(pcol[:, 2:3], pcol[:, 1:2]))
            link(v.tensor_scalar(s1row, e1, pcol[:, 2:3], None, ALU.mult))
            v.tensor_tensor(out=prow[:, 3 * CG:4 * CG], in0=s1row, in1=par[:, PAR["wpw"]], op=ALU.mult)
            link(v.tensor_tensor(out=prow[:, 4 * CG:5 * CG], in0=s1row, in1=cc("own"), op=ALU.mult))
            vcol, s1col = pcol[:, 3:4], pcol[:, 4:5]
            v.tensor_reduce(out=vcol, in_=prow[:, 3 * CG:4 * CG], axis=AX_X, op=ALU.add)
            link(v.tensor_reduce(out=s1col, in_=prow[:, 4 * CG:5 * CG], axis=AX_X, op=ALU.add))
            v.tensor_scalar(pcol[:, 5:14], par[:, PAR["wdw"]], vcol, None, ALU.mult)
            link(v.tensor_scalar(pcol[:, 14:15], vcol, col("bdw"), None, ALU.mult))
            v.scalar_tensor_tensor(out=pcol[:, 15:16], in0=s1col, scalar=col("bpw"), in1=pcol[:, 14:15],
                                   op0=ALU.mult, op1=ALU.add)
            v.memset(tapw, 0.0).then_inc(dve_step, 1)
            steps[0] += 1
            dve.wait_ge(dve_step, steps[0])
            group = cc("blocks")[:, 0:P:CG]
            for k in range(TAPS * TAPS):
                ins = v.tensor_scalar(tapw[:, k % TAPS, k // TAPS * 32:k // TAPS * 32 + P // CG], group,
                                      pcol[:, 5 + k:6 + k], None, ALU.mult)
            ins.then_inc(tapw_done, 1)
            dve.wait_ge(small_mm, 1)
            for a in range(HALVES):
                v.tensor_tensor(out=wgc[:, a, :], in0=par[:, PAR["wg"].start + a * E:PAR["wg"].start + (a + 1) * E],
                                in1=ps[:, 5, 0:E], op=ALU.subtract)
            diag(w1d[:, :], par[:, PAR["w1"]]).then_inc(small_ready, 1)
            diag(wpwd[:, :], par[:, PAR["wpw"]])
            link(v.tensor_reduce(out=prow[:, 5 * CG:6 * CG], in_=par[:, PAR["wfp"]].rearrange("p (o c) -> p o c", c=CG),
                                 axis=AX_X, op=ALU.add))
            diag(wfpd[:, :], prow[:, 5 * CG:6 * CG])
            for b in range(2, B):
                if b + 1 < B:
                    stats_c(b + 1)
                norm_c(b)
                power(2 * (b - 2))
                power(2 * (b - 2) + 1)
                if b in (3, 5):
                    split_lo({3: 1, 5: 3}[b])
                if b == 4:
                    dve.wait_ge(b2_in, 16)
                    link(v.tensor_scalar(b2c[:, :], b2f, WS, None, ALU.mult))
                    v.scalar_tensor_tensor(out=b2c[32:33, :], in0=b2f[32:33, :], scalar=WS, in1=b2c[32:33, :],
                                           op0=ALU.mult, op1=ALU.subtract).then_inc(b2_done, 1)
            for b in (B - 2, B - 1):
                power(2 * b)
                power(2 * b + 1)
                if b == B - 2:
                    split_lo(5)

            dve.wait_ge(x_logit_mm, 1)
            v.tensor_tensor(out=xlg[:, :, :], in0=ps[:, 7, 0:NBLK * E].rearrange("p (k e) -> p k e", e=E),
                            in1=dev[:, :].unsqueeze(2).broadcast_to([P, NBLK, E]), op=ALU.mult)
            dve.wait_ge(padded, POOL_PADS)
            dve.wait_ge(tr_copied, B)
            link(v.tensor_reduce(out=tot[:, :], in_=rc[:, :, 0:H], axis=AX_X, op=ALU.add))
            v.tensor_copy(r3[:, :, 1:2], tot[:, :].unsqueeze(2))
            v.tensor_tensor(out=r3[:, :, 0:1], in0=tot[:, :].unsqueeze(2), in1=rc[:, :, H - 1:H], op=ALU.subtract)
            v.tensor_tensor(out=r3[:, :, 2:3], in0=tot[:, :].unsqueeze(2), in1=rc[:, :, 0:1], op=ALU.subtract)
            for n, c in ((0, W - 1), (1, 0)):
                v.tensor_copy(q3[:, :, 1, n:n + 1], rc[:, :, H + c:H + c + 1])
                for d, r in ((0, H - 1), (2, 0)):
                    ins = v.tensor_tensor(out=q3[:, :, d, n:n + 1], in0=rc[:, :, H + c:H + c + 1],
                                          in1=xln_pad[:, :, 1 + r, 1 + c:2 + c], op=ALU.subtract)
            link(ins)
            v.tensor_copy(s9[:, :, :, 1], r3[:, :, :])
            v.tensor_tensor(out=s9[:, :, :, 0], in0=r3[:, :, :], in1=q3[:, :, :, 0], op=ALU.subtract)
            link(v.tensor_tensor(out=s9[:, :, :, 2], in0=r3[:, :, :], in1=q3[:, :, :, 1], op=ALU.subtract))
            s9v = s9[:, :, :, :].rearrange("p t a b -> p t (a b)")
            link(v.tensor_tensor(out=s9v, in0=s9v, in1=par[:, PAR["wdw"]].unsqueeze(1).broadcast_to([P, NT, 9]),
                                 op=ALU.mult))
            link(v.tensor_reduce(out=dwm[:, :], in_=s9v, axis=AX_X, op=ALU.add))
            v.tensor_scalar(dwm[:, :], dwm[:, :], 1.0 / PX, col("bdw"), ALU.mult, ALU.add).then_inc(small_ready, 1)

            def gate(t):
                dve.wait_ge(gate_row, t + 1)
                gv = gated[:, t].rearrange("p (h w) -> p h w", w=W)
                v.tensor_tensor(out=gv, in0=gv, in1=sg[:, t, H:H + W].unsqueeze(1).broadcast_to([P, H, W]),
                                op=ALU.mult).then_inc(gated_done, 1)

            dve.wait_ge(small_mm, 2)
            logits = ps[0:NT, 5, 128:256].rearrange("p (g c) -> p g c", c=CG)
            row = lambda n: s2r[:, n, :].rearrange("p (g c) -> p g c", c=CG)
            wide = lambda n: s2s[:, n, :].unsqueeze(2).broadcast_to([NT, P // CG, CG])
            link(v.tensor_reduce(out=s2s[:, 0, :], in_=logits, axis=AX_X, op=ALU.max))
            v.tensor_tensor(out=row(0), in0=logits, in1=wide(0), op=ALU.subtract).then_inc(exp_in, 1)
            for t in range(NT):
                if t < DVE_GATES:
                    gate(t)
                if t > 0:
                    if t <= DVE_GATES:
                        dve.wait_ge(gated_done, t)
                    else:
                        dve.wait_ge(gate_col, t - DVE_GATES)
                    v.bn_stats(gbn6[:, t - 1, :], gated[:, t - 1, :])
                if t == NT // 2:
                    dve.wait_ge(exp_done, 2)
                    link(v.tensor_reduce(out=s2s[:, 1, :], in_=row(1), axis=AX_X, op=ALU.add))
                    link(v.reciprocal(s2s[:, 0, :], s2s[:, 1, :]))
                    v.tensor_tensor(out=row(2), in0=row(1), in1=wide(0), op=ALU.mult).then_inc(small_ready, 1)
            dve.wait_ge(gate_col, NT - DVE_GATES)
            link(v.bn_stats(gbn6[:, NT - 1, :], gated[:, NT - 1, :]))
            for t in range(NT):
                ins = v.bn_aggr(gmv[:, t, :], gbn6[:, t, :])
            ins.then_inc(var_g, 1)
            dve.wait_ge(dev_g, 1)
            link(v.reciprocal(grs[:, :], grs[:, :]))
            v.tensor_scalar(grs[:, :], grs[:, :], col("gamma"), None, ALU.mult)
            dve.wait_ge(small_mm, 3)
            link(v.tensor_copy(s2c[:, :], ps[:, 5, 256:256 + NT]))
            link(v.tensor_tensor(out=coef[:, :], in0=s2c[:, :], in1=grs[:, :], op=ALU.mult))
            link(v.tensor_tensor(out=bterm[:, :], in0=coef[:, :], in1=gmv[:, :, 0], op=ALU.mult))
            link(v.scalar_tensor_tensor(out=bterm[:, :], in0=s2c[:, :], scalar=col("beta"), in1=bterm[:, :],
                                        op0=ALU.mult, op1=ALU.subtract))
            v.tensor_scalar(bterm[:, :], bterm[:, :], pcol[:, 15:16], None, ALU.add).then_inc(small_ready, 1)
            def weigh(t):
                if t >= 4:
                    dve.wait_ge(map_done, t // 2 - 1)
                v.tensor_scalar(coefw[:, t % 4, :], cc("blocks"), coef[:, t:t + 1], None, ALU.mult).then_inc(coef_done, 1)

            dve.wait_ge(dve_step, steps[0])
            for t in range(4):
                weigh(t)
            dve.wait_ge(root_done, 1)
            v.tensor_reduce(out=fm[:, :, :], in_=mag.rearrange("p t (i j) -> p t i j", j=KW), axis=AX_X,
                            op=ALU.add).then_inc(fm_done, 1)
            dve.wait_ge(small_mm, 4)
            v.tensor_scalar(bias[:, :], ps[:, 5, 288:288 + NT], col("bfp"), None, ALU.add).then_inc(coef_done, 1)
            split_lo(7)

            def apply_gate(t):
                dve.wait_ge(sig_done, t + 1)
                v.tensor_tensor(out=z[:, t, :].rearrange("p (h w) -> p h w", w=W), in0=inner(t, 1)[:, 0],
                                in1=sig[:, t % 2, :].rearrange("p (h w) -> p h w", w=W), op=ALU.mult).then_inc(z_done, 1)

            def add_x(b):
                dve.wait_ge(zt_done, b + 1)
                v.tensor_tensor(out=xt[:, 2 * b:2 * b + 2, :], in0=ps[:, 2 + b % 2, :].rearrange("p (k c) -> p k c", c=C),
                                in1=xt[:, 2 * b:2 * b + 2, :], op=ALU.add).then_inc(t_done, 1)

            def stats_t(b):
                dve.wait_ge(t_done, b + 1)
                for k in (2 * b, 2 * b + 1):
                    ins = v.bn_stats(bn6[:, k, :], xt[:, k, :])
                link(ins)
                for k in (2 * b, 2 * b + 1):
                    ins = v.bn_aggr(tmv[:, k, :], bn6[:, k, :])
                ins.then_inc(var_t, 1)

            def invert(b):
                dve.wait_ge(dev_t, b // 4 + 1)
                at = slice(2 * b, 2 * b + 8)
                link(v.reciprocal(trs[:, at], trs[:, at]))
                link(v.tensor_scalar(trs64[:, at], trs[:, at], XS, None, ALU.mult))

            def norm_t(b):
                for k in (2 * b, 2 * b + 1):
                    if k >= 4:
                        dve.wait_ge(xlo_done, k - 3)
                        dve.wait_ge(xhi_done, k - 3)
                    v.tensor_scalar(xn[:, k % 4, :], xt[:, k, :], tmv[:, k, 0:1], trs64[:, k:k + 1],
                                    ALU.subtract, ALU.mult).then_inc(xn_done, 1)

            for b in range(B + 2):
                if b < B:
                    apply_gate(2 * b)
                    apply_gate(2 * b + 1)
                if b + 2 < B:
                    weigh(2 * b + 4)
                    weigh(2 * b + 5)
                if b >= 2:
                    add_x(b - 2)
                    stats_t(b - 2)
                if b in (0, 2, 5):
                    split_lo({0: 6, 2: 9, 5: 15}[b])
                if b == B:
                    invert(0)
                    norm_t(0)
            norm_t(1)

            invert(4)
            dve.wait_ge(logit_mm, 1)
            link(v.tensor_tensor(out=lg[:, :, :], in0=ps[:, 4, 0:NBLK * E].rearrange("p (k e) -> p k e", e=E),
                                 in1=xlg[:, :, :], op=ALU.add))
            link(v.tensor_tensor(out=lg[:, :, :], in0=lg[:, :, :],
                                 in1=trs[:, :].unsqueeze(2).broadcast_to([P, NBLK, E]), op=ALU.mult))
            spread = lambda x: x.unsqueeze(2).broadcast_to([P, NBLK, E])
            rev = cc("rev").unsqueeze(1).broadcast_to([P, NBLK, E])
            source = lg
            for a in range(TOP_K):
                link(v.tensor_reduce(out=best[:, 0, :], in_=source[:, :, :], axis=AX_X, op=ALU.max))
                link(v.tensor_tensor(out=eq, in0=source[:, :, :], in1=spread(best[:, 0, :]), op=ALU.is_equal))
                link(v.tensor_tensor(out=eq, in0=eq, in1=rev, op=ALU.mult))
                link(v.tensor_reduce(out=best[:, 1, :], in_=eq, axis=AX_X, op=ALU.max))
                link(v.tensor_tensor(out=pick[:, a], in0=rev, in1=spread(best[:, 1, :]), op=ALU.is_equal))
                if a == 0:
                    source = rest
                    v.scalar_tensor_tensor(out=rest[:, :, :], in0=pick[:, 0], scalar=LOW, in1=lg[:, :, :],
                                           op0=ALU.mult, op1=ALU.add).then_inc(logit_done, 1)
                    dve.wait_ge(logit_done, 1)
            v.tensor_tensor(out=sel16[:, :, :], in0=pick[:, 0], in1=pick[:, 1], op=ALU.add).then_inc(sel_done, 1)
            norm_t(2)
            norm_t(3)
            dve.wait_ge(prefix_mm, 1)
            link(v.tensor_copy(cnt[:, :], ps[:, 5, NBLK * E:(NBLK + 1) * E]))
            over = view(2176, E * NBLK).rearrange("p (e k) -> p e k", k=NBLK)
            link(v.tensor_tensor(out=over, in0=cnt[:, :].unsqueeze(2).broadcast_to([P, E, NBLK]),
                                 in1=cc("steps").unsqueeze(1).broadcast_to([P, E, NBLK]), op=ALU.is_gt))
            link(v.tensor_reduce(out=tcnt[:, 0, :], in_=over, axis=AX_X, op=ALU.add))
            low = view(2176 + E * NBLK, E * E).rearrange("p (e j) -> p e j", j=E)
            link(v.tensor_tensor(out=low, in0=cc("before").rearrange("p (e j) -> p e j", j=E),
                                 in1=tcnt[:, 0, :].unsqueeze(1).broadcast_to([P, E, E]), op=ALU.mult))
            link(v.tensor_reduce(out=tcnt[:, 1, :], in_=low, axis=AX_X, op=ALU.add))
            v.tensor_tensor(out=tcnt[:, 2, :], in0=tcnt[:, 1, :], in1=tcnt[:, 0, :], op=ALU.add)
            link(v.tensor_scalar(cnt[:, :], tcnt[:, 1, :], float(P), None, ALU.mult))
            link(v.tensor_tensor(out=slot[:, :, :], in0=ps[:, 5, 0:NBLK * E].rearrange("p (k e) -> p k e", e=E),
                                 in1=cnt[:, :].unsqueeze(1).broadcast_to([P, NBLK, E]), op=ALU.add))
            dve.wait_ge(sigl_done, 1)
            picked = view(1152, 4 * NBLK * E).rearrange("p (a v k e) -> p a v k e", a=2, v=2, k=NBLK)
            for a in range(TOP_K):
                v.tensor_tensor(out=picked[:, a, 0], in0=pick[:, a], in1=slot[:, :, :], op=ALU.mult)
                ins = v.tensor_tensor(out=picked[:, a, 1], in0=pick[:, a], in1=sgl[:, :, :], op=ALU.mult)
            link(ins)
            link(v.tensor_reduce(out=psum_pick[:, :, :, :].rearrange("p a v k -> p (a v k)"),
                                 in_=picked.rearrange("p a v k e -> p (a v k) e"), axis=AX_X, op=ALU.add))
            link(v.tensor_copy(sloti[:, 0], psum_pick[:, :, 0, :]))
            v.tensor_scalar(sloti[:, 1], sloti[:, 0], 7, None, ALU.arith_shift_right)
            link(v.tensor_scalar(sloti[:, 2], sloti[:, 0], P - 1, None, ALU.bitwise_and))
            v.tensor_copy(place16[:, 0], sloti[:, 2])
            v.tensor_copy(place16[:, 1], sloti[:, 1])
            v.tensor_copy(tok16[:, :], cc("token"))
            link(v.tensor_scalar(place16[:, 2], psum_pick[:, :, 1, :], GS, None, ALU.mult))
            link(v.scalar_tensor_tensor(out=place16[:, 3], in0=psum_pick[:, :, 1, :], scalar=GS, in1=place16[:, 2],
                                        op0=ALU.mult, op1=ALU.subtract))
            dve.wait_ge(t_out, 16 * B)
            dve.wait_ge(xn_done, 8)
            flat = lambda n: place16[:, n].rearrange("p a k -> p (a k)")
            by_tile = lambda x: x.unsqueeze(2).broadcast_to([P, 2 * NBLK, TCOL])
            v.tensor_tensor(out=pay[:, :, 0, :], in0=c16[:, C16["tiles"]].unsqueeze(1).broadcast_to([P, 2 * NBLK, TCOL]),
                            in1=by_tile(flat(1)), op=ALU.is_equal).then_inc(pay_done, 1)
            for a in range(TOP_K):
                half = slice(a * NBLK, (a + 1) * NBLK)
                v.tensor_tensor(out=hot[:, half, :], in0=c16[:, C16["iota"]].unsqueeze(1).broadcast_to([P, NBLK, P]),
                                in1=flat(0)[:, half].unsqueeze(2).broadcast_to([P, NBLK, P]), op=ALU.is_equal)
                dve.wait_ge(pay_done, 1)
                v.tensor_tensor(out=pay[:, half, 1, :], in0=pay[:, half, 0, :],
                                in1=tok16[:, :].unsqueeze(2).broadcast_to([P, NBLK, TCOL]), op=ALU.mult)\
                    .then_inc(hot_done, 1)
                norm_t(4 + a)
            split_lo(11)
            link(v.tensor_tensor(out=texpf[:, :, :], in0=cc("tiles").unsqueeze(2).broadcast_to([P, TCOL, E]),
                                 in1=tcnt[:, 2, :].unsqueeze(1).broadcast_to([P, TCOL, E]), op=ALU.is_ge))
            link(v.tensor_reduce(out=texpc[:, :], in_=texpf[:, :, :], axis=AX_X, op=ALU.add))
            v.tensor_scalar(texp[:, :], texpc[:, :], float(E - 1), None, ALU.min)
            norm_t(6)
            dve.wait_ge(table_mm, 1)
            link(v.tensor_scalar(found[:, :], ps[:, 7, TCOL:2 * TCOL], cc("spare"), None, ALU.add))
            v.scalar_tensor_tensor(out=idx[:, :], in0=ps[:, 7, 0:TCOL], scalar=cc("minusrow"), in1=found[:, :],
                                   op0=ALU.mult, op1=ALU.add).then_inc(table_done, 1)
            norm_t(7)
            for n in (2, 3):
                ins = v.tensor_tensor(out=pay[:, :, n, :], in0=pay[:, :, 0, :], in1=by_tile(flat(n)), op=ALU.mult)
            ins.then_inc(hot_done, 1)
            split_lo(13)
            dve.wait_ge(table_mm, 2)
            unscale = 1.0 / (GS * WS * HS)
            link(v.tensor_scalar(gates[:, :], ps[:, 6, 0:TCOL], unscale, None, ALU.mult))
            link(v.scalar_tensor_tensor(out=gates[:, :], in0=ps[:, 6, TCOL:2 * TCOL], scalar=unscale, in1=gates[:, :],
                                        op0=ALU.mult, op1=ALU.add))

            def rows_T(j, n):
                i, s = UNROLL * j + n, n % 2
                dve.wait_ge(xT_mm, i + 1)
                if n >= 2:
                    dve.wait_ge(l1_mm, i - 1)
                v.tensor_copy(xT[:, s, :], xT_ps).then_inc(xT_done, 1)

            def halves(j, n):
                i, s = UNROLL * j + n, n % 2
                dve.wait_ge(gelu_done, i + 1)
                if n >= 2:
                    dve.wait_ge(l2_mm, i - 1)
                v.tensor_scalar(hhi[:, s, :], hid[:, s, :], HS, None, ALU.mult).then_inc(hhi_done, 1)
                dve.wait_ge(hhi_done, i + 1)
                v.scalar_tensor_tensor(out=hlo[:, s, :], in0=hid[:, s, :], scalar=HS, in1=hhi[:, s, :],
                                       op0=ALU.mult, op1=ALU.subtract).then_inc(h_done, 1)

            def scaled(j, n):
                i, s = UNROLL * j + n, n % 2
                gate = gates[:, bass.ds(i, 1)]
                dve.wait_ge(l2_mm, i + 1)
                if n >= 2:
                    dve.wait_ge(add_out, 16 * i - 16)
                v.tensor_scalar(yb[:, s, :], y_ps(s)[:, C:2 * C], gate, None, ALU.mult).then_inc(ylo_done, 1)
                dve.wait_ge(ylo_done, i + 1)
                v.scalar_tensor_tensor(out=yb[:, s, :], in0=y_ps(s)[:, 0:C], scalar=gate, in1=yb[:, s, :],
                                       op0=ALU.mult, op1=ALU.add).then_inc(y_done, 1)

            def step(j, n):
                if not isinstance(j, int) or n + 1 < TILES:
                    rows_T(j, n + 1)
                if n >= 1:
                    halves(j, n - 1)
                if n >= 2:
                    scaled(j, n - 2)

            rows_T(0, 0)
            moe(dve, step)
            for n in range(TILES, TILES + 2):
                if n == TILES:
                    halves(0, n - 1)
                scaled(0, n - 2)


def _constants():
    p = np.arange(P)
    c = np.zeros((P, NCONST), np.float32)
    c[:, CONST["ident"]] = np.eye(P)
    c[:, CONST["blocks"]] = p[:, None] // CG == p[None, :] // CG
    pos = np.clip((np.arange(H) + 0.5) * (CG / H) - 0.5, 0, CG - 1)
    lo = np.floor(pos).astype(int)
    resize = np.zeros((CG, H))
    np.add.at(resize, (lo, np.arange(H)), 1 - (pos - lo))
    np.add.at(resize, (np.minimum(lo + 1, CG - 1), np.arange(H)), pos - lo)
    c[:, CONST["resize"]] = resize[p % CG] / KW
    c[:, CONST["own"]] = p[:, None] % CG == np.arange(CG)
    c[:, CONST["tiles"]] = np.arange(TCOL)
    c[:, CONST["before"]] = (np.arange(E)[None, :] < np.arange(E)[:, None]).ravel()
    c[:, CONST["steps"]] = P * np.arange(NBLK)
    c[:, CONST["token"]] = P * np.arange(NBLK)[None, :] + p[:, None] - NTOK
    c[:, CONST["rev"]] = E - np.arange(E)
    c[:, CONST["minusrow"]] = -p[:, None]
    c[:, CONST["spare"]] = NTOK + p[:, None]
    c[:, CONST["spread"]] = p[:, None] % 32 == p[None, :] // CG
    px = np.arange(PX)
    n = np.arange(NF)
    turns = (np.outer(px // W, n // KW) % H) / H + (np.outer(px % W, n % KW) % W) / W
    quarter = np.round(turns * 4 * 4).astype(int) % 16
    cos = np.cos(2 * np.pi * np.arange(16) / 16)
    cos[[4, 12]] = 0
    dft = np.concatenate([cos[quarter], cos[(quarter - 4) % 16]], 1) / np.sqrt(PX)
    dft = np.concatenate([dft, px[:, None] // W == np.arange(H), px[:, None] % W == np.arange(W)], 1)
    c[:, CONST["dft"]] = dft.reshape(DC, P, NMIX).transpose(1, 0, 2).reshape(P, -1)
    h = np.zeros((P, NC16), np.float16)
    h[:, C16["ident"]] = np.eye(P)
    h[:, C16["earlier"]] = p[:, None] < p[None, :]
    h[:, C16["ones"]] = 1
    h[[0, 32], C16["bias"]] = HS
    h[:, C16["iota"]] = p[None, :]
    h[:, C16["tiles"]] = np.arange(TCOL)
    return c, h


def kernel(**inputs):
    import concourse.bacc as bacc
    from concourse.bass_utils import run_bass_kernel_spmd

    a = {k: np.asarray(v) for k, v in inputs.items()}
    g = {k[len("L0_conv_"):]: v for k, v in a.items() if k.startswith("L0_conv_")}
    f = {k[len("L0_ffn_"):]: v for k, v in a.items() if k.startswith("L0_ffn_")}
    n = P // CG
    par = np.zeros((P, NPAR), np.float32)
    par[:, PAR["w1"]] = np.tile(g["w1"].T, (n, 1))
    par[:, PAR["wpw"]] = np.tile(g["w_pw"].T, (n, 1))
    par[:, PAR["wdw"]] = np.tile(g["w_dw"].reshape(CG, 9), (n, 1))
    for name, key in (("b1", "b1"), ("gamma", "gn_gamma"), ("beta", "gn_beta"), ("bdw", "b_dw"), ("bpw", "b_pw"), ("bfp", "b_fp")):
        par[:, PAR[name]] = np.tile(g[key][:, None], (n, 1))
    par[:, PAR["betarow"]] = g["gn_beta"][None, :]
    par[:, PAR["wfp"]] = g["w_fp"].reshape(1, -1)
    par[:, PAR["bpwrow"]] = np.tile(g["b_pw"], n)[None, :]
    par[:, PAR["wg"]] = f["Wg"].reshape(HALVES, P, E).transpose(1, 0, 2).reshape(P, -1)
    par[:, PAR["b1e"]] = f["b1"].reshape(E, FC, P).transpose(2, 0, 1).reshape(P, -1)
    const, const16 = _constants()
    x = a["x"]
    arrays = {
        "x_tok": np.ascontiguousarray(x.reshape(B, C, PX).transpose(0, 2, 1).reshape(NTOK, C)),
        "const": const, "const16": const16, "params": par,
        "w1": np.ascontiguousarray(f["W1"]), "w2": np.ascontiguousarray(f["W2"]),
        "b2": np.ascontiguousarray(f["b2"].reshape(1, -1)),
    }
    nc = bacc.Bacc("TRN2", target_bir_lowering=False, num_devices=1)
    aps = [nc.dram_tensor(k, v.shape, mybir.dt.from_np(v.dtype), kind="ExternalInput").ap() for k, v in arrays.items()]
    out = nc.dram_tensor("out", (TROWS, C), F32, kind="ExternalOutput").ap()
    build(nc, *aps, out)
    r = run_bass_kernel_spmd(nc, [arrays], core_ids=[0])
    got = np.asarray(r.results[0]["out"])[:NTOK]
    return np.ascontiguousarray(got.reshape(B, PX, C).transpose(0, 2, 1)).reshape(B, C, H, W)
```
